# Optimizing a Trainium2 kernel written in Bass

```python
import numpy as np
import jax
import jax.numpy as jnp

def _softmax(x, axis=-1):
    return jax.nn.softmax(x, axis=axis)

def _gelu(x):
    return jax.nn.gelu(x, approximate=True)

def _silu(x):
    return jax.nn.silu(x)

def _sigmoid(x):
    return jax.nn.sigmoid(x)

def _layernorm(x, axis=-1, eps=1e-05):
    m = jnp.mean(x, axis=axis, keepdims=True)
    v = jnp.var(x, axis=axis, keepdims=True)
    return (x - m) / jnp.sqrt(v + eps)

def _scatter_add(tgt, idx, src, axis=0):
    return tgt.at[idx].add(src)

def _segment_sum(src, seg, n):
    return jax.ops.segment_sum(src, seg, n)
kernel_name = 'mk_decoder_postln_d1_seqx_r4_60ae14'

def setup_inputs(seed: int=0):
    np.random.seed(seed)
    _w = jnp.asarray

    def _rec_inputs():
        import jax
        import jax.numpy as jnp
        _rk = jax.random.key(seed)
        x = -0.0005207 + 1.001 * jax.random.normal(jax.random.fold_in(_rk, 1), (8, 512, 256), jnp.float32)
        _lenS = 512 - jax.random.randint(jax.random.fold_in(_rk, 7), (8,), 0, max(1, 512 // 4) + 1, jnp.int32)
        _lenS2 = 1601 - jax.random.randint(jax.random.fold_in(_rk, 8), (8,), 0, max(1, 1601 // 4) + 1, jnp.int32)
        _ctx_1024P = jax.random.normal(jax.random.fold_in(_rk, 11), (8, 16, 256), jnp.float32)
        _ctx_1024c = jax.random.dirichlet(jax.random.fold_in(_rk, 511), 0.3 * jnp.ones((16,), jnp.float32), (8, 1601))
        _ctx_1024t = jnp.einsum('bsk,bkd->bsd', _ctx_1024c, _ctx_1024P)
        _ctx_1024t = _ctx_1024t * jax.lax.rsqrt(jnp.mean(jnp.square(_ctx_1024t)) + 1e-12) * 0.953939
        ctx_1024 = 2.81802e-05 + 1.00001 * (_ctx_1024t + 0.3 * jax.random.normal(jax.random.fold_in(_rk, 611), (8, 1601, 256), jnp.float32))
        _validS = jnp.arange(512)[None, :] < _lenS[:, None]
        _validS2 = jnp.arange(1601)[None, :] < _lenS2[:, None]
        _causal = jnp.tril(jnp.ones((512, 512), dtype=bool))
        mask_Bx1x1xS2_bf1 = jnp.ones((8, 1, 1, 1601), dtype=bool)
        return (x, ctx_1024, mask_Bx1x1xS2_bf1)
    x, ctx_1024, mask_Bx1x1xS2_bf1 = _rec_inputs()

    def _L0_attn_setup():
        import jax, jax.numpy as jnp
        import numpy as np
        DIMS, HEAD = (256, 16)
        HD = DIMS // HEAD
        MAX_ITER = 3
        B, T = (4, 512)

        def _ln(x, w, eps=1e-05):
            m = jnp.mean(x, axis=-1, keepdims=True)
            v = jnp.var(x, axis=-1, keepdims=True)
            return (x - m) * jax.lax.rsqrt(v + eps) * w
        key = jax.random.key(seed)
        ks = jax.random.split(key, 10)
        n = lambda k, s: jax.random.normal(k, s, jnp.float32) * 0.02
        z = lambda s: jnp.zeros(s, jnp.float32)
        o = lambda s: jnp.ones(s, jnp.float32)
        return {'x': jax.random.normal(ks[0], (B, T, DIMS), jnp.float32), 'Wq': n(ks[1], (DIMS, DIMS)), 'bq': z((DIMS,)), 'Wk': n(ks[2], (DIMS, DIMS)), 'Wv': n(ks[3], (DIMS, DIMS)), 'bv': z((DIMS,)), 'Wo': n(ks[4], (DIMS, DIMS)), 'bo': z((DIMS,)), 'lna_w': o((DIMS,)), 'lnc_w': o((HD,)), 'lnd_w': o((HD,)), 'Wlq': n(ks[5], (HD, HD)), 'blq': z((HD,)), 'Wlk': n(ks[6], (HD, HD)), 'blk': z((HD,)), 'Wlv': n(ks[7], (HD, HD)), 'blv': z((HD,)), 'temp': jnp.float32(1.0), 'threshold': jnp.float32(0.01), 'factor': jnp.float32(0.1)}
    _L0_attn_all = _L0_attn_setup()
    _L0_attn_in = {k: v for k, v in _L0_attn_all.items() if k in ('Wq', 'bq', 'Wk', 'Wv', 'bv', 'Wo', 'bo', 'lna_w', 'lnc_w', 'lnd_w', 'Wlq', 'blq', 'Wlk', 'blk', 'Wlv', 'blv', 'temp', 'threshold', 'factor')}
    del _L0_attn_all

    def _L0_xattn_setup():
        import jax, jax.numpy as jnp
        import numpy as np
        D_MODEL = 256
        N_HEADS = 16
        D_HEAD = D_MODEL // N_HEADS

        def _split_heads(x):
            B, L, D = x.shape
            return x.reshape(B, L, N_HEADS, D_HEAD).transpose(0, 2, 1, 3)
        key = jax.random.key(seed)
        ks = jax.random.split(key, 6)
        B, LQ, LK = (4, 128, 1024)
        scale = 1.0 / np.sqrt(D_MODEL)
        return {'q_in': jax.random.normal(ks[0], (B, LQ, D_MODEL), dtype=jnp.float32), 'mem': jax.random.normal(ks[1], (B, LK, D_MODEL), dtype=jnp.float32), 'mem_mask': jnp.ones((B, 1, 1, LK), dtype=bool), 'Wq': jax.random.normal(ks[2], (D_MODEL, D_MODEL), dtype=jnp.float32) * scale, 'Wk': jax.random.normal(ks[3], (D_MODEL, D_MODEL), dtype=jnp.float32) * scale, 'Wv': jax.random.normal(ks[4], (D_MODEL, D_MODEL), dtype=jnp.float32) * scale, 'Wo': jax.random.normal(ks[5], (D_MODEL, D_MODEL), dtype=jnp.float32) * scale}
    _L0_xattn_all = _L0_xattn_setup()
    _L0_xattn_in = {k: v for k, v in _L0_xattn_all.items() if k in ('Wq', 'Wk', 'Wv', 'Wo')}
    del _L0_xattn_all

    def _L0_ffn_setup():
        import jax, jax.numpy as jnp
        import numpy as np
        B, T, D, H, R, N = (16, 256, 256, 64, 64, 8)
        key = jax.random.key(seed)
        ks = jax.random.split(key, 8)
        s = lambda k, shape, fan: jax.random.normal(k, shape, jnp.float32) / np.sqrt(fan)
        return {'x': jax.random.normal(ks[0], (B, T, D), jnp.float32), 'W_base': s(ks[1], (D, D), D), 'b_base': jnp.zeros((D,), jnp.float32), 'W_enc': s(ks[2], (N, D, H), D), 'b_enc': jnp.zeros((N, H), jnp.float32), 'W_dec': s(ks[3], (N, H, D), H), 'b_dec': jnp.zeros((N, D), jnp.float32), 'W_down': s(ks[4], (N, D, R), D), 'b_down': jnp.zeros((N, R), jnp.float32), 'W_up': s(ks[5], (N, R, D), R), 'b_up': jnp.zeros((N, D), jnp.float32), 'connected_idx': jnp.arange(N, dtype=jnp.int32)}
    _L0_ffn_all = _L0_ffn_setup()
    _L0_ffn_in = {k: v for k, v in _L0_ffn_all.items() if k in ('W_base', 'b_base', 'W_enc', 'b_enc', 'W_dec', 'b_dec', 'W_down', 'b_down', 'W_up', 'b_up', 'connected_idx')}
    del _L0_ffn_all
    return {'x': x, 'ctx_1024': ctx_1024, 'mask_Bx1x1xS2_bf1': mask_Bx1x1xS2_bf1, 'L0_attn_Wq': _L0_attn_in['Wq'], 'L0_attn_bq': _L0_attn_in['bq'], 'L0_attn_Wk': _L0_attn_in['Wk'], 'L0_attn_Wv': _L0_attn_in['Wv'], 'L0_attn_bv': _L0_attn_in['bv'], 'L0_attn_Wo': _L0_attn_in['Wo'], 'L0_attn_bo': _L0_attn_in['bo'], 'L0_attn_lna_w': _L0_attn_in['lna_w'], 'L0_attn_lnc_w': _L0_attn_in['lnc_w'], 'L0_attn_lnd_w': _L0_attn_in['lnd_w'], 'L0_attn_Wlq': _L0_attn_in['Wlq'], 'L0_attn_blq': _L0_attn_in['blq'], 'L0_attn_Wlk': _L0_attn_in['Wlk'], 'L0_attn_blk': _L0_attn_in['blk'], 'L0_attn_Wlv': _L0_attn_in['Wlv'], 'L0_attn_blv': _L0_attn_in['blv'], 'L0_attn_temp': _L0_attn_in['temp'], 'L0_attn_threshold': _L0_attn_in['threshold'], 'L0_attn_factor': _L0_attn_in['factor'], 'L0_xattn_Wq': _L0_xattn_in['Wq'], 'L0_xattn_Wk': _L0_xattn_in['Wk'], 'L0_xattn_Wv': _L0_xattn_in['Wv'], 'L0_xattn_Wo': _L0_xattn_in['Wo'], 'L0_ffn_W_base': _L0_ffn_in['W_base'], 'L0_ffn_b_base': _L0_ffn_in['b_base'], 'L0_ffn_W_enc': _L0_ffn_in['W_enc'], 'L0_ffn_b_enc': _L0_ffn_in['b_enc'], 'L0_ffn_W_dec': _L0_ffn_in['W_dec'], 'L0_ffn_b_dec': _L0_ffn_in['b_dec'], 'L0_ffn_W_down': _L0_ffn_in['W_down'], 'L0_ffn_b_down': _L0_ffn_in['b_down'], 'L0_ffn_W_up': _L0_ffn_in['W_up'], 'L0_ffn_b_up': _L0_ffn_in['b_up'], 'L0_ffn_connected_idx': _L0_ffn_in['connected_idx']}

def reference(x, ctx_1024, mask_Bx1x1xS2_bf1, L0_attn_Wq, L0_attn_bq, L0_attn_Wk, L0_attn_Wv, L0_attn_bv, L0_attn_Wo, L0_attn_bo, L0_attn_lna_w, L0_attn_lnc_w, L0_attn_lnd_w, L0_attn_Wlq, L0_attn_blq, L0_attn_Wlk, L0_attn_blk, L0_attn_Wlv, L0_attn_blv, L0_attn_temp, L0_attn_threshold, L0_attn_factor, L0_xattn_Wq, L0_xattn_Wk, L0_xattn_Wv, L0_xattn_Wo, L0_ffn_W_base, L0_ffn_b_base, L0_ffn_W_enc, L0_ffn_b_enc, L0_ffn_W_dec, L0_ffn_b_dec, L0_ffn_W_down, L0_ffn_b_down, L0_ffn_W_up, L0_ffn_b_up, L0_ffn_connected_idx):
    import jax
    import jax.numpy as jnp

    def _L0_attn_ref(x, Wq, bq, Wk, Wv, bv, Wo, bo, lna_w, lnc_w, lnd_w, Wlq, blq, Wlk, blk, Wlv, blv, temp, threshold, factor):
        import jax, jax.numpy as jnp
        import numpy as np
        DIMS, HEAD = (256, 16)
        HD = DIMS // HEAD
        MAX_ITER = 3
        B, T = (4, 512)

        def _ln(x, w, eps=1e-05):
            m = jnp.mean(x, axis=-1, keepdims=True)
            v = jnp.var(x, axis=-1, keepdims=True)
            return (x - m) * jax.lax.rsqrt(v + eps) * w
        Bn, Tn, D = x.shape
        H, hd = (HEAD, HD)
        temp0 = jax.lax.stop_gradient(temp)
        thr = jax.lax.stop_gradient(threshold)
        fac = jax.lax.stop_gradient(factor)
        scale = hd ** (-0.25)
        xn = _ln(x, lna_w)
        q = (xn @ Wq.T + bq) * scale
        k = xn @ Wk.T * scale
        v = xn @ Wv.T + bv
        shp = lambda t: t.reshape(Bn, Tn, H, hd).transpose(0, 2, 1, 3)
        q, k, v = (shp(q), shp(k), shp(v))
        E = H
        sm_scale = 1.0 / float(np.sqrt(hd))
        qcur, kcur, vcur = (q, k, v)
        prev = jnp.zeros_like(q)
        attn_out = jnp.zeros_like(q)
        done = jnp.asarray(False)
        for it in range(MAX_ITER):
            ql = qcur[:, :, :E] @ Wlq.T + blq
            kl = kcur[:, :, :E] @ Wlk.T + blk
            vl = vcur[:, :, :E] @ Wlv.T + blv
            t_it = temp0 + 0.005 * it
            tscale = jnp.where((t_it != 1.0) & (t_it > 0), jax.lax.rsqrt(t_it), 1.0)
            qs = _ln(ql, lnc_w) * tscale
            ks_ = _ln(kl, lnd_w)
            logits = jnp.einsum('bhqd,bhkd->bhqk', qs, ks_) * sm_scale
            ai = jnp.einsum('bhqk,bhkd->bhqd', jax.nn.softmax(logits, axis=-1), vl)
            iter_out = jnp.zeros_like(qcur).at[:, :, :E].set(ai)
            diff = jnp.mean(jnp.abs(iter_out - prev))
            attn_out = jnp.where(done, attn_out, iter_out)
            done = done | (diff < thr + fac * diff) & (it > 0)
            prev = iter_out
            qcur = qcur + iter_out
            kcur, vcur = (kl, vl)
        out = attn_out.transpose(0, 2, 1, 3).reshape(Bn, Tn, D)
        return out @ Wo.T + bo

    def _L0_xattn_ref(q_in, mem, mem_mask, Wq, Wk, Wv, Wo):
        import jax, jax.numpy as jnp
        import numpy as np
        D_MODEL = 256
        N_HEADS = 16
        D_HEAD = D_MODEL // N_HEADS

        def _split_heads(x):
            B, L, D = x.shape
            return x.reshape(B, L, N_HEADS, D_HEAD).transpose(0, 2, 1, 3)
        q = _split_heads(q_in @ Wq.T)
        k = _split_heads(mem @ Wk.T)
        v = _split_heads(mem @ Wv.T)
        scores = jnp.einsum('bhqd,bhkd->bhqk', q, k) / jnp.sqrt(jnp.float32(D_HEAD))
        scores = jnp.where(mem_mask, scores, -jnp.inf)
        attn = jax.nn.softmax(scores, axis=-1)
        out = jnp.einsum('bhqk,bhkd->bhqd', attn, v)
        B, H, LQ, Dh = out.shape
        out = out.transpose(0, 2, 1, 3).reshape(B, LQ, H * Dh)
        return out @ Wo.T

    def _L0_ffn_ref(x, W_base, b_base, W_enc, b_enc, W_dec, b_dec, W_down, b_down, W_up, b_up, connected_idx):
        import jax, jax.numpy as jnp
        import numpy as np
        B, T, D, H, R, N = (16, 256, 256, 64, 64, 8)
        base = jnp.einsum('btd,de->bte', x, W_base) + b_base
        h = jax.nn.relu(jnp.einsum('btd,ndh->nbth', x, W_enc) + b_enc[:, None, None, :])
        recon = jnp.einsum('nbth,nhd->nbtd', h, W_dec) + b_dec[:, None, None, :]
        losses = jnp.mean((recon - x[None]) ** 2, axis=(2, 3))
        top1 = jnp.argmin(losses, axis=0)
        adp = connected_idx[top1]
        Wd, bd = (W_down[adp], b_down[adp])
        Wu, bu = (W_up[adp], b_up[adp])
        mid = jax.nn.relu(jnp.einsum('btd,bdr->btr', x, Wd) + bd[:, None, :])
        adapter_out = jnp.einsum('btr,brd->btd', mid, Wu) + bu[:, None, :]
        return base + adapter_out
    x = _layernorm(x + _L0_attn_ref(x, L0_attn_Wq, L0_attn_bq, L0_attn_Wk, L0_attn_Wv, L0_attn_bv, L0_attn_Wo, L0_attn_bo, L0_attn_lna_w, L0_attn_lnc_w, L0_attn_lnd_w, L0_attn_Wlq, L0_attn_blq, L0_attn_Wlk, L0_attn_blk, L0_attn_Wlv, L0_attn_blv, L0_attn_temp, L0_attn_threshold, L0_attn_factor), axis=-1)
    x = _layernorm(x + _L0_xattn_ref(x, ctx_1024, mask_Bx1x1xS2_bf1, L0_xattn_Wq, L0_xattn_Wk, L0_xattn_Wv, L0_xattn_Wo), axis=-1)
    x = _layernorm(x + _L0_ffn_ref(x, L0_ffn_W_base, L0_ffn_b_base, L0_ffn_W_enc, L0_ffn_b_enc, L0_ffn_W_dec, L0_ffn_b_dec, L0_ffn_W_down, L0_ffn_b_down, L0_ffn_W_up, L0_ffn_b_up, L0_ffn_connected_idx), axis=-1)
    return x

_drawn_inputs = setup_inputs


def setup_inputs(seed=0):
    import zlib

    import numpy as np

    out = dict(_drawn_inputs(seed))
    spreads = {'L0_attn_bq': (0.0, 0.8),
     'L0_attn_bv': (0.0, 0.8),
     'L0_attn_bo': (0.0, 0.1),
     'L0_attn_lna_w': (1.0, 0.6),
     'L0_attn_lnc_w': (1.0, 0.6),
     'L0_attn_lnd_w': (1.0, 0.6),
     'L0_attn_blq': (0.0, 0.8),
     'L0_attn_blk': (0.0, 0.8),
     'L0_attn_blv': (0.0, 0.8),
     'L0_ffn_b_base': (0.0, 0.1),
     'L0_ffn_b_enc': (0.0, 0.1),
     'L0_ffn_b_dec': (0.0, 0.1),
     'L0_ffn_b_down': (0.0, 0.1),
     'L0_ffn_b_up': (0.0, 0.1)}
    factors = {'L0_attn_Wq': 8.0,
     'L0_attn_Wk': 8.0,
     'L0_attn_Wv': 8.0,
     'L0_attn_Wo': 8.0,
     'L0_attn_Wlq': 8.0,
     'L0_attn_Wlk': 8.0,
     'L0_attn_Wlv': 8.0}
    for name, (base, spread) in spreads.items():
        noise = np.random.default_rng([zlib.crc32(name.encode()), seed]).standard_normal(out[name].shape)
        drawn = base * np.exp(spread * noise) if base else spread * noise
        out[name] = jnp.asarray(drawn.astype(out[name].dtype))
    for name, factor in factors.items():
        out[name] = (out[name] * factor).astype(out[name].dtype)
    return out
```

```python
from contextlib import ExitStack

import concourse.bass as bass
from concourse import mybir

F32 = mybir.dt.float32
BF16 = mybir.dt.bfloat16
U8 = mybir.dt.uint8
I32 = mybir.dt.int32
ALU = mybir.AluOpType
ACT = mybir.ActivationFunctionType
AX = mybir.AxisListType

P = 128
B, T, D = 8, 512, 256
H, HD = 16, 16
S2 = 1601
QT = T // P
CH = D // P
HC = P // HD
GH = 4
NG = HC // GH
ITERS = 3
TOK = B * HD
EPS = 1e-5
NEG = -1e30
PARTS = 3
QPART = (0, 0, 1, 0, 1, 2)
KPART = (0, 1, 0, 2, 1, 0)
R_MASK = 6 * HD
R_MAX = R_MASK + 1
ROWS = R_MAX + 2


class Shared:

    def __init__(self, a):
        self.x, self.ctxT, self.mask = a["x"], a["ctxT"], a["mask"]
        self.WqT, self.WkT, self.WvT, self.WoT = a["WqT"], a["WkT"], a["WvT"], a["WoT"]
        self.WlqT, self.WlkT, self.WlvT = a["WlqT"], a["WlkT"], a["WlvT"]
        self.bq, self.bv, self.bo, self.blq, self.blk, self.blv = a["bq"], a["bv"], a["bo"], a["blq"], a["blk"], a["blv"]
        self.lna, self.lnc, self.lnd = a["lna"], a["lnc"], a["lnd"]
        self.temp, self.threshold, self.factor = a["temp"], a["threshold"], a["factor"]
        self.xWqT, self.xWkT, self.xWvT, self.xWoT = a["xWqT"], a["xWkT"], a["xWvT"], a["xWoT"]
        self.Wbase, self.bbase, self.Wenc, self.benc = a["Wbase"], a["bbase"], a["Wenc"], a["benc"]
        self.Wdec, self.bdec, self.Wdown, self.bdown = a["Wdec"], a["bdec"], a["Wdown"], a["bdown"]
        self.Wup, self.bup, self.cidx = a["Wup"], a["bup"], a["cidx"]
        self.c_ident, self.c_head, self.c_hide, self.c_iota = a["c_ident"], a["c_head"], a["c_hide"], a["c_iota"]


class Phase:

    def __init__(self, tail, order):
        self.tail, self.order = tail, Order(order)


class Order:

    def __init__(self, names):
        self.names = list(names)
        self.index = {n: i for i, n in enumerate(self.names)}

    def before(self, name):
        return self.index[name]

    def after(self, name):
        return self.index[name] + 1


def sbuf(nc, stack, name, shape, dt=F32):
    return stack.enter_context(nc.sbuf_tensor(name, shape, dt))


def program(nc, g):
    with ExitStack() as whole:
        g.sem = lambda name: whole.enter_context(nc.semaphore(name))
        g.st = [whole.enter_context(nc.psum_tensor(f"scores{i}", [P, 2, T], F32)) for i in range(2)]
        g.mx = [whole.enter_context(nc.psum_tensor(f"max_scores{i}", [P, T], F32)) for i in range(2)]
        g.av = whole.enter_context(nc.psum_tensor("values", [P, T], F32))
        g.W = whole.enter_context(nc.psum_tensor("work", [P, T], F32))
        g.ident = sbuf(nc, whole, "ident", [P, P])
        g.ident_b = sbuf(nc, whole, "ident_b", [P, P], BF16)
        g.mhalf = sbuf(nc, whole, "mhalf", [P, 2 * H])
        g.attn_dram = nc.dram_tensor("attn_dram", (B, HD, D), F32, kind="Internal").ap()
        g.part_dram = nc.dram_tensor("parts_dram", (PARTS, P, T), BF16, kind="Internal").ap()
        g.kpart_dram = nc.dram_tensor("key_parts_dram", (PARTS, P, S2), BF16, kind="Internal").ap()
        g.mask_dram = nc.dram_tensor("mask_dram", (B, SP_), BF16, kind="Internal").ap()
        g.x1_dram = nc.dram_tensor("x1_dram", (B, T, D), F32, kind="Internal").ap()
        g.max_dram = nc.dram_tensor("max_dram", (2 * GH * QT, P), BF16, kind="Internal").ap()

        short_self_attention(nc, g)
        cross_attention_and_ffn(nc, g)


def short_self_attention(nc, g):
    ident, W, av, st, mx, sem = g.ident, g.W, g.av, g.st, g.mx, g.sem
    with ExitStack() as s:
        def sb(name, shape, dt=F32):
            return sbuf(nc, s, name, shape, dt)

        x = sb("s_x", [TOK, D])
        wq, wk, wv, wo = (sb(f"s_w{n}", [P, CH, D]) for n in "qkvo")
        wl = [sb(f"s_wl{n}", [P, P]) for n in "qkv"]
        bq, bv = (sb(f"s_b{n}", [P, CH]) for n in "qv")
        bl = sb("s_bl", [TOK, 3, HD])
        lna = sb("s_lna", [TOK, D])
        lncd = sb("s_lncd", [TOK, 2, HD])
        tt = sb("s_t", [TOK, ITERS])
        tf = sb("s_threshold_factor", [P, 2])
        head = sb("s_head_mask", [P, HC])
        hide = sb("s_hide", [TOK, TOK])
        m8 = sb("s_mask_bytes", [B, S2], U8)
        tone, tpos, tpow = (sb(n, [TOK, ITERS]) for n in ("s_tone", "s_tpos", "s_tpow"))
        ln_w = sb("s_ln_w", [TOK, ITERS, 2, HD])
        stats = sb("s_stats", [TOK, 6])
        meanvar = sb("s_meanvar", [TOK, 2])
        xn = sb("s_xn", [TOK, D])
        xnT = sb("s_xnT", [P, CH, TOK])
        state = sb("s_state", [P, 3, CH, TOK])
        rows = sb("s_rows", [TOK, 3, H, HD])
        cen = sb("s_centered", [TOK, 2 * H, HD])
        sq = sb("s_squares", [TOK, 2 * H, HD])
        msum = sb("s_sums", [TOK, 2 * H])
        var = sb("s_vars", [TOK, 2 * H])
        qsT = sb("s_qsT", [P, CH, TOK])
        ksM = sb("s_ksM", [P, CH, HC, TOK])
        sc = sb("s_scores", [TOK, H, TOK])
        nmax = sb("s_neg_max", [TOK, H])
        rsum = sb("s_rsum", [TOK, H])
        pT = sb("s_probsT", [TOK, H, TOK])
        outs = sb("s_outs", [TOK, ITERS, D])
        adiff = sb("s_abs_diff", [TOK, D])
        asum = sb("s_abs_sum", [TOK, 1])
        ones = sb("s_ones", [P, P])
        diff, lim, keep, other = (sb(n, [P, 1]) for n in ("s_diff", "s_lim", "s_keep", "s_other"))
        proj = sb("s_proj", [TOK, D])
        mb = sb("s_mask_addend", [B, SP_], BF16)

        early = sem("s_early_in")
        loaded = sem("s_in")
        zeroed = sem("s_zeroed")
        own = sem("s_own")
        xn_ready = sem("s_x_normed")
        bias_ready = sem("s_bias")
        kv_made = sem("s_kv_transposed")
        oT_made = sem("s_out_transposed")
        diff_ready = sem("s_diff")
        asum_ready = sem("s_abs")
        sel_ready = sem("s_selected")
        mm = sem("s_products")
        read = sem("s_read")
        var_ready = sem("s_var")
        root_ready = sem("s_roots")
        cen_ready = sem("s_centered_in")
        sq_ready = sem("s_squared")
        qk_ready = sem("s_qk_normed")
        rows_ready = sem("s_rows_in")
        t_ready = sem("s_transposed")
        sc_ready = sem("s_scored")
        p_ready = sem("s_exped")
        p_out = sem("s_probs_taken")
        o_ready = sem("s_out")
        st_ready = sem("s_state_in")
        mask_ready = sem("s_mask")
        stored = sem("s_stored")
        early_n = 16 * (B + 2)
        loaded_n = 16 * (4 + 3 * HC + 2 + 3 + 2 + ITERS + 2 + 2 + 1)
        MMS = 8

        with nc.Block() as blk:
            @blk.sync
            def _(sp):
                for b in range(B):
                    sp.dma_start(x[b * HD:(b + 1) * HD, :], g.x[b, 0:HD, :]).then_inc(early, 16)
                sp.dma_start(ident[:], g.c_ident).then_inc(early, 16)
                sp.dma_start(lna[:], g.lna.unsqueeze(0).broadcast_to([TOK, D])).then_inc(early, 16)
                for dst, src in ((wq, g.WqT), (wk, g.WkT), (wv, g.WvT), (wo, g.WoT)):
                    sp.dma_start(dst[:], src.rearrange("(c p) d -> p c d", p=P)).then_inc(loaded, 16)
                with nc.allow_non_contiguous_dma(reason="small vectors, once"):
                    for dst, src in ((bq, g.bq), (bv, g.bv)):
                        sp.dma_start(dst[:], src.rearrange("(c p) -> p c", p=P)).then_inc(loaded, 16)
                for i, src in enumerate((g.blq, g.blk, g.blv)):
                    sp.dma_start(bl[:, i, :], src.unsqueeze(0).broadcast_to([TOK, HD])).then_inc(loaded, 16)
                for i, src in enumerate((g.lnc, g.lnd)):
                    sp.dma_start(lncd[:, i, :], src.unsqueeze(0).broadcast_to([TOK, HD])).then_inc(loaded, 16)
                for i in range(ITERS):
                    sp.dma_start(tt[:, i:i + 1], g.temp.to_broadcast([TOK, 1])).then_inc(loaded, 16)
                sp.dma_start(tf[:, 0:1], g.threshold.to_broadcast([P, 1])).then_inc(loaded, 16)
                sp.dma_start(tf[:, 1:2], g.factor.to_broadcast([P, 1])).then_inc(loaded, 16)
                sp.dma_start(head[:], g.c_head).then_inc(loaded, 16)
                sp.dma_start(hide[:], g.c_hide).then_inc(loaded, 16)
                sp.dma_start(m8[:], g.mask).then_inc(loaded, 16)
                sp.wait_ge(mask_ready, 1)
                sp.dma_start(g.mask_dram, mb[:]).then_inc(stored, 16)
                sp.wait_ge(read, 3)
                sp.dma_start(g.attn_dram.rearrange("b t d -> (b t) d"), proj[:]).then_inc(stored, 16)
                sp.wait_ge(stored, 32)

            @blk.gpsimd
            def _(pool):
                p = nc.gpsimd
                for n, one in enumerate(wl):
                    p.memset(one[:], 0.0).then_inc(zeroed, 1)
                p.memset(g.mhalf[:], -0.5).then_inc(zeroed, 1)
                p.memset(ones[:], 1.0).then_inc(zeroed, 1)
                p.memset(mb[:], NEG).then_inc(zeroed, 1)
                pool.wait_ge(zeroed, 6)

                def root(buf, n):
                    pool.wait_ge(var_ready, n)
                    p.tensor_tensor(buf, buf, g.mhalf[:, 0:buf.shape[-1]], ALU.pow).then_inc(root_ready, 1)

                root(meanvar[:, 1:2], 1)
                root(tpow[:], 2)
                for it in range(ITERS):
                    root(var[:], 3 + it)

            @blk.scalar
            def _(act):
                a = nc.scalar
                act.wait_ge(zeroed, 3)
                for i, src in enumerate((g.WlqT, g.WlkT, g.WlvT)):
                    for h in range(HC):
                        act.dma_start(wl[i][h * HD:(h + 1) * HD, h * HD:(h + 1) * HD], src).then_inc(loaded, 16)
                act.wait_ge(mm, 1)
                a.activation(xnT[:], W[:, 0:D].rearrange("p (c t) -> p c t", c=CH), ACT.Copy).then_inc(read, 1)
                act.wait_ge(loaded, loaded_n)
                act.wait_ge(bias_ready, 1)
                for i, bank in enumerate((W, mx[0], mx[1])):
                    act.wait_ge(mm, 2 + i)
                    for c in range(CH):
                        src = bank[:, c * TOK:(c + 1) * TOK]
                        if i == 0:
                            last = a.activation(state[:, i, c, :], src, ACT.Identity, bias=bq[:, c:c + 1],
                                                scale=float(HD) ** -0.25)
                        elif i == 1:
                            last = a.activation(state[:, i, c, :], src, ACT.Copy, scale=float(HD) ** -0.25)
                        else:
                            last = a.activation(state[:, i, c, :], src, ACT.Identity, bias=bv[:, c:c + 1])
                    last.then_inc(st_ready, 1)
                for it in range(ITERS):
                    base = 4 + MMS * it
                    act.wait_ge(cen_ready, it + 1)
                    a.activation(sq[:], cen[:], ACT.Square).then_inc(sq_ready, 1)
                    act.wait_ge(mm, base + 3)
                    a.activation(qsT[:], mx[0][:, 0:D].rearrange("p (c t) -> p c t", c=CH), ACT.Copy).then_inc(t_ready, 1)
                    if it < ITERS - 1:
                        act.wait_ge(kv_made, it + 1)
                        a.activation(state[:, 1:3, :, :], mx[1][:].rearrange("p (i c t) -> p i c t", i=2, c=CH),
                                     ACT.Copy).then_inc(st_ready, 1)
                    act.wait_ge(sc_ready, it + 1)
                    for h in range(H):
                        last = a.activation(sc[:, h, :], sc[:, h, :], ACT.Exp, bias=nmax[:, h:h + 1],
                                            accum_out=rsum[:, h:h + 1])
                        if h % HC == HC - 1:
                            last.then_inc(p_ready, 1)
                    act.wait_ge(mm, base + 6)
                    a.activation(pT[:, 0:HC, :], st[0][:].rearrange("p a (h t) -> p (a h) t", t=TOK),
                                 ACT.Copy).then_inc(p_out, 1)
                act.wait_ge(diff_ready, 1)
                a.activation(adiff[:], adiff[:], ACT.Abs, accum_out=asum[:]).then_inc(asum_ready, 1)

            @blk.tensor
            def _(pe):
                def transposes(bank, pieces):
                    for i, src in enumerate(pieces):
                        last = pe.transpose(bank[:, i * TOK:(i + 1) * TOK], src, ident[:])
                    return last

                pe.wait_ge(early, early_n)
                pe.wait_ge(xn_ready, 1)
                transposes(W, [xn[:, c * P:(c + 1) * P] for c in range(CH)]).then_inc(mm, 1)
                pe.wait_ge(read, 1)
                pe.wait_ge(loaded, loaded_n)
                for w, bank in ((wq, W), (wk, mx[0]), (wv, mx[1])):
                    for c in range(CH):
                        for kin in range(CH):
                            last = pe.matmul(bank[:, c * TOK:(c + 1) * TOK], w[:, kin, c * P:(c + 1) * P],
                                             xnT[:, kin, :], start=kin == 0, stop=kin == CH - 1)
                    last.then_inc(mm, 1)
                for it in range(ITERS):
                    pe.wait_ge(st_ready, 3 + 2 * it)
                    for n, bank, first in ((0, W, 0), (1, W, D), (2, av, 0)):
                        for c in range(CH):
                            last = pe.matmul(bank[:, first + c * P:first + (c + 1) * P], state[:, n, c, :], wl[n][:],
                                             start=True, stop=True)
                        if n:
                            last.then_inc(mm, 1)
                    pe.wait_ge(qk_ready, it + 1)
                    cenr = cen[:].rearrange("p (n c h) d -> p n c (h d)", n=2, c=CH)
                    transposes(mx[0], [cenr[:, 0, c, :] for c in range(CH)])
                    pe.wait_ge(rows_ready, it + 1)
                    transposes(av, [cenr[:, 1, c, :] for c in range(CH)]).then_inc(mm, 1)
                    if it < ITERS - 1:
                        rowsr = rows[:].rearrange("p n (c h) d -> p n c (h d)", c=CH)
                        transposes(mx[1], [rowsr[:, n, c, :] for n in (1, 2) for c in range(CH)]).then_inc(kv_made, 1)
                    pe.wait_ge(t_ready, (1 + CH) * (it + 1))
                    for c in range(CH):
                        for half in range(2):
                            last = pe.matmul(st[c][:, half, :], qsT[:, c, :],
                                             ksM[:, c, half * GH:(half + 1) * GH, :].rearrange("p h t -> p (h t)"),
                                             start=True, stop=True)
                        last.then_inc(mm, 1)
                    for c in range(CH):
                        pe.wait_ge(p_ready, CH * it + c + 1)
                        for h in range(HC):
                            last = pe.transpose(st[c][:, h // GH, h % GH * TOK:(h % GH + 1) * TOK],
                                                sc[:, c * HC + h, :], ident[:])
                        last.then_inc(mm, 1)
                    pe.wait_ge(p_out, 2 * it + 2)
                    for h in range(H):
                        last = pe.matmul(av[:, h * HD:(h + 1) * HD], pT[:, h, :], rows[:, 2, h, :], start=True, stop=True)
                    last.then_inc(mm, 1)
                    if it < ITERS - 1:
                        pe.wait_ge(o_ready, it + 1)
                        transposes(W, [outs[:, it, c * P:(c + 1) * P] for c in range(CH)]).then_inc(oT_made, 1)
                pe.wait_ge(asum_ready, 1)
                pe.matmul(W[:, 0:1], ones[:], asum[:], start=True, stop=True).then_inc(mm, 1)
                pe.wait_ge(sel_ready, 1)
                transposes(mx[0], [xn[:, c * P:(c + 1) * P] for c in range(CH)]).then_inc(mm, 1)
                pe.wait_ge(read, 2)
                for kin in range(CH):
                    last = pe.matmul(av[:, 0:D], xnT[:, kin, :], wo[:, kin, :], start=kin == 0, stop=kin == CH - 1)
                last.then_inc(mm, 1)

            @blk.vector
            def _(dve):
                v = nc.vector
                n = [0]

                def link(ins):
                    n[0] += 1
                    ins.then_inc(own, 1)
                    dve.wait_ge(own, n[0])

                dve.wait_ge(early, early_n)
                link(v.bn_stats(stats[:], x[:]))
                link(v.bn_aggr(meanvar[:], stats[:]))
                v.tensor_scalar(meanvar[:, 1:2], meanvar[:, 1:2], EPS, None, ALU.add).then_inc(var_ready, 1)
                dve.wait_ge(root_ready, 1)
                link(v.tensor_scalar(xn[:], x[:], meanvar[:, 0:1], meanvar[:, 1:2], ALU.subtract, ALU.mult))
                v.tensor_tensor(xn[:], xn[:], lna[:], ALU.mult).then_inc(xn_ready, 1)
                v.tensor_copy(g.ident_b[:], ident[:])
                dve.wait_ge(loaded, loaded_n)
                for i in range(1, ITERS):
                    link(v.tensor_scalar(tt[:, i:i + 1], tt[:, i:i + 1], 0.005 * i, None, ALU.add))
                v.tensor_scalar(tpow[:], tt[:], 1e-37, None, ALU.max).then_inc(var_ready, 1)
                link(v.tensor_scalar(tone[:], tt[:], 1.0, None, ALU.not_equal))
                link(v.tensor_scalar(tpos[:], tt[:], 0.0, None, ALU.is_gt))
                link(v.tensor_tensor(tone[:], tone[:], tpos[:], ALU.mult))
                v.tensor_scalar(bq[:], bq[:], float(HD) ** -0.25, None, ALU.mult).then_inc(bias_ready, 1)
                dve.wait_ge(root_ready, 2)
                link(v.tensor_scalar(tpow[:], tpow[:], 1.0, None, ALU.subtract))
                link(v.tensor_tensor(tpow[:], tpow[:], tone[:], ALU.mult))
                link(v.tensor_scalar(tpow[:], tpow[:], 1.0, None, ALU.add))
                for it in range(ITERS):
                    v.tensor_scalar(ln_w[:, it, 0, :], lncd[:, 0, :], tpow[:, it:it + 1], float(HD) ** -0.5,
                                    ALU.mult, ALU.mult)
                    link(v.tensor_copy(ln_w[:, it, 1, :], lncd[:, 1, :]))
                dve.wait_ge(zeroed, 6)
                v.tensor_scalar(mb[:, 0:S2], m8[:], 0.0, NEG, ALU.is_equal, ALU.mult).then_inc(mask_ready, 1)
                for it in range(ITERS):
                    base = 4 + MMS * it
                    heads = W[:].rearrange("p (n h d) -> p n h d", n=2, d=HD)
                    dve.wait_ge(mm, base + 1)
                    link(v.tensor_tensor(rows[:, 0:2, :, :], heads,
                                         bl[:, 0:2, :].unsqueeze(2).broadcast_to([TOK, 2, H, HD]), ALU.add))
                    dve.wait_ge(mm, base + 2)
                    v.tensor_tensor(rows[:, 2, :, :], av[:, 0:D].rearrange("p (h d) -> p h d", d=HD),
                                    bl[:, 2, :].unsqueeze(1).broadcast_to([TOK, H, HD]), ALU.add).then_inc(rows_ready, 1)
                    qk = rows[:, 0:2, :, :].rearrange("p n h d -> p (n h) d")
                    link(v.tensor_reduce(msum[:], qk, AX.X, ALU.add))
                    link(v.tensor_scalar(msum[:], msum[:], 1.0 / HD, None, ALU.mult))
                    v.tensor_tensor(cen[:], qk, msum[:].unsqueeze(2).broadcast_to([TOK, 2 * H, HD]),
                                    ALU.subtract).then_inc(cen_ready, 1)
                    dve.wait_ge(sq_ready, it + 1)
                    link(v.tensor_reduce(var[:], sq[:], AX.X, ALU.add))
                    v.tensor_scalar(var[:], var[:], 1.0 / HD, EPS, ALU.mult, ALU.add).then_inc(var_ready, 1)
                    link(v.tensor_tensor(cen[:].rearrange("p (n h) d -> p n h d", n=2),
                                         cen[:].rearrange("p (n h) d -> p n h d", n=2),
                                         ln_w[:, it, :, :].unsqueeze(2).broadcast_to([TOK, 2, H, HD]), ALU.mult))
                    dve.wait_ge(root_ready, 3 + it)
                    v.tensor_tensor(cen[:], cen[:], var[:].unsqueeze(2).broadcast_to([TOK, 2 * H, HD]),
                                    ALU.mult).then_inc(qk_ready, 1)
                    dve.wait_ge(mm, base + 3)
                    for c in range(CH):
                        v.tensor_tensor(ksM[:, c, :, :],
                                        av[:, c * TOK:(c + 1) * TOK].unsqueeze(1).broadcast_to([P, HC, TOK]),
                                        head[:].unsqueeze(2).broadcast_to([P, HC, TOK]), ALU.mult).then_inc(t_ready, 1)
                    for c in range(CH):
                        dve.wait_ge(mm, base + 4 + c)
                        link(v.tensor_tensor(sc[:, c * HC:(c + 1) * HC, :], st[c][:].rearrange("p a (h t) -> p (a h) t", t=TOK),
                                             hide[:].unsqueeze(1).broadcast_to([TOK, HC, TOK]), ALU.add))
                    v.tensor_reduce(nmax[:], sc[:], AX.X, ALU.max, negate=True).then_inc(sc_ready, 1)
                    dve.wait_ge(p_ready, CH * (it + 1))
                    link(v.reciprocal(rsum[:], rsum[:]))
                    dve.wait_ge(mm, base + 7)
                    v.tensor_copy(pT[:, HC:H, :], st[1][:].rearrange("p a (h t) -> p (a h) t", t=TOK)).then_inc(p_out, 1)
                    dve.wait_ge(mm, base + 8)
                    v.tensor_tensor(outs[:, it, :].rearrange("p (h d) -> p h d", d=HD),
                                    av[:, 0:D].rearrange("p (h d) -> p h d", d=HD),
                                    rsum[:].unsqueeze(2).broadcast_to([TOK, H, HD]), ALU.mult).then_inc(o_ready, 1)
                    if it < ITERS - 1:
                        dve.wait_ge(oT_made, it + 1)
                        v.tensor_tensor(state[:, 0, :, :], state[:, 0, :, :],
                                        W[:, 0:D].rearrange("p (c t) -> p c t", c=CH), ALU.add).then_inc(st_ready, 1)
                dve.wait_ge(o_ready, ITERS)
                v.tensor_tensor(adiff[:], outs[:, 1, :], outs[:, 0, :], ALU.subtract).then_inc(diff_ready, 1)
                end = 4 + MMS * ITERS
                dve.wait_ge(mm, end + 1)
                link(v.tensor_scalar(diff[:], W[:, 0:1], 1.0 / (B * T * D), None, ALU.mult))
                link(v.tensor_scalar(lim[:], diff[:], tf[:, 1:2], tf[:, 0:1], ALU.mult, ALU.add))
                link(v.tensor_tensor(keep[:], diff[:], lim[:], ALU.is_lt))
                link(v.tensor_scalar(other[:], keep[:], -1.0, 1.0, ALU.mult, ALU.add))
                link(v.tensor_scalar(outs[:, 1, :], outs[:, 1, :], keep[:], None, ALU.mult))
                v.scalar_tensor_tensor(xn[:], outs[:, 2, :], other[:], outs[:, 1, :], ALU.mult,
                                       ALU.add).then_inc(sel_ready, 1)
                dve.wait_ge(mm, end + 2)
                v.tensor_copy(xnT[:], mx[0][:, 0:D].rearrange("p (c t) -> p c t", c=CH)).then_inc(read, 1)
                dve.wait_ge(mm, end + 3)
                v.tensor_copy(proj[:], av[:, 0:D]).then_inc(read, 1)


XKT = -(-S2 // P)
SP_ = XKT * P
PIECES = ((0, 401), (401, 400), (801, 400), (1201, 400))
MXG = GH * QT * len(PIECES)
MXS = 5
XSLOTS = CH * NG * XKT
LEAD = 2
NE, EH, ER = 8, 64, 64
NDEC = NE * CH


def cross_attention_and_ffn(nc, g):
    sem, W, ident, ident_b, st, mx, av = g.sem, g.W, g.ident, g.ident_b, g.st, g.mx, g.av
    Wb = W[:].bitcast(BF16)
    with ExitStack() as s:
        def sb(name, shape, dt=F32):
            return sbuf(nc, s, name, shape, dt)

        xqT, xkT, xvT, xoT, wbase = (sb(n, [P, CH, D]) for n in ("xqT", "xkT", "xvT", "xoT", "wbase"))
        wenc = sb("wenc", [P, CH, NE, EH])
        wdec = sb("wdec", [P, NE, D])
        bo = sb("bo_rows", [P, D])
        benc = sb("benc_cols", [P, NE * EH // P])
        bdec = sb("bdec_cols", [P, NE, CH])
        cidx = sb("cidx", [P, NE], I32)
        cidxf = sb("cidx_f", [P, NE])
        iota = sb("iota", [P, NE])
        iotam = sb("iota_minus", [P, NE])
        ones = sb("ones", [P, P])
        wdown = sb("wdown", [P, CH, ER])
        bdown = sb("bdown_col", [ER, 1])
        wup = sb("wup", [ER + 2, D])
        midT = sb("midT", [ER + 2, T])
        ctxT = sb("ctxT_sb", [P, CH, S2])
        kst = sb("xk_stacks", [P, 2, HC, SP_], BF16)
        qst = sb("xq_stacks", [P, 2, HC, T], BF16)
        vals = sb("xv_rows", [P, 2, XKT, HC, HD + 1])
        probs = sb("xprobs", [P, 2, GH, T])
        oS = sb("xo_unnormed", [P, T])
        rz = sb("xrsum", [P, QT, GH])
        nmp = sb("xneg_max_pieces", [P, GH * QT, len(PIECES)])
        nm = sb("xneg_max", [P, GH * QT])
        comb = sb("xneg_max_parts", [P, 2, GH * QT], BF16)
        mrow = sb("xneg_max_rows", [2 * GH * QT, P], BF16)
        kpart = sb("xk_parts", [P, 2, PARTS, PIECES[0][1]], BF16)
        krest = sb("xk_rest", [P, 2, PIECES[0][1]])
        qpart = sb("xq_parts", [P, PARTS, T], BF16)
        qrest = sb("xq_rest", [P, T])
        xa = sb("xa", [P, QT, D])
        at = sb("attn_rows", [HD, D])
        xT = sb("xT", [P, CH, T])
        ox = sb("ox", [P, QT, D])
        x2 = sb("x2", [P, QT, D])
        x2T = sb("x2T", [P, CH, T])
        hT = sb("hT", [P, NE * EH // P, T])
        err = sb("err", [P, 2, T])
        loss = sb("loss", [P, NDEC])
        l8 = sb("l8", [P, NE])
        pick = sb("pick", [P, NE])
        sc = sb("sc", [P, 4])
        adp = sb("adp", [1, 1], I32)
        stats = sb("xstats", [P, QT, 6])
        meanvar = sb("xmeanvar", [P, QT, 2])
        rstd = sb("xrstd", [P, QT])

        loaded = sem("x_weights_in")
        zeroed = sem("x_zeroed")
        made = sem("x_made")
        exped = sem("x_exped")
        summed = sem("x_summed")
        evac = sem("x_values_out")
        mxd = sem("x_max_made")
        mxr = sem("x_max_read")
        comb_ready = sem("x_max_parts")
        mrow_out = sem("x_max_rows_out")
        max_in = sem("x_max_in")
        w_full = sem("x_work_full")
        w_free = sem("x_work_free")
        khigh = sem("x_k_high")
        kmid = sem("x_k_mid")
        klow = sem("x_k_low")
        kparts_out = [sem(f"x_k_parts_out{i}") for i in range(2)]
        qhigh = sem("x_q_high")
        qmid = sem("x_q_mid")
        qlow = sem("x_q_low")
        qparts_out = sem("x_q_parts_out")
        stacked = sem("x_stacked")
        c_in = sem("x_ctx_in")
        x_in = sem("x_x_in")
        sum_ready = sem("x_summed_x")
        mv_ready = sem("x_meanvar")
        rstd_ready = sem("x_rstd")
        normed = sem("x_normed")
        x1_out = sem("x_x1_out")
        x1_in = sem("x_x1_in")
        e_ready = sem("x_err")
        sq_done = sem("x_err_squared")
        adp_ready = sem("x_adapter")
        adp_in = sem("x_adapter_in")
        out_done = sem("x_out")
        own = {e: sem(f"x_own_{e}") for e in ("dve", "pool")}
        arrived = sem("x_arrived")
        go = sem("x_go")
        cleared = [made, exped, summed, evac, mxd, mxr, comb_ready, mrow_out, max_in, w_full, w_free, khigh, kmid,
                   klow, *kparts_out, qhigh, qmid, qlow, qparts_out, stacked, c_in, x_in, sum_ready, mv_ready,
                   rstd_ready, normed, x1_out, x1_in, e_ready, sq_done, adp_ready, adp_in, out_done,
                   *own.values(), arrived]

        NP = len(PIECES)
        keys = [("kproj", i) for i in range(NP)]
        SLOT_WORK = {
            (0, 0): {0: [("v", 0)], 1: [("v", 1)], 2: [("v", 2)], 3: [("v", 3)], 4: [("oT", 0)], 5: [("oT", 1)],
                     6: [("xo", 0)], 7: [("xo", 1)], 10: [("x2T", 0)], 11: [("max", 1), ("x2T", 1)],
                     12: [("enc", 0)]},
            (0, 1): {0: [("enc", 1)], 1: [("otr", 0), ("enc", 2)], 2: [("enc", 3)], 4: [("norm1",)], 7: [keys[0]], 8: [keys[1]], 9: [keys[2], ("x1T", 0)],
                     10: [keys[3], ("x1T", 1)], 11: [("max", 2)], 12: [("qproj", 0)]},
            (1, 0): {0: [("v", 4)], 1: [("otr", 1), ("v", 5)], 2: [("v", 6)], 3: [("v", 7)],
                     **{4 + i: [("dec", 2 * i), ("dec", 2 * i + 1)] for i in range(7)},
                     11: [("max", 3), ("dec", 14)], 12: [("dec", 15)]},
            (1, 1): {1: [("loss",)], 2: [("otr", 2)], 3: [("kproj", NP)], 4: [("kproj", NP + 1)],
                     5: [("kproj", NP + 2)], 6: [("kproj", NP + 3)], 7: [("qproj", 1)], 8: [("mid",)],
                     9: [("y", 0)], 10: [("y", 1)], 11: [("max", 4)]},
        }
        TAIL = ("oT", "xo", "x2T", "enc", "dec", "loss", "mid", "y")

        def work_at(tail, k, gr, t):
            w = SLOT_WORK[k, gr].get(t, [])
            return [j for j in w if (tail or j[0] not in TAIL) and j != ("norm1",)]

        def body_order(tail):
            w = [j for k in range(CH) for gr in range(NG) for t in range(XKT) for j in work_at(tail, k, gr, t)]
            return w + [("otr", 3)]

        FIRST = Phase(False, keys + [("x1T", 0), ("x1T", 1), ("qproj", 0)] + [("v", i) for i in range(4, 8)]
                      + [("kproj", NP + i) for i in range(NP)] + [("qproj", 1), ("max", 0)])
        BODY0 = Phase(False, body_order(False))
        BODY = Phase(True, body_order(True))
        LAST = Phase(True, [j for kg in SLOT_WORK.values() for t in sorted(kg) for j in kg[t] if j[0] in TAIL])

        def pe_begin(ph, job):
            if ph.order.before(job):
                nc.tensor.wait_ge(w_free, ph.order.before(job))

        def transposes(src, c):
            for q in range(QT):
                last = nc.tensor.transpose(W[:, q * P:(q + 1) * P], src[:, q, c * P:(c + 1) * P], ident[:])
            return last

        def rows_of(lhs, rhs, half, extra=None):
            for i in range(2):
                q = 2 * half + i
                for c in range(CH):
                    last = nc.tensor.matmul(W[:, i * D:(i + 1) * D], lhs[:, c, q * P:(q + 1) * P], rhs[:, c, :],
                                            start=c == 0, stop=c == CH - 1 and extra is None)
                if extra:
                    last = nc.tensor.matmul(W[:, i * D:(i + 1) * D], extra[0][:, q * P:(q + 1) * P], extra[1][:],
                                            start=False, stop=True)
            return last

        def pe_job(ph, job):
            pe = nc.tensor
            name, i = job[0], job[1] if len(job) > 1 else 0
            pe_begin(ph, job)
            if name == "x1T":
                pe.wait_ge(normed, normed_of(ph, "x1"))
                last = transposes(xa, i)
            elif name == "oT":
                last = transposes(ox, i)
            elif name == "x2T":
                pe.wait_ge(normed, normed_of(ph, "x2"))
                last = transposes(x2, i)
            elif name == "xo":
                pe.wait_ge(w_free, ph.order.after(("oT", 1)))
                last = rows_of(x2T, xoT, i)
            elif name == "y":
                pe.wait_ge(w_free, ph.order.after(("mid",)))
                last = rows_of(x2T, wbase, i, (midT, wup))
            elif name == "kproj":
                c, piece = divmod(i, NP)
                k0, n = PIECES[piece]
                pe.wait_ge(c_in, 16)
                for kin in range(CH):
                    last = pe.matmul(W[:, 0:n], xkT[:, kin, c * P:(c + 1) * P], ctxT[:, kin, k0:k0 + n],
                                     start=kin == 0, stop=kin == CH - 1)
            elif name == "qproj":
                pe.wait_ge(w_free, ph.order.after(("x1T", 1)))
                for kin in range(CH):
                    last = pe.matmul(W[:], xqT[:, kin, i * P:(i + 1) * P], xT[:, kin, :],
                                     start=kin == 0, stop=kin == CH - 1)
            elif name == "v":
                c = (i // 4 + 1) % CH
                for tt in range(4 * (i % 4), min(4 * (i % 4) + 4, XKT)):
                    rows = min(P, S2 - tt * P)
                    for kin in range(CH):
                        last = pe.matmul(W[0:rows, (tt % 4) * P:(tt % 4 + 1) * P], ctxT[:, kin, tt * P:tt * P + rows],
                                         xvT[:, kin, c * P:(c + 1) * P], start=kin == 0, stop=kin == CH - 1)
            elif name == "enc":
                pe.wait_ge(w_free, ph.order.after(("x2T", 1)))
                for kin in range(CH):
                    last = pe.matmul(W[:], wenc[:, kin, 2 * i:2 * i + 2, :].rearrange("p n h -> p (n h)"),
                                     x2T[:, kin, :], start=kin == 0, stop=kin == CH - 1)
            elif name == "dec":
                n, c = divmod(i, CH)
                pe.wait_ge(w_free, ph.order.after(("enc", n // 2)))
                last = pe.matmul(W[:], wdec[:, n, c * P:(c + 1) * P], hT[:, n // 2, :], start=True, stop=True)
            elif name == "loss":
                pe.wait_ge(sq_done, NDEC)
                last = pe.matmul(W[:, 0:NDEC], ones[:], loss[:], start=True, stop=True)
            elif name == "mid":
                pe.wait_ge(adp_in, 64)
                for kin in range(CH):
                    last = pe.matmul(W[0:ER, :], wdown[:, kin, :], x2T[:, kin, :], start=kin == 0, stop=kin == CH - 1)
            elif name == "max":
                pe.wait_ge(comb_ready, i if ph is not FIRST else 1)
                last = pe.transpose(Wb[0:2 * GH * QT, 0:P], comb[:].rearrange("p a b -> p (a b)"), ident_b[:])
            elif name == "otr":
                pe.wait_ge(evac, i + 1)
                last = transposes(oS[:].rearrange("p (q n) -> p q n", q=QT), 0)
            last.then_inc(w_full, 1)

        def normed_of(ph, what):
            order = [n for n in ("x2", "x1", "y") if n == "x1" and ph is not LAST or n != "x1" and ph.tail]
            return order.index(what) + 1

        def max_event(e):
            m, x = divmod(e + LEAD * MXS, XKT * MXS)
            return (m + 1, x) if x < MXG else None

        MAXES = [max_event(e) for e in range(XSLOTS * MXS)]
        COUNT = [0]
        for one in MAXES:
            COUNT.append(COUNT[-1] + (one is not None))

        def pe_max_piece(m, x, n):
            pe = nc.tensor
            jq, piece = divmod(x, NP)
            j, q = divmod(jq, QT)
            k, gr = divmod(m, NG)
            k0, w = PIECES[piece]
            h = gr * GH + j
            if n >= 2:
                pe.wait_ge(mxr, n - 1)
            pe.matmul(mx[n % 2][:, 0:w], qst[0:R_MAX, k % 2, h, q * P:(q + 1) * P], kst[0:R_MAX, k % 2, h, k0:k0 + w],
                      start=True, stop=True).then_inc(mxd, 1)

        STACK_DMAS = 2 * len(QPART) + 1

        def pe_max(e):
            one = MAXES[e]
            if one:
                if one == (2, 0):
                    nc.tensor.wait_ge(stacked, 16 * STACK_DMAS)
                if one == (4, 0):
                    nc.tensor.wait_ge(stacked, 32 * STACK_DMAS)
                pe_max_piece(*one, COUNT[e])

        def pe_scores(k, gr, t, ab):
            pe = nc.tensor
            m = NG * k + gr
            sl = XKT * m + t
            if t == 0 and m and ab == 0:
                pe.wait_ge(max_in, 16 * m)
            if sl:
                pe.wait_ge(exped, 2 * (sl - 1) + ab + 1)
            for j in range(2):
                h = gr * GH + 2 * ab + j
                last = pe.matmul(st[ab][:, j, :], kst[0:ROWS, k, h, t * P:(t + 1) * P], qst[0:ROWS, k, h, :],
                                 start=True, stop=True)
            last.then_inc(made, 1)

        def pe_values(ph, sl):
            pe = nc.tensor
            m, t = divmod(sl, XKT)
            k, gr = divmod(m, NG)
            pe.wait_ge(exped, 2 * (sl + 1))
            if t == 0 and m:
                pe.wait_ge(evac, m)
            if t == 0 and m == NG:
                pe.wait_ge(w_free, ph.order.after(("v", 3)))
            for j in range(GH):
                last = pe.matmul(av[32 * j:32 * j + HD + 1, :], vals[:, k, t, gr * GH + j, :], probs[:, sl % 2, j, :],
                                 start=t == 0, stop=t == XKT - 1)
            last.then_inc(summed, 1)

        def pe_body(ph):
            for k in range(CH):
                for gr in range(NG):
                    for t in range(XKT):
                        sl = XKT * (NG * k + gr) + t
                        jobs = work_at(ph.tail, k, gr, t)
                        pe_max(MXS * sl)
                        pe_scores(k, gr, t, 0)
                        pe_max(MXS * sl + 1)
                        pe_scores(k, gr, t, 1)
                        pe_max(MXS * sl + 2)
                        if jobs and sl:
                            pe_job(ph, jobs[0])
                        if sl:
                            pe_values(ph, sl - 1)
                        elif jobs:
                            pe_job(ph, jobs[0])
                        pe_max(MXS * sl + 3)
                        for j in jobs[1:]:
                            pe_job(ph, j)
                        pe_max(MXS * sl + 4)
            pe_values(ph, XSLOTS - 1)
            pe_job(ph, ("otr", 3))

        def act_job(ph, job):
            act = nc.scalar
            name, i = job[0], job[1] if len(job) > 1 else 0
            if name not in ("oT", "x1T", "x2T", "kproj", "qproj", "enc", "mid"):
                return
            act.wait_ge(w_full, ph.order.after(job))
            if name == "x1T":
                act.activation(xT[:, i, :], W[:], ACT.Copy).then_inc(w_free, 1)
            elif name in ("oT", "x2T"):
                act.activation(x2T[:, i, :], W[:], ACT.Copy).then_inc(w_free, 1)
            elif name == "enc":
                act.activation(hT[:, i, :], W[:], ACT.Relu, bias=benc[:, i:i + 1]).then_inc(w_free, 1)
            elif name == "mid":
                act.activation(midT[0:ER, :], W[0:ER, :], ACT.Relu, bias=bdown[:]).then_inc(w_free, 1)
            elif name == "kproj":
                n = PIECES[i % NP][1]
                if i >= 2:
                    act.wait_ge(klow, i - 1)
                    act.wait_ge(kparts_out[i % 2], 48 * (i // 2))
                act.activation(kpart[:, i % 2, 0, 0:n], W[:, 0:n], ACT.Copy).then_inc(khigh, 1)
            elif name == "qproj":
                if i:
                    act.wait_ge(qparts_out, 48)
                act.activation(qpart[:, 0, :], W[:], ACT.Copy, scale=float(HD) ** -0.5).then_inc(qhigh, 1)

        def act_later(ph, job):
            act = nc.scalar
            name, i = job[0], job[1] if len(job) > 1 else 0
            if name == "kproj":
                n = PIECES[i % NP][1]
                act.wait_ge(w_free, ph.order.after(job))
                act.activation(kpart[:, i % 2, 1, 0:n], krest[:, i % 2, 0:n], ACT.Copy).then_inc(kmid, 1)
            elif name == "qproj":
                act.wait_ge(w_free, ph.order.after(job))
                act.activation(qpart[:, 1, :], qrest[:], ACT.Copy).then_inc(qmid, 1)
            elif name == "dec":
                act.wait_ge(w_free, ph.order.after(job))
                act.activation(err[:, i % 2, :], err[:, i % 2, :], ACT.Square,
                               accum_out=loss[:, i:i + 1]).then_inc(sq_done, 1)

        def act_max_out(ph, m, n):
            nc.scalar.wait_ge(w_free, ph.order.after(("max", m)))
            nc.scalar.dma_start(g.max_dram, mrow[:]).then_inc(mrow_out, 16)

        def act_max_in(m, n):
            k, gr = divmod(m, NG)
            nc.scalar.wait_ge(mrow_out, 16 * n)
            nc.scalar.dma_start(qst[R_MAX:ROWS, k % CH, gr * GH:(gr + 1) * GH, :],
                                g.max_dram.rearrange("(r j q) n -> r j (q n)", r=2, j=GH)).then_inc(max_in, 16)

        def act_values_out(m):
            nc.scalar.wait_ge(summed, XKT * (m + 1))
            nc.scalar.activation(oS[:], av[:], ACT.Copy).then_inc(evac, 1)

        def act_body(ph):
            later = []
            for k in range(CH):
                for gr in range(NG):
                    for t in range(XKT):
                        m = NG * k + gr
                        sl = XKT * m + t
                        for ab in range(2):
                            nc.scalar.wait_ge(made, 2 * sl + ab + 1)
                            if sl >= 2:
                                nc.scalar.wait_ge(summed, sl - 1)
                            nc.scalar.activation(probs[:, sl % 2, 2 * ab:2 * ab + 2, :], st[ab][:],
                                                 ACT.Exp).then_inc(exped, 1)
                        if t == 0 and m:
                            if m >= 2:
                                nc.scalar.wait_ge(w_full, ph.order.after(("otr", m - 2)))
                            act_values_out(m - 1)
                        for j in previous_jobs(ph, k, gr, t):
                            act_later(ph, j)
                        for j in work_at(ph.tail, k, gr, t):
                            act_job(ph, j)
                        if t == XKT - 2:
                            act_max_out(ph, m + 1, m + 1)
                        if t == XKT - 1:
                            act_max_in(m + 1, m + 1)
            nc.scalar.wait_ge(w_full, ph.order.after(("otr", CH * NG - 2)))
            act_values_out(CH * NG - 1)

        def previous_jobs(ph, k, gr, t):
            sl = XKT * (NG * k + gr) + t - 1
            if sl < 0:
                return []
            m, t = divmod(sl, XKT)
            return work_at(ph.tail, *divmod(m, NG), t)

        links = {"dve": 0, "mv": 0}

        def dve_link(ins):
            links["dve"] += 1
            ins.then_inc(own["dve"], 1)
            nc.vector.wait_ge(own["dve"], links["dve"])

        def dve_norm(x):
            for q in range(QT):
                last = nc.vector.bn_stats(stats[:, q, :], x[:, q, :])
            dve_link(last)
            for q in range(QT):
                last = nc.vector.bn_aggr(meanvar[:, q, :], stats[:, q, :])
            dve_link(last)
            links["mv"] += 1
            nc.vector.tensor_scalar(rstd[:], meanvar[:, :, 1], EPS, None, ALU.add).then_inc(mv_ready, 1)
            nc.vector.wait_ge(rstd_ready, links["mv"])
            for q in range(QT):
                last = nc.vector.tensor_scalar(x[:, q, :], x[:, q, :], meanvar[:, q, 0:1], rstd[:, q:q + 1],
                                               ALU.subtract, ALU.mult)
            last.then_inc(normed, 1)

        def dve_norm1():
            nc.vector.wait_ge(sum_ready, 1)
            dve_norm(xa)

        def dve_choose():
            v = nc.vector
            dve_link(v.tensor_reduce(l8[:], W[:, 0:NDEC].rearrange("p (n c) -> p n c", c=CH), AX.X, ALU.add))
            v.tensor_copy(sc[:, 3:4], l8[:, 0:1]).then_inc(w_free, 1)
            dve_link(v.tensor_reduce(sc[:, 0:1], l8[:], AX.X, ALU.min))
            dve_link(v.tensor_scalar(pick[:], l8[:], sc[:, 0:1], None, ALU.is_le))
            dve_link(v.tensor_tensor(pick[:], pick[:], iotam[:], ALU.mult))
            dve_link(v.tensor_reduce(sc[:, 1:2], pick[:], AX.X, ALU.min))
            dve_link(v.tensor_scalar(pick[:], iotam[:], sc[:, 1:2], None, ALU.is_equal))
            dve_link(v.tensor_tensor(pick[:], pick[:], cidxf[:], ALU.mult))
            dve_link(v.tensor_reduce(sc[:, 2:3], pick[:], AX.X, ALU.add))
            dve_link(v.tensor_scalar(sc[:, 3:4], sc[:, 2:3], 0.0, float(NE), ALU.is_lt, ALU.mult))
            dve_link(v.tensor_tensor(sc[:, 2:3], sc[:, 2:3], sc[:, 3:4], ALU.add))
            dve_link(v.tensor_scalar(sc[:, 2:3], sc[:, 2:3], 0.0, float(NE - 1), ALU.max, ALU.min))
            v.tensor_copy(adp[:], sc[0:1, 2:3]).then_inc(adp_ready, 1)

        def dve_job(ph, job):
            v = nc.vector
            name, i = job[0], job[1] if len(job) > 1 else 0
            if name not in ("kproj", "qproj", "xo", "y", "v", "dec", "loss", "max", "otr"):
                return
            v.wait_ge(w_full, ph.order.after(job))
            W2 = W[:].rearrange("p (q d) -> p q d", q=2)
            if name == "kproj":
                n = PIECES[i % NP][1]
                v.wait_ge(khigh, i + 1)
                if i >= 2:
                    v.wait_ge(klow, i - 1)
                v.tensor_tensor(krest[:, i % 2, 0:n], W[:, 0:n], kpart[:, i % 2, 0, 0:n],
                                ALU.subtract).then_inc(w_free, 1)
            elif name == "qproj":
                v.wait_ge(qhigh, i + 1)
                if i:
                    v.wait_ge(qlow, 1)
                v.scalar_tensor_tensor(qrest[:], W[:], float(HD) ** -0.5, qpart[:, 0, :], ALU.mult,
                                       ALU.subtract).then_inc(w_free, 1)
            elif name in ("xo", "y"):
                if name == "xo" and i == 0:
                    v.wait_ge(x1_in, 16)
                v.tensor_tensor(x2[:, 2 * i:2 * i + 2, :], W2, x2[:, 2 * i:2 * i + 2, :], ALU.add).then_inc(w_free, 1)
                if i == 1:
                    v.wait_ge(w_free, ph.order.after(job))
                    dve_norm(x2)
            elif name == "v":
                c = (i // 4 + 1) % CH
                tiles = range(4 * (i % 4), min(4 * (i % 4) + 4, XKT))
                full = [tt for tt in tiles if (tt + 1) * P <= S2]
                if full:
                    v.tensor_copy(vals[:, c, full[0]:full[-1] + 1, :, 0:HD],
                                  W[:, 0:len(full) * P].rearrange("p (t h d) -> p t h d", t=len(full), d=HD)
                                  ).then_inc(w_free, 1)
                else:
                    rows = S2 - tiles[0] * P
                    v.tensor_copy(vals[0:rows, c, tiles[0], :, 0:HD],
                                  W[0:rows, 0:P].rearrange("p (h d) -> p h d", d=HD)).then_inc(w_free, 1)
            elif name == "dec":
                n, c = divmod(i, CH)
                if i >= 2:
                    v.wait_ge(sq_done, i - 1)
                v.scalar_tensor_tensor(err[:, i % 2, :], W[:], bdec[:, n, c:c + 1], x2T[:, c, :], ALU.add,
                                       ALU.subtract).then_inc(w_free, 1)
            elif name == "loss":
                dve_choose()
            elif name == "max":
                if ph is not FIRST and i >= 2:
                    v.wait_ge(mrow_out, 16 * (i - 1))
                v.tensor_copy(mrow[:], Wb[0:2 * GH * QT, 0:P]).then_inc(w_free, 1)
            elif name == "otr":
                w4 = W[:].rearrange("p (q j r) -> p q j r", q=QT, r=2 * HD)
                dve_link(v.reciprocal(rz[:], w4[:, :, :, HD]))
                v.tensor_tensor(ox[:, :, i * GH * HD:(i + 1) * GH * HD].rearrange("p q (j d) -> p q j d", d=HD),
                                w4[:, :, :, 0:HD], rz[:].unsqueeze(3).broadcast_to([P, QT, GH, HD]),
                                ALU.mult).then_inc(w_free, 1)

        def dve_max_piece(x, n):
            w = PIECES[x % NP][1]
            nc.vector.wait_ge(mxd, n + 1)
            nc.vector.tensor_reduce(nmp[:, x // NP, x % NP:x % NP + 1], mx[n % 2][:, 0:w], AX.X, ALU.max,
                                    negate=True).then_inc(mxr, 1)

        def dve_max(e):
            if MAXES[e]:
                dve_max_piece(MAXES[e][1], COUNT[e])

        def dve_max_parts(ph, n_read, n):
            nc.vector.wait_ge(mxr, n_read)
            dve_link(nc.vector.tensor_reduce(nm[:], nmp[:], AX.X, ALU.min))
            if n >= 2:
                nc.vector.wait_ge(w_full, ph.order.after(("max", n - 1)))
            dve_link(nc.vector.tensor_copy(comb[:, 0, :], nm[:]))
            nc.vector.tensor_tensor(comb[:, 1, :], nm[:], comb[:, 0, :], ALU.subtract).then_inc(comb_ready, 1)

        def dve_body(ph):
            for k in range(CH):
                for gr in range(NG):
                    for t in range(XKT):
                        m = NG * k + gr
                        sl = XKT * m + t
                        jobs = work_at(ph.tail, k, gr, t)
                        if t == XKT - 2:
                            dve_max_parts(ph, COUNT[MXS * sl], m + 1)
                        for i in range(3):
                            dve_max(MXS * sl + i)
                        if jobs:
                            dve_job(ph, jobs[0])
                        dve_max(MXS * sl + 3)
                        for j in jobs[1:]:
                            dve_job(ph, j)
                        if ("norm1",) in SLOT_WORK[k, gr].get(t, []):
                            dve_norm1()
                        dve_max(MXS * sl + 4)
            dve_job(ph, ("otr", 3))

        def pool_sum():
            p = nc.gpsimd
            p.wait_ge(x_in, 32)
            p.tensor_tensor(xa[:], xa[:], bo[:].unsqueeze(1).broadcast_to([P, QT, D]), ALU.add).then_inc(own["pool"], 1)
            p.wait_ge(own["pool"], 1)
            p.tensor_tensor(xa[0:HD, 0, :], xa[0:HD, 0, :], at[:], ALU.add).then_inc(sum_ready, 1)

        def pool_rstd(n):
            nc.gpsimd.wait_ge(mv_ready, n)
            nc.gpsimd.tensor_tensor(rstd[:], rstd[:], g.mhalf[:, 0:QT], ALU.pow).then_inc(rstd_ready, 1)

        def pool_klow(i):
            n = PIECES[i % NP][1]
            nc.gpsimd.wait_ge(kmid, i + 1)
            nc.gpsimd.tensor_tensor(kpart[:, i % 2, 2, 0:n], krest[:, i % 2, 0:n], kpart[:, i % 2, 1, 0:n],
                                    ALU.subtract).then_inc(klow, 1)

        def pool_qlow(i):
            nc.gpsimd.wait_ge(qmid, i + 1)
            nc.gpsimd.tensor_tensor(qpart[:, 2, :], qrest[:], qpart[:, 1, :], ALU.subtract).then_inc(qlow, 1)

        def pool_body(ph):
            if ph.tail:
                pool_rstd(1)
            pool_sum()
            pool_rstd(1 + ph.tail)
            for i in range(NP):
                pool_klow(i)
            pool_qlow(0)
            for i in range(NP):
                pool_klow(NP + i)
            pool_qlow(1)
            if ph.tail:
                pool_rstd(3)

        def sp_load_x(b):
            nc.sync.dma_start(xa[:], g.x[bass.ds(b, 1)].rearrange("b (q p) d -> p (b q) d", p=P)).then_inc(x_in, 16)
            nc.sync.dma_start(at[:], g.attn_dram[bass.ds(b, 1)].rearrange("b t d -> (b t) d")).then_inc(x_in, 16)

        def sp_load_ctx(b):
            nc.sync.dma_start(ctxT[:], g.ctxT[bass.ds(b, 1)].rearrange("b (c p) n -> p (b c) n", p=P)).then_inc(c_in, 16)

        def sp_key_parts(i, read):
            k0, n = PIECES[i % NP]
            if i % NP == 0 and read:
                nc.sync.wait_ge(stacked, read)
            nc.sync.wait_ge(khigh, i + 1)
            nc.sync.wait_ge(kmid, i + 1)
            nc.sync.wait_ge(klow, i + 1)
            for part in range(PARTS):
                nc.sync.dma_start(g.kpart_dram[part, :, k0:k0 + n], kpart[:, i % 2, part, 0:n]).then_inc(kparts_out[i % 2], 16)

        def sp_key_parts_out(n):
            for i in range(2):
                nc.sync.wait_ge(kparts_out[i], 48 * (n * NP // 2))

        def sp_query_parts(i):
            nc.sync.wait_ge(qlow, i + 1)
            nc.sync.wait_ge(qmid, i + 1)
            for part in range(PARTS):
                nc.sync.dma_start(g.part_dram[part], qpart[:, part, :]).then_inc(qparts_out, 16)

        def sp_stacks(b, c):
            for j, (pq, pk) in enumerate(zip(QPART, KPART)):
                rows = slice(HD * j, HD * (j + 1))
                nc.sync.dma_start(kst[rows, c, :, 0:S2],
                                  g.kpart_dram[pk].rearrange("(h d) n -> d h n", d=HD)).then_inc(stacked, 16)
                nc.sync.dma_start(qst[rows, c, :, :],
                                  g.part_dram[pq].rearrange("(h d) n -> d h n", d=HD)).then_inc(stacked, 16)
            nc.sync.dma_start(kst[R_MASK:R_MASK + 1, c, :, :],
                              g.mask_dram[bass.ds(b, 1)].unsqueeze(1).broadcast_to([1, HC, SP_])).then_inc(stacked, 16)

        def sp_load_x1(b):
            nc.sync.dma_start(x2[:], g.x1_dram[bass.ds(b, 1)].rearrange("b (q p) d -> p (b q) d", p=P)).then_inc(x1_in, 16)

        def sp_store_x1(ph, b):
            nc.sync.wait_ge(normed, normed_of(ph, "x1"))
            nc.sync.dma_start(g.x1_dram[bass.ds(b, 1)].rearrange("b (q p) d -> p (b q) d", p=P), xa[:]).then_inc(x1_out, 16)

        def sp_adapter():
            sp = nc.sync
            sp.wait_ge(adp_ready, 1)
            n = sp.value_load(adp[0:1, 0:1], min_val=0, max_val=NE - 1)
            sp.dma_start(wdown[:], g.Wdown[bass.ds(n, 1)].rearrange("n (c p) r -> p (n c) r", p=P)).then_inc(adp_in, 16)
            sp.dma_start(wup[0:ER, :], g.Wup[bass.ds(n, 1)].rearrange("n r d -> (n r) d")).then_inc(adp_in, 16)
            sp.dma_start(wup[ER:ER + 1, :], g.bup[bass.ds(n, 1)]).then_inc(adp_in, 16)
            with nc.allow_non_contiguous_dma(reason="a bias column"):
                sp.dma_start(bdown[:], g.bdown[bass.ds(n, 1)].rearrange("n r -> r n")).then_inc(adp_in, 16)

        def sp_store_out(ph, b):
            nc.sync.wait_ge(normed, normed_of(ph, "y"))
            nc.sync.dma_start(g.out[bass.ds(b, 1)].rearrange("b (q p) d -> p (b q) d", p=P), x2[:]).then_inc(out_done, 16)

        def sp_body(ph, b, nxt):
            if ph.tail:
                sp_load_x1(b - 1)
            sp_load_x(nxt)
            sp_stacks(b, 1)
            nc.sync.wait_ge(w_full, ph.order.after(("v", 3)))
            sp_load_ctx(nxt)
            sp_store_x1(ph, nxt)
            for i in range(NP):
                sp_key_parts(i, 16 * STACK_DMAS)
            sp_query_parts(0)
            nc.sync.wait_ge(made, 2 * NG * XKT)
            sp_key_parts_out(1)
            nc.sync.wait_ge(qparts_out, 48)
            sp_stacks(nxt, 0)
            if ph.tail:
                sp_adapter()
            for i in range(NP):
                sp_key_parts(NP + i, 32 * STACK_DMAS)
            sp_query_parts(1)
            if ph.tail:
                sp_store_out(ph, b - 1)
                nc.sync.wait_ge(out_done, 16)
            nc.sync.wait_ge(x1_out, 16)
            sp_key_parts_out(2)
            nc.sync.wait_ge(qparts_out, 96)
            nc.sync.wait_ge(stacked, 32 * STACK_DMAS)
            nc.sync.wait_ge(max_in, 16 * NG * CH)

        first_pieces = [(0, x) for x in range(MXG)] + [(1, x) for x in range(LEAD * MXS)]
        N_LOADS = 16 * (5 + 2 * NE + 6)
        with nc.Block() as blk:
            @blk.sync
            def _(sp):
                n = 0
                sp_load_x(0)
                sp_load_ctx(0)
                sp.wait_ge(zeroed, 3)
                with nc.allow_non_contiguous_dma(reason="bias columns and rows, once"):
                    for dst, src in ((xqT[:], g.xWqT), (xkT[:], g.xWkT), (xvT[:], g.xWvT),
                                     (xoT[:], g.xWoT), (wbase[:], g.Wbase)):
                        sp.dma_start(dst, src.rearrange("(c p) d -> p c d", p=P)).then_inc(loaded, 16)
                        n += 16
                    for e in range(NE):
                        sp.dma_start(wenc[:, :, e, :], g.Wenc[e].rearrange("(c p) h -> p c h", p=P)).then_inc(loaded, 16)
                        half = EH * (e % 2)
                        sp.dma_start(wdec[half:half + EH, e, :], g.Wdec[e]).then_inc(loaded, 16)
                        n += 32
                    for dst, src in ((bo[:], g.bo.unsqueeze(0).broadcast_to([P, D])),
                                     (benc[:], g.benc.rearrange("n h -> (n h)").rearrange("(j p) -> p j", p=P)),
                                     (bdec[:], g.bdec.rearrange("n (c p) -> p n c", p=P)),
                                     (cidx[:], g.cidx.unsqueeze(0).broadcast_to([P, NE])),
                                     (iota[:], g.c_iota.broadcast_to([P, NE])),
                                     (wup[ER + 1:ER + 2, :], g.bbase.unsqueeze(0))):
                        sp.dma_start(dst, src).then_inc(loaded, 16)
                        n += 16
                assert n == N_LOADS
                sp_store_x1(FIRST, 0)
                for i in range(NP):
                    sp_key_parts(i, 0)
                sp_query_parts(0)
                sp_key_parts_out(1)
                sp.wait_ge(qparts_out, 48)
                sp_stacks(0, 0)
                for i in range(NP):
                    sp_key_parts(NP + i, 16 * STACK_DMAS)
                sp_query_parts(1)
                sp.wait_ge(x1_out, 16)
                sp_key_parts_out(2)
                sp.wait_ge(qparts_out, 96)
                sp.wait_ge(max_in, 16)
                sp.wait_ge(loaded, N_LOADS)

            @blk.gpsimd
            def _(pool):
                p = nc.gpsimd
                p.memset(wdec[:], 0.0).then_inc(zeroed, 1)
                p.memset(ones[:], 1.0).then_inc(zeroed, 1)
                pool.wait_ge(zeroed, 2)
                p.memset(midT[ER:ER + 2, :], 1.0).then_inc(zeroed, 1)
                pool.wait_ge(zeroed, 3)
                p.memset(kst[64:128, :, :, :], 1.0).then_inc(zeroed, 1)
                pool.wait_ge(zeroed, 4)
                p.memset(qst[96:128, :, :, :], 1.0).then_inc(zeroed, 1)
                pool.wait_ge(zeroed, 5)
                p.memset(kst[0:96, :, :, S2:SP_], 0.0).then_inc(zeroed, 1)
                pool.wait_ge(zeroed, 6)
                p.memset(vals[:], 0.0).then_inc(zeroed, 1)
                pool.wait_ge(zeroed, 7)
                p.memset(vals[:, :, :, :, HD:HD + 1], 1.0).then_inc(zeroed, 1)
                pool.wait_ge(loaded, N_LOADS)
                pool.wait_ge(zeroed, 8)
                pool_sum()
                pool_rstd(1)
                for i in range(NP):
                    pool_klow(i)
                pool_qlow(0)
                for i in range(NP):
                    pool_klow(NP + i)
                pool_qlow(1)

            first_jobs = FIRST.order.names

            @blk.scalar
            def _(act):
                before = None
                for job in first_jobs[:-1]:
                    if before:
                        act_later(FIRST, before)
                    act_job(FIRST, job)
                    before = job
                act_later(FIRST, before)
                act_max_out(FIRST, 0, 1)
                act_max_in(0, 1)

            @blk.vector
            def _(dve):
                v = nc.vector
                dve.wait_ge(zeroed, 8)
                dve_link(v.memset(av[:], 0.0))
                dve.wait_ge(loaded, N_LOADS)
                dve_link(v.tensor_copy(cidxf[:], cidx[:]))
                dve_link(v.tensor_scalar(iotam[:], iota[:], float(NE), None, ALU.subtract))
                dve_norm1()
                for job in first_jobs[:-1]:
                    dve_job(FIRST, job)
                for n, (m, x) in enumerate(first_pieces):
                    if n == MXG:
                        dve_max_parts(FIRST, MXG, 1)
                        dve_job(FIRST, ("max", 0))
                    dve_max_piece(x, n)

            @blk.tensor
            def _(pe):
                pe.wait_ge(loaded, N_LOADS)
                pe.wait_ge(zeroed, 8)
                for job in first_jobs[:-1]:
                    pe_job(FIRST, job)
                for n, (m, x) in enumerate(first_pieces):
                    if n == 0:
                        pe.wait_ge(stacked, 16 * STACK_DMAS)
                    if n == MXG:
                        pe_job(FIRST, ("max", 0))
                    pe_max_piece(m, x, n)

        def clear():
            with nc.Block() as blk:
                @blk.sync
                def _(sp):
                    for one in cleared:
                        sp.sem_clear(one)
            links.update(dve=0, mv=0)

        clear()

        with nc.Block() as blk:
            @blk.tensor
            def _(pe):
                pe_body(BODY0)

            @blk.scalar
            def _(act):
                act_body(BODY0)

            @blk.vector
            def _(dve):
                dve_body(BODY0)

            @blk.gpsimd
            def _(pool):
                pool_body(BODY0)

            @blk.sync
            def _(sp):
                sp_body(BODY0, 0, 1)

        clear()

        def leave(eng, i):
            eng.drain().then_inc(arrived, 1)
            eng.wait_ge(go, i)

        with nc.Block() as blk:
            @blk.tensor
            def _(pe):
                with pe.Fori(1, B) as i:
                    pe_body(BODY)
                    leave(pe, i)

            @blk.scalar
            def _(act):
                with act.Fori(1, B) as i:
                    act_body(BODY)
                    leave(act, i)

            @blk.vector
            def _(dve):
                with dve.Fori(1, B) as i:
                    dve_body(BODY)
                    leave(dve, i)

            @blk.gpsimd
            def _(pool):
                with pool.Fori(1, B) as i:
                    pool_body(BODY)
                    leave(pool, i)

            @blk.sync
            def _(sp):
                with sp.Fori(1, B) as i:
                    sp_body(BODY, i, (i + 1) % B)
                    sp.wait_ge(arrived, 4)
                    for one in cleared:
                        sp.sem_clear(one)
                    sp.sem_inc(go, 1)

        links.update(dve=0, mv=0)

        with nc.Block() as blk:
            last_jobs = LAST.order.names

            @blk.sync
            def _(sp):
                sp_load_x1(B - 1)
                sp_adapter()
                sp_store_out(LAST, B - 1)
                sp.wait_ge(out_done, 16)

            @blk.gpsimd
            def _(pool):
                pool_rstd(1)
                pool_rstd(2)

            @blk.scalar
            def _(act):
                before = None
                for job in last_jobs:
                    if before:
                        act_later(LAST, before)
                    act_job(LAST, job)
                    before = job

            @blk.vector
            def _(dve):
                for job in last_jobs:
                    dve_job(LAST, job)

            @blk.tensor
            def _(pe):
                for job in last_jobs:
                    pe_job(LAST, job)


def constants():
    import numpy as np
    head = np.arange(P)[:, None] // HD == np.arange(HC)[None]
    batch = np.arange(TOK) // HD
    return {
        "c_ident": np.eye(P, dtype=np.float32),
        "c_head": head.astype(np.float32),
        "c_hide": np.where(batch[:, None] == batch[None], 0.0, NEG).astype(np.float32),
        "c_iota": np.arange(NE, dtype=np.float32)[None],
    }


def layout(inputs):
    import numpy as np
    a = {k: np.asarray(v) for k, v in inputs.items()}

    def t(name):
        return np.ascontiguousarray(a[name].T)

    r = {"x": a["x"], "ctxT": np.ascontiguousarray(a["ctx_1024"].transpose(0, 2, 1)),
         "mask": np.ascontiguousarray(a["mask_Bx1x1xS2_bf1"]).view(np.uint8).reshape(B, S2),
         **{f"W{n}T": t(f"L0_attn_W{n}") for n in ("q", "k", "v", "o", "lq", "lk", "lv")},
         "xWqT": t("L0_xattn_Wq"), "xWkT": t("L0_xattn_Wk"), "xWvT": t("L0_xattn_Wv"),
         "xWoT": t("L0_xattn_Wo")}
    for k, n in (("bq", "bq"), ("bv", "bv"), ("bo", "bo"), ("lna", "lna_w"), ("lnc", "lnc_w"), ("lnd", "lnd_w"),
                 ("blq", "blq"), ("blk", "blk"), ("blv", "blv")):
        r[k] = a[f"L0_attn_{n}"]
    for k in ("temp", "threshold", "factor"):
        r[k] = a[f"L0_attn_{k}"].reshape(1, 1)
    for k, n in (("Wbase", "W_base"), ("bbase", "b_base"), ("Wenc", "W_enc"), ("benc", "b_enc"), ("Wdec", "W_dec"),
                 ("bdec", "b_dec"), ("Wdown", "W_down"), ("bdown", "b_down"), ("Wup", "W_up"), ("bup", "b_up"),
                 ("cidx", "connected_idx")):
        r[k] = a[f"L0_ffn_{n}"]
    return {**r, **constants()}


def kernel(**inputs):
    import numpy as np
    import concourse.bacc as bacc
    from concourse.bass_utils import run_bass_kernel_spmd

    nc = bacc.Bacc("TRN2", target_bir_lowering=False, num_devices=1)
    arrays = {f"in_{k}": np.ascontiguousarray(v) for k, v in layout(inputs).items()}
    g = Shared({k[3:]: nc.dram_tensor(k, v.shape, mybir.dt.from_np(v.dtype), kind="ExternalInput").ap()
                for k, v in arrays.items()})
    g.out = nc.dram_tensor("out_dram", (B, T, D), F32, kind="ExternalOutput").ap()
    program(nc, g)
    r = run_bass_kernel_spmd(nc, [arrays], core_ids=[0])
    return r.results[0]["out_dram"]
```

```python
from contextlib import ExitStack

import concourse.bass as bass
from concourse import mybir

F32 = mybir.dt.float32
BF16 = mybir.dt.bfloat16
U8 = mybir.dt.uint8
I32 = mybir.dt.int32
ALU = mybir.AluOpType
ACT = mybir.ActivationFunctionType
AX = mybir.AxisListType

P = 128
B, T, D = 8, 512, 256
H, HD = 16, 16
S2 = 1601
QT = T // P
CH = D // P
HC = P // HD
GH = 4
NG = HC // GH
ITERS = 3
TOK = B * HD
EPS = 1e-5
SRING, MRING = 3, 3
NEG = -1e30
PARTS = 3
QPART = (0, 0, 1, 0, 1, 2)
KPART = (0, 1, 0, 2, 1, 0)
R_MASK = 6 * HD
R_MAX = R_MASK + 1
ROWS = R_MAX + 2


class Shared:

    def __init__(self, a):
        self.x, self.ctxT, self.mask = a["x"], a["ctxT"], a["mask"]
        self.WqT, self.WkT, self.WvT, self.WoT = a["WqT"], a["WkT"], a["WvT"], a["WoT"]
        self.WlqT, self.WlkT, self.WlvT = a["WlqT"], a["WlkT"], a["WlvT"]
        self.bq, self.bv, self.bo, self.blq, self.blk, self.blv = a["bq"], a["bv"], a["bo"], a["blq"], a["blk"], a["blv"]
        self.lna, self.lnc, self.lnd = a["lna"], a["lnc"], a["lnd"]
        self.temp, self.threshold, self.factor = a["temp"], a["threshold"], a["factor"]
        self.xWqT, self.xWkT, self.xWvT, self.xWoT = a["xWqT"], a["xWkT"], a["xWvT"], a["xWoT"]
        self.Wbase, self.bbase, self.Wenc, self.benc = a["Wbase"], a["bbase"], a["Wenc"], a["benc"]
        self.Wdec, self.bdec, self.Wdown, self.bdown = a["Wdec"], a["bdec"], a["Wdown"], a["bdown"]
        self.Wup, self.bup, self.cidx = a["Wup"], a["bup"], a["cidx"]
        self.c_ident, self.c_head, self.c_hide, self.c_iota = a["c_ident"], a["c_head"], a["c_hide"], a["c_iota"]


class Phase:

    def __init__(self, tail, order):
        self.tail, self.order = tail, Order(order)


class Order:

    def __init__(self, names):
        self.names = list(names)
        self.index = {n: i for i, n in enumerate(self.names)}

    def before(self, name):
        return self.index[name]

    def after(self, name):
        return self.index[name] + 1


def sbuf(nc, stack, name, shape, dt=F32):
    return stack.enter_context(nc.sbuf_tensor(name, shape, dt))


def program(nc, g):
    with ExitStack() as whole:
        g.sem = lambda name: whole.enter_context(nc.semaphore(name))
        banks = whole.enter_context(nc.psum_tensor("banks", [P, 6, T], F32))
        g.st = [banks[:, 2 * i:2 * i + 2, :] for i in range(2)]
        g.mx = [banks[:, 4 + i, :] for i in range(2)]
        g.scores = [banks[:, i, :] for i in range(SRING)]
        g.max_scores = [banks[:, SRING + i, :] for i in range(MRING)]
        g.av = whole.enter_context(nc.psum_tensor("values", [P, T], F32))
        g.W = whole.enter_context(nc.psum_tensor("work", [P, T], F32))
        g.ident = sbuf(nc, whole, "ident", [P, P])
        g.ident_b = sbuf(nc, whole, "ident_b", [P, P], BF16)
        g.mhalf = sbuf(nc, whole, "mhalf", [P, 2 * H])
        g.attn_dram = nc.dram_tensor("attn_dram", (B, HD, D), F32, kind="Internal").ap()
        g.part_dram = nc.dram_tensor("parts_dram", (PARTS, P, T), BF16, kind="Internal").ap()
        g.kpart_dram = nc.dram_tensor("key_parts_dram", (PARTS, P, S2), BF16, kind="Internal").ap()
        g.mask_dram = nc.dram_tensor("mask_dram", (B, SP_), BF16, kind="Internal").ap()
        g.x1_dram = nc.dram_tensor("x1_dram", (B, T, D), F32, kind="Internal").ap()
        g.max_dram = nc.dram_tensor("max_dram", (2 * GH * QT, P), BF16, kind="Internal").ap()

        short_self_attention(nc, g)
        cross_attention_and_ffn(nc, g)


def short_self_attention(nc, g):
    ident, W, av, st, mx, sem = g.ident, g.W, g.av, g.st, g.mx, g.sem
    with ExitStack() as s:
        def sb(name, shape, dt=F32):
            return sbuf(nc, s, name, shape, dt)

        x = sb("s_x", [TOK, D])
        wq, wk, wv, wo = (sb(f"s_w{n}", [P, CH, D]) for n in "qkvo")
        wl = [sb(f"s_wl{n}", [P, P]) for n in "qkv"]
        bq, bv = (sb(f"s_b{n}", [P, CH]) for n in "qv")
        bl = sb("s_bl", [TOK, 3, HD])
        lna = sb("s_lna", [TOK, D])
        lncd = sb("s_lncd", [TOK, 2, HD])
        tt = sb("s_t", [TOK, ITERS])
        tf = sb("s_threshold_factor", [P, 2])
        head = sb("s_head_mask", [P, HC])
        hide = sb("s_hide", [TOK, TOK])
        m8 = sb("s_mask_bytes", [B, S2], U8)
        tone, tpos, tpow = (sb(n, [TOK, ITERS]) for n in ("s_tone", "s_tpos", "s_tpow"))
        ln_w = sb("s_ln_w", [TOK, ITERS, 2, HD])
        stats = sb("s_stats", [TOK, 6])
        meanvar = sb("s_meanvar", [TOK, 2])
        xn = sb("s_xn", [TOK, D])
        xnT = sb("s_xnT", [P, CH, TOK])
        state = sb("s_state", [P, 3, CH, TOK])
        rows = sb("s_rows", [TOK, 3, H, HD])
        cen = sb("s_centered", [TOK, 2 * H, HD])
        sq = sb("s_squares", [TOK, 2 * H, HD])
        msum = sb("s_sums", [TOK, 2 * H])
        var = sb("s_vars", [TOK, 2 * H])
        qsT = sb("s_qsT", [P, CH, TOK])
        ksM = sb("s_ksM", [P, CH, HC, TOK])
        sc = sb("s_scores", [TOK, H, TOK])
        nmax = sb("s_neg_max", [TOK, H])
        rsum = sb("s_rsum", [TOK, H])
        pT = sb("s_probsT", [TOK, H, TOK])
        outs = sb("s_outs", [TOK, ITERS, D])
        adiff = sb("s_abs_diff", [TOK, D])
        asum = sb("s_abs_sum", [TOK, 1])
        ones = sb("s_ones", [P, P])
        diff, lim, keep, other = (sb(n, [P, 1]) for n in ("s_diff", "s_lim", "s_keep", "s_other"))
        proj = sb("s_proj", [TOK, D])
        mb = sb("s_mask_addend", [B, SP_], BF16)

        early = sem("s_early_in")
        loaded = sem("s_in")
        zeroed = sem("s_zeroed")
        own = sem("s_own")
        xn_ready = sem("s_x_normed")
        bias_ready = sem("s_bias")
        kv_made = sem("s_kv_transposed")
        oT_made = sem("s_out_transposed")
        diff_ready = sem("s_diff")
        asum_ready = sem("s_abs")
        sel_ready = sem("s_selected")
        mm = sem("s_products")
        read = sem("s_read")
        var_ready = sem("s_var")
        root_ready = sem("s_roots")
        cen_ready = sem("s_centered_in")
        sq_ready = sem("s_squared")
        qk_ready = sem("s_qk_normed")
        rows_ready = sem("s_rows_in")
        t_ready = sem("s_transposed")
        sc_ready = sem("s_scored")
        p_ready = sem("s_exped")
        p_out = sem("s_probs_taken")
        o_ready = sem("s_out")
        st_ready = sem("s_state_in")
        mask_ready = sem("s_mask")
        stored = sem("s_stored")
        early_n = 16 * (B + 2)
        loaded_n = 16 * (4 + 3 * HC + 2 + 3 + 2 + ITERS + 2 + 2 + 1)
        MMS = 8

        with nc.Block() as blk:
            @blk.sync
            def _(sp):
                for b in range(B):
                    sp.dma_start(x[b * HD:(b + 1) * HD, :], g.x[b, 0:HD, :]).then_inc(early, 16)
                sp.dma_start(ident[:], g.c_ident).then_inc(early, 16)
                sp.dma_start(lna[:], g.lna.unsqueeze(0).broadcast_to([TOK, D])).then_inc(early, 16)
                for dst, src in ((wq, g.WqT), (wk, g.WkT), (wv, g.WvT), (wo, g.WoT)):
                    sp.dma_start(dst[:], src.rearrange("(c p) d -> p c d", p=P)).then_inc(loaded, 16)
                with nc.allow_non_contiguous_dma(reason="small vectors, once"):
                    for dst, src in ((bq, g.bq), (bv, g.bv)):
                        sp.dma_start(dst[:], src.rearrange("(c p) -> p c", p=P)).then_inc(loaded, 16)
                for i, src in enumerate((g.blq, g.blk, g.blv)):
                    sp.dma_start(bl[:, i, :], src.unsqueeze(0).broadcast_to([TOK, HD])).then_inc(loaded, 16)
                for i, src in enumerate((g.lnc, g.lnd)):
                    sp.dma_start(lncd[:, i, :], src.unsqueeze(0).broadcast_to([TOK, HD])).then_inc(loaded, 16)
                for i in range(ITERS):
                    sp.dma_start(tt[:, i:i + 1], g.temp.to_broadcast([TOK, 1])).then_inc(loaded, 16)
                sp.dma_start(tf[:, 0:1], g.threshold.to_broadcast([P, 1])).then_inc(loaded, 16)
                sp.dma_start(tf[:, 1:2], g.factor.to_broadcast([P, 1])).then_inc(loaded, 16)
                sp.dma_start(head[:], g.c_head).then_inc(loaded, 16)
                sp.dma_start(hide[:], g.c_hide).then_inc(loaded, 16)
                sp.dma_start(m8[:], g.mask).then_inc(loaded, 16)
                sp.wait_ge(mask_ready, 1)
                sp.dma_start(g.mask_dram, mb[:]).then_inc(stored, 16)
                sp.wait_ge(read, 3)
                sp.dma_start(g.attn_dram.rearrange("b t d -> (b t) d"), proj[:]).then_inc(stored, 16)
                sp.wait_ge(stored, 32)

            @blk.gpsimd
            def _(pool):
                p = nc.gpsimd
                for n, one in enumerate(wl):
                    p.memset(one[:], 0.0).then_inc(zeroed, 1)
                p.memset(g.mhalf[:], -0.5).then_inc(zeroed, 1)
                p.memset(ones[:], 1.0).then_inc(zeroed, 1)
                p.memset(mb[:], NEG).then_inc(zeroed, 1)
                pool.wait_ge(zeroed, 6)

                def root(buf, n):
                    pool.wait_ge(var_ready, n)
                    p.tensor_tensor(buf, buf, g.mhalf[:, 0:buf.shape[-1]], ALU.pow).then_inc(root_ready, 1)

                root(meanvar[:, 1:2], 1)
                root(tpow[:], 2)
                for it in range(ITERS):
                    root(var[:], 3 + it)

            @blk.scalar
            def _(act):
                a = nc.scalar
                act.wait_ge(zeroed, 3)
                for i, src in enumerate((g.WlqT, g.WlkT, g.WlvT)):
                    for h in range(HC):
                        act.dma_start(wl[i][h * HD:(h + 1) * HD, h * HD:(h + 1) * HD], src).then_inc(loaded, 16)
                act.wait_ge(mm, 1)
                a.activation(xnT[:], W[:, 0:D].rearrange("p (c t) -> p c t", c=CH), ACT.Copy).then_inc(read, 1)
                act.wait_ge(loaded, loaded_n)
                act.wait_ge(bias_ready, 1)
                for i, bank in enumerate((W, mx[0], mx[1])):
                    act.wait_ge(mm, 2 + i)
                    for c in range(CH):
                        src = bank[:, c * TOK:(c + 1) * TOK]
                        if i == 0:
                            last = a.activation(state[:, i, c, :], src, ACT.Identity, bias=bq[:, c:c + 1],
                                                scale=float(HD) ** -0.25)
                        elif i == 1:
                            last = a.activation(state[:, i, c, :], src, ACT.Copy, scale=float(HD) ** -0.25)
                        else:
                            last = a.activation(state[:, i, c, :], src, ACT.Identity, bias=bv[:, c:c + 1])
                    last.then_inc(st_ready, 1)
                for it in range(ITERS):
                    base = 4 + MMS * it
                    act.wait_ge(cen_ready, it + 1)
                    a.activation(sq[:], cen[:], ACT.Square).then_inc(sq_ready, 1)
                    act.wait_ge(mm, base + 3)
                    a.activation(qsT[:], mx[0][:, 0:D].rearrange("p (c t) -> p c t", c=CH), ACT.Copy).then_inc(t_ready, 1)
                    if it < ITERS - 1:
                        act.wait_ge(kv_made, it + 1)
                        a.activation(state[:, 1:3, :, :], mx[1].rearrange("p (i c t) -> p i c t", i=2, c=CH),
                                     ACT.Copy).then_inc(st_ready, 1)
                    act.wait_ge(sc_ready, it + 1)
                    for h in range(H):
                        last = a.activation(sc[:, h, :], sc[:, h, :], ACT.Exp, bias=nmax[:, h:h + 1],
                                            accum_out=rsum[:, h:h + 1])
                        if h % HC == HC - 1:
                            last.then_inc(p_ready, 1)
                    act.wait_ge(mm, base + 6)
                    a.activation(pT[:, 0:HC, :], st[0].rearrange("p a (h t) -> p (a h) t", t=TOK),
                                 ACT.Copy).then_inc(p_out, 1)
                act.wait_ge(diff_ready, 1)
                a.activation(adiff[:], adiff[:], ACT.Abs, accum_out=asum[:]).then_inc(asum_ready, 1)

            @blk.tensor
            def _(pe):
                def transposes(bank, pieces):
                    for i, src in enumerate(pieces):
                        last = pe.transpose(bank[:, i * TOK:(i + 1) * TOK], src, ident[:])
                    return last

                pe.wait_ge(early, early_n)
                pe.wait_ge(xn_ready, 1)
                transposes(W, [xn[:, c * P:(c + 1) * P] for c in range(CH)]).then_inc(mm, 1)
                pe.wait_ge(read, 1)
                pe.wait_ge(loaded, loaded_n)
                for w, bank in ((wq, W), (wk, mx[0]), (wv, mx[1])):
                    for c in range(CH):
                        for kin in range(CH):
                            last = pe.matmul(bank[:, c * TOK:(c + 1) * TOK], w[:, kin, c * P:(c + 1) * P],
                                             xnT[:, kin, :], start=kin == 0, stop=kin == CH - 1)
                    last.then_inc(mm, 1)
                for it in range(ITERS):
                    pe.wait_ge(st_ready, 3 + 2 * it)
                    for n, bank, first in ((0, W, 0), (1, W, D), (2, av, 0)):
                        for c in range(CH):
                            last = pe.matmul(bank[:, first + c * P:first + (c + 1) * P], state[:, n, c, :], wl[n][:],
                                             start=True, stop=True)
                        if n:
                            last.then_inc(mm, 1)
                    pe.wait_ge(qk_ready, it + 1)
                    cenr = cen[:].rearrange("p (n c h) d -> p n c (h d)", n=2, c=CH)
                    transposes(mx[0], [cenr[:, 0, c, :] for c in range(CH)])
                    pe.wait_ge(rows_ready, it + 1)
                    transposes(av, [cenr[:, 1, c, :] for c in range(CH)]).then_inc(mm, 1)
                    if it < ITERS - 1:
                        rowsr = rows[:].rearrange("p n (c h) d -> p n c (h d)", c=CH)
                        transposes(mx[1], [rowsr[:, n, c, :] for n in (1, 2) for c in range(CH)]).then_inc(kv_made, 1)
                    pe.wait_ge(t_ready, (1 + CH) * (it + 1))
                    for c in range(CH):
                        for half in range(2):
                            last = pe.matmul(st[c][:, half, :], qsT[:, c, :],
                                             ksM[:, c, half * GH:(half + 1) * GH, :].rearrange("p h t -> p (h t)"),
                                             start=True, stop=True)
                        last.then_inc(mm, 1)
                    for c in range(CH):
                        pe.wait_ge(p_ready, CH * it + c + 1)
                        for h in range(HC):
                            last = pe.transpose(st[c][:, h // GH, h % GH * TOK:(h % GH + 1) * TOK],
                                                sc[:, c * HC + h, :], ident[:])
                        last.then_inc(mm, 1)
                    pe.wait_ge(p_out, 2 * it + 2)
                    for h in range(H):
                        last = pe.matmul(av[:, h * HD:(h + 1) * HD], pT[:, h, :], rows[:, 2, h, :], start=True, stop=True)
                    last.then_inc(mm, 1)
                    if it < ITERS - 1:
                        pe.wait_ge(o_ready, it + 1)
                        transposes(W, [outs[:, it, c * P:(c + 1) * P] for c in range(CH)]).then_inc(oT_made, 1)
                pe.wait_ge(asum_ready, 1)
                pe.matmul(W[:, 0:1], ones[:], asum[:], start=True, stop=True).then_inc(mm, 1)
                pe.wait_ge(sel_ready, 1)
                transposes(mx[0], [xn[:, c * P:(c + 1) * P] for c in range(CH)]).then_inc(mm, 1)
                pe.wait_ge(read, 2)
                for kin in range(CH):
                    last = pe.matmul(av[:, 0:D], xnT[:, kin, :], wo[:, kin, :], start=kin == 0, stop=kin == CH - 1)
                last.then_inc(mm, 1)

            @blk.vector
            def _(dve):
                v = nc.vector
                n = [0]

                def link(ins):
                    n[0] += 1
                    ins.then_inc(own, 1)
                    dve.wait_ge(own, n[0])

                dve.wait_ge(early, early_n)
                link(v.bn_stats(stats[:], x[:]))
                link(v.bn_aggr(meanvar[:], stats[:]))
                v.tensor_scalar(meanvar[:, 1:2], meanvar[:, 1:2], EPS, None, ALU.add).then_inc(var_ready, 1)
                dve.wait_ge(root_ready, 1)
                link(v.tensor_scalar(xn[:], x[:], meanvar[:, 0:1], meanvar[:, 1:2], ALU.subtract, ALU.mult))
                v.tensor_tensor(xn[:], xn[:], lna[:], ALU.mult).then_inc(xn_ready, 1)
                v.tensor_copy(g.ident_b[:], ident[:])
                dve.wait_ge(loaded, loaded_n)
                for i in range(1, ITERS):
                    link(v.tensor_scalar(tt[:, i:i + 1], tt[:, i:i + 1], 0.005 * i, None, ALU.add))
                v.tensor_scalar(tpow[:], tt[:], 1e-37, None, ALU.max).then_inc(var_ready, 1)
                link(v.tensor_scalar(tone[:], tt[:], 1.0, None, ALU.not_equal))
                link(v.tensor_scalar(tpos[:], tt[:], 0.0, None, ALU.is_gt))
                link(v.tensor_tensor(tone[:], tone[:], tpos[:], ALU.mult))
                v.tensor_scalar(bq[:], bq[:], float(HD) ** -0.25, None, ALU.mult).then_inc(bias_ready, 1)
                dve.wait_ge(root_ready, 2)
                link(v.tensor_scalar(tpow[:], tpow[:], 1.0, None, ALU.subtract))
                link(v.tensor_tensor(tpow[:], tpow[:], tone[:], ALU.mult))
                link(v.tensor_scalar(tpow[:], tpow[:], 1.0, None, ALU.add))
                for it in range(ITERS):
                    v.tensor_scalar(ln_w[:, it, 0, :], lncd[:, 0, :], tpow[:, it:it + 1], float(HD) ** -0.5,
                                    ALU.mult, ALU.mult)
                    link(v.tensor_copy(ln_w[:, it, 1, :], lncd[:, 1, :]))
                dve.wait_ge(zeroed, 6)
                v.tensor_scalar(mb[:, 0:S2], m8[:], 0.0, NEG, ALU.is_equal, ALU.mult).then_inc(mask_ready, 1)
                for it in range(ITERS):
                    base = 4 + MMS * it
                    heads = W[:].rearrange("p (n h d) -> p n h d", n=2, d=HD)
                    dve.wait_ge(mm, base + 1)
                    link(v.tensor_tensor(rows[:, 0:2, :, :], heads,
                                         bl[:, 0:2, :].unsqueeze(2).broadcast_to([TOK, 2, H, HD]), ALU.add))
                    dve.wait_ge(mm, base + 2)
                    v.tensor_tensor(rows[:, 2, :, :], av[:, 0:D].rearrange("p (h d) -> p h d", d=HD),
                                    bl[:, 2, :].unsqueeze(1).broadcast_to([TOK, H, HD]), ALU.add).then_inc(rows_ready, 1)
                    qk = rows[:, 0:2, :, :].rearrange("p n h d -> p (n h) d")
                    link(v.tensor_reduce(msum[:], qk, AX.X, ALU.add))
                    link(v.tensor_scalar(msum[:], msum[:], 1.0 / HD, None, ALU.mult))
                    v.tensor_tensor(cen[:], qk, msum[:].unsqueeze(2).broadcast_to([TOK, 2 * H, HD]),
                                    ALU.subtract).then_inc(cen_ready, 1)
                    dve.wait_ge(sq_ready, it + 1)
                    link(v.tensor_reduce(var[:], sq[:], AX.X, ALU.add))
                    v.tensor_scalar(var[:], var[:], 1.0 / HD, EPS, ALU.mult, ALU.add).then_inc(var_ready, 1)
                    link(v.tensor_tensor(cen[:].rearrange("p (n h) d -> p n h d", n=2),
                                         cen[:].rearrange("p (n h) d -> p n h d", n=2),
                                         ln_w[:, it, :, :].unsqueeze(2).broadcast_to([TOK, 2, H, HD]), ALU.mult))
                    dve.wait_ge(root_ready, 3 + it)
                    v.tensor_tensor(cen[:], cen[:], var[:].unsqueeze(2).broadcast_to([TOK, 2 * H, HD]),
                                    ALU.mult).then_inc(qk_ready, 1)
                    dve.wait_ge(mm, base + 3)
                    for c in range(CH):
                        v.tensor_tensor(ksM[:, c, :, :],
                                        av[:, c * TOK:(c + 1) * TOK].unsqueeze(1).broadcast_to([P, HC, TOK]),
                                        head[:].unsqueeze(2).broadcast_to([P, HC, TOK]), ALU.mult).then_inc(t_ready, 1)
                    for c in range(CH):
                        dve.wait_ge(mm, base + 4 + c)
                        link(v.tensor_tensor(sc[:, c * HC:(c + 1) * HC, :], st[c].rearrange("p a (h t) -> p (a h) t", t=TOK),
                                             hide[:].unsqueeze(1).broadcast_to([TOK, HC, TOK]), ALU.add))
                    v.tensor_reduce(nmax[:], sc[:], AX.X, ALU.max, negate=True).then_inc(sc_ready, 1)
                    dve.wait_ge(p_ready, CH * (it + 1))
                    link(v.reciprocal(rsum[:], rsum[:]))
                    dve.wait_ge(mm, base + 7)
                    v.tensor_copy(pT[:, HC:H, :], st[1].rearrange("p a (h t) -> p (a h) t", t=TOK)).then_inc(p_out, 1)
                    dve.wait_ge(mm, base + 8)
                    v.tensor_tensor(outs[:, it, :].rearrange("p (h d) -> p h d", d=HD),
                                    av[:, 0:D].rearrange("p (h d) -> p h d", d=HD),
                                    rsum[:].unsqueeze(2).broadcast_to([TOK, H, HD]), ALU.mult).then_inc(o_ready, 1)
                    if it < ITERS - 1:
                        dve.wait_ge(oT_made, it + 1)
                        v.tensor_tensor(state[:, 0, :, :], state[:, 0, :, :],
                                        W[:, 0:D].rearrange("p (c t) -> p c t", c=CH), ALU.add).then_inc(st_ready, 1)
                dve.wait_ge(o_ready, ITERS)
                v.tensor_tensor(adiff[:], outs[:, 1, :], outs[:, 0, :], ALU.subtract).then_inc(diff_ready, 1)
                end = 4 + MMS * ITERS
                dve.wait_ge(mm, end + 1)
                link(v.tensor_scalar(diff[:], W[:, 0:1], 1.0 / (B * T * D), None, ALU.mult))
                link(v.tensor_scalar(lim[:], diff[:], tf[:, 1:2], tf[:, 0:1], ALU.mult, ALU.add))
                link(v.tensor_tensor(keep[:], diff[:], lim[:], ALU.is_lt))
                link(v.tensor_scalar(other[:], keep[:], -1.0, 1.0, ALU.mult, ALU.add))
                link(v.tensor_scalar(outs[:, 1, :], outs[:, 1, :], keep[:], None, ALU.mult))
                v.scalar_tensor_tensor(xn[:], outs[:, 2, :], other[:], outs[:, 1, :], ALU.mult,
                                       ALU.add).then_inc(sel_ready, 1)
                dve.wait_ge(mm, end + 2)
                v.tensor_copy(xnT[:], mx[0][:, 0:D].rearrange("p (c t) -> p c t", c=CH)).then_inc(read, 1)
                dve.wait_ge(mm, end + 3)
                v.tensor_copy(proj[:], av[:, 0:D]).then_inc(read, 1)


XKT = -(-S2 // P)
SP_ = XKT * P
PIECES = ((0, 401), (401, 400), (801, 400), (1201, 400))
MXG = GH * QT * len(PIECES)
MXS = 5
XSLOTS = CH * NG * XKT
KBUF = 4
LEAD = 4
NE, EH, ER = 8, 64, 64
NDEC = NE * CH


def cross_attention_and_ffn(nc, g):
    sem, W, ident, ident_b, scores, mx, av = g.sem, g.W, g.ident, g.ident_b, g.scores, g.max_scores, g.av
    Wb = W[:].bitcast(BF16)
    with ExitStack() as s:
        def sb(name, shape, dt=F32):
            return sbuf(nc, s, name, shape, dt)

        xqT, xkT, xvT, xoT, wbase = (sb(n, [P, CH, D]) for n in ("xqT", "xkT", "xvT", "xoT", "wbase"))
        wenc = sb("wenc", [P, CH, NE, EH])
        wdec = sb("wdec", [P, NE, D])
        bo = sb("bo_rows", [P, D])
        benc = sb("benc_cols", [P, NE * EH // P])
        bdec = sb("bdec_cols", [P, NE, CH])
        cidx = sb("cidx", [P, NE], I32)
        cidxf = sb("cidx_f", [P, NE])
        iota = sb("iota", [P, NE])
        iotam = sb("iota_minus", [P, NE])
        ones = sb("ones", [P, P])
        wdown = sb("wdown", [P, CH, ER])
        bdown = sb("bdown_col", [ER, 1])
        wup = sb("wup", [ER + 2, D])
        midT = sb("midT", [ER + 2, T])
        ctxT = sb("ctxT_sb", [P, CH, S2])
        kst = sb("xk_stacks", [P, 2, HC, SP_], BF16)
        qst = sb("xq_stacks", [P, 2, HC, T], BF16)
        vals = sb("xv_rows", [P, 2, XKT, HC, HD + 1])
        probs = sb("xprobs", [P, 2, GH, T])
        oS = sb("xo_unnormed", [P, T])
        rz = sb("xrsum", [P, QT, GH])
        nmp = sb("xneg_max_pieces", [P, GH * QT, len(PIECES)])
        nm = sb("xneg_max", [P, GH * QT])
        comb = sb("xneg_max_parts", [P, 2, GH * QT], BF16)
        mrow = sb("xneg_max_rows", [2 * GH * QT, P], BF16)
        kpart = sb("xk_parts", [P, KBUF, PARTS, PIECES[0][1]], BF16)
        krest = sb("xk_rest", [P, KBUF, PIECES[0][1]])
        qpart = sb("xq_parts", [P, PARTS, T], BF16)
        qrest = sb("xq_rest", [P, T])
        xa = sb("xa", [P, QT, D])
        at = sb("attn_rows", [HD, D])
        xT = sb("xT", [P, CH, T])
        ox = sb("ox", [P, QT, D])
        x2 = sb("x2", [P, QT, D])
        x2T = sb("x2T", [P, CH, T])
        hT = sb("hT", [P, NE * EH // P, T])
        err = sb("err", [P, 2, T])
        loss = sb("loss", [P, NDEC])
        l8 = sb("l8", [P, NE])
        pick = sb("pick", [P, NE])
        sc = sb("sc", [P, 4])
        adp = sb("adp", [1, 1], I32)
        stats = sb("xstats", [P, QT, 6])
        meanvar = sb("xmeanvar", [P, QT, 2])
        rstd = sb("xrstd", [P, QT])

        loaded = sem("x_weights_in")
        zeroed = sem("x_zeroed")
        made = sem("x_made")
        exped = sem("x_exped")
        summed = sem("x_summed")
        evac = sem("x_values_out")
        mxd = sem("x_max_made")
        mxr = sem("x_max_read")
        comb_ready = sem("x_max_parts")
        mrow_out = sem("x_max_rows_out")
        max_in = sem("x_max_in")
        w_full = sem("x_work_full")
        w_free = sem("x_work_free")
        khigh = sem("x_k_high")
        kmid = sem("x_k_mid")
        klow = sem("x_k_low")
        kparts_out = [sem(f"x_k_parts_out{i}") for i in range(KBUF)]
        qhigh = sem("x_q_high")
        qmid = sem("x_q_mid")
        qlow = sem("x_q_low")
        qparts_out = sem("x_q_parts_out")
        stacked = sem("x_stacked")
        c_in = sem("x_ctx_in")
        x_in = sem("x_x_in")
        sum_ready = sem("x_summed_x")
        mv_ready = sem("x_meanvar")
        rstd_ready = sem("x_rstd")
        normed = sem("x_normed")
        x1_out = sem("x_x1_out")
        x1_in = sem("x_x1_in")
        sq_done = sem("x_err_squared")
        adp_ready = sem("x_adapter")
        adp_in = sem("x_adapter_in")
        out_done = sem("x_out")
        own = {e: sem(f"x_own_{e}") for e in ("dve", "pool")}
        arrived = sem("x_arrived")
        go = sem("x_go")
        cleared_early = [mrow_out, max_in, khigh, kmid, klow, *kparts_out, qhigh, qmid, qlow, qparts_out, stacked, c_in,
                         x_in, sum_ready, mv_ready, rstd_ready, normed, x1_out, x1_in, sq_done, adp_ready, adp_in]
        cleared = [made, exped, summed, evac, mxd, mxr, comb_ready, w_full, w_free, *own.values(), arrived]

        NP = len(PIECES)
        keys = [("kproj", i) for i in range(NP)]
        SLOT_WORK = {
            (0, 0): {0: [("v", 0)], 1: [("otr", 3), ("v", 1)], 2: [("v", 2)], 3: [("v", 3)], 4: [("oT", 0)],
                     5: [("oT", 1)], 6: [("xo", 0)], 7: [("xo", 1)], 8: [("x1T", 0)], 9: [("max", 1)],
                     10: [("x1T", 1)], 11: [keys[0]], 12: [keys[1]]},
            (0, 1): {0: [("x2T", 0)], 1: [("otr", 0), ("x2T", 1)], **{2 + i: [("enc", i)] for i in range(4)},
                     6: [keys[2]], 7: [keys[3]], 8: [("qproj", 0)], 9: [("max", 2), ("dec", 0)],
                     **{10 + i: [("dec", 1 + i)] for i in range(3)}},
            (1, 0): {0: [("v", 4)], 1: [("otr", 1), ("v", 5)], 2: [("v", 6)], 3: [("v", 7)],
                     **{4 + i: [("dec", 4 + i)] for i in range(5)}, 9: [("max", 3), ("dec", 9)],
                     **{10 + i: [("dec", 10 + i)] for i in range(3)}},
            (1, 1): {0: [("dec", 13)], 1: [("otr", 2), ("dec", 14)], 2: [("dec", 15)], 3: [("kproj", NP), ("loss",)],
                     4: [("kproj", NP + 1)], 5: [("kproj", NP + 2)], 6: [("kproj", NP + 3)], 7: [("mid",), ("y", 0)],
                     8: [("y", 1)], 9: [("max", 4), ("qproj", 1)]},
        }
        VECTOR_WORK = {
            (0, 0): {2: [("stats", "x1", 0)], 3: [("stats", "x1", 1)], 4: [("aggr", "x1")], 5: [("apply", "x1", 0)],
                     6: [("apply", "x1", 1)], 7: [("stats", "x2", 0)], 8: [("stats", "x2", 1)], 9: [("aggr", "x2")],
                     10: [("apply", "x2", 0)], 11: [("apply", "x2", 1)]},
            (0, 1): {}, (1, 0): {},
            (1, 1): {4: [("choose", 0)], 5: [("choose", 1), ("choose", 2)], 8: [("stats", "y", 0)],
                     9: [("stats", "y", 1)], 10: [("aggr", "y")], 11: [("apply", "y", 0), ("apply", "y", 1)]},
        }
        TAIL = ("oT", "xo", "x2T", "enc", "dec", "loss", "mid", "y")

        def of_tail(job):
            return job[0] in TAIL or job == ("otr", 3)

        def work_at(tail, k, gr, t):
            w = SLOT_WORK[k, gr].get(t, [])
            return [j for j in w if tail or not of_tail(j)]

        def vector_work_at(tail, k, gr, t):
            w = VECTOR_WORK[k, gr].get(t, [])
            return [j for j in w if tail or j[1] == "x1"]

        def body_order(tail):
            return [j for k in range(CH) for gr in range(NG) for t in range(XKT) for j in work_at(tail, k, gr, t)]

        FIRST = Phase(False, keys + [("x1T", 0), ("x1T", 1), ("qproj", 0)] + [("v", i) for i in range(4, 8)]
                      + [("kproj", NP + i) for i in range(NP)] + [("qproj", 1), ("max", 0)])
        BODY0 = Phase(False, body_order(False))
        BODY = Phase(True, body_order(True))
        LAST = Phase(True, [j for kg in SLOT_WORK.values() for t in sorted(kg) for j in kg[t] if of_tail(j)])

        def pe_begin(ph, job):
            if ph.order.before(job):
                nc.tensor.wait_ge(w_free, ph.order.before(job))

        def transposes(src, c):
            for q in range(QT):
                last = nc.tensor.transpose(W[:, q * P:(q + 1) * P], src[:, q, c * P:(c + 1) * P], ident[:])
            return last

        def rows_of(lhs, rhs, half, extra=None):
            for i in range(2):
                q = 2 * half + i
                for c in range(CH):
                    last = nc.tensor.matmul(W[:, i * D:(i + 1) * D], lhs[:, c, q * P:(q + 1) * P], rhs[:, c, :],
                                            start=c == 0, stop=c == CH - 1 and extra is None)
                if extra:
                    last = nc.tensor.matmul(W[:, i * D:(i + 1) * D], extra[0][:, q * P:(q + 1) * P], extra[1][:],
                                            start=False, stop=True)
            return last

        def pe_job(ph, job):
            pe = nc.tensor
            name, i = job[0], job[1] if len(job) > 1 else 0
            pe_begin(ph, job)
            if name == "x1T":
                pe.wait_ge(normed, normed_of(ph, "x1"))
                last = transposes(xa, i)
            elif name == "oT":
                last = transposes(ox, i)
            elif name == "x2T":
                pe.wait_ge(normed, normed_of(ph, "x2"))
                last = transposes(x2, i)
            elif name == "xo":
                pe.wait_ge(w_free, ph.order.after(("oT", 1)))
                last = rows_of(x2T, xoT, i)
            elif name == "y":
                pe.wait_ge(w_free, ph.order.after(("mid",)))
                last = rows_of(x2T, wbase, i, (midT, wup))
            elif name == "kproj":
                c, piece = divmod(i, NP)
                k0, n = PIECES[piece]
                pe.wait_ge(c_in, 16)
                for kin in range(CH):
                    last = pe.matmul(W[:, 0:n], xkT[:, kin, c * P:(c + 1) * P], ctxT[:, kin, k0:k0 + n],
                                     start=kin == 0, stop=kin == CH - 1)
            elif name == "qproj":
                pe.wait_ge(w_free, ph.order.after(("x1T", 1)))
                for kin in range(CH):
                    last = pe.matmul(W[:], xqT[:, kin, i * P:(i + 1) * P], xT[:, kin, :],
                                     start=kin == 0, stop=kin == CH - 1)
            elif name == "v":
                c = (i // 4 + 1) % CH
                for tt in range(4 * (i % 4), min(4 * (i % 4) + 4, XKT)):
                    rows = min(P, S2 - tt * P)
                    for kin in range(CH):
                        last = pe.matmul(W[0:rows, (tt % 4) * P:(tt % 4 + 1) * P], ctxT[:, kin, tt * P:tt * P + rows],
                                         xvT[:, kin, c * P:(c + 1) * P], start=kin == 0, stop=kin == CH - 1)
            elif name == "enc":
                pe.wait_ge(w_free, ph.order.after(("x2T", 1)))
                for kin in range(CH):
                    last = pe.matmul(W[:], wenc[:, kin, 2 * i:2 * i + 2, :].rearrange("p n h -> p (n h)"),
                                     x2T[:, kin, :], start=kin == 0, stop=kin == CH - 1)
            elif name == "dec":
                n, c = divmod(i, CH)
                pe.wait_ge(w_free, ph.order.after(("enc", n // 2)))
                last = pe.matmul(W[:], wdec[:, n, c * P:(c + 1) * P], hT[:, n // 2, :], start=True, stop=True)
            elif name == "loss":
                pe.wait_ge(sq_done, NDEC)
                last = pe.matmul(W[:, 0:NDEC], ones[:], loss[:], start=True, stop=True)
            elif name == "mid":
                pe.wait_ge(adp_in, 64)
                for kin in range(CH):
                    last = pe.matmul(W[0:ER, :], wdown[:, kin, :], x2T[:, kin, :], start=kin == 0, stop=kin == CH - 1)
            elif name == "max":
                pe.wait_ge(comb_ready, i if ph is not FIRST else 1)
                last = pe.transpose(Wb[0:2 * GH * QT, 0:P], comb[:].rearrange("p a b -> p (a b)"), ident_b[:])
            elif name == "otr":
                pe.wait_ge(evac, 1 if i == CH * NG - 1 else i + 1 + ph.tail)
                last = transposes(oS[:].rearrange("p (q n) -> p q n", q=QT), 0)
            last.then_inc(w_full, 1)

        def normed_of(ph, what):
            order = [n for n in ("x1", "x2", "y") if n == "x1" and ph is not LAST or n != "x1" and ph.tail]
            return order.index(what) + 1

        def max_event(e):
            m, x = divmod(e + LEAD * MXS, XKT * MXS)
            return (m + 1, x) if x < MXG else None

        MAXES = [max_event(e) for e in range(XSLOTS * MXS)]
        COUNT = [0]
        for one in MAXES:
            COUNT.append(COUNT[-1] + (one is not None))

        def pe_max_piece(m, x, n):
            pe = nc.tensor
            jq, piece = divmod(x, NP)
            j, q = divmod(jq, QT)
            k, gr = divmod(m, NG)
            k0, w = PIECES[piece]
            h = gr * GH + j
            if n >= MRING:
                pe.wait_ge(mxr, n - MRING + 1)
            pe.matmul(mx[n % MRING][:, 0:w], qst[0:R_MAX, k % 2, h, q * P:(q + 1) * P], kst[0:R_MAX, k % 2, h, k0:k0 + w],
                      start=True, stop=True).then_inc(mxd, 1)

        STACK_DMAS = 2 * len(QPART) + 1

        def pe_max(e):
            one = MAXES[e]
            if one:
                if one == (2, 0):
                    nc.tensor.wait_ge(stacked, 16 * STACK_DMAS)
                if one == (4, 0):
                    nc.tensor.wait_ge(stacked, 32 * STACK_DMAS)
                pe_max_piece(*one, COUNT[e])

        def pe_scores(k, gr, t, j):
            pe = nc.tensor
            m = NG * k + gr
            n = GH * (XKT * m + t) + j
            if t == 0 and m and j == 0:
                pe.wait_ge(max_in, 16 * m)
            if n >= SRING:
                pe.wait_ge(exped, n - SRING + 1)
            h = gr * GH + j
            pe.matmul(scores[n % SRING], kst[0:ROWS, k, h, t * P:(t + 1) * P], qst[0:ROWS, k, h, :],
                      start=True, stop=True).then_inc(made, 1)

        def pe_values(ph, sl):
            pe = nc.tensor
            m, t = divmod(sl, XKT)
            k, gr = divmod(m % (CH * NG), NG)
            if sl >= 0:
                pe.wait_ge(exped, GH * (sl + 1))
            if t == 0 and m + ph.tail:
                pe.wait_ge(evac, m + ph.tail)
            if t == 0 and m == NG:
                pe.wait_ge(w_free, ph.order.after(("v", 3)))
            for j in range(GH):
                last = pe.matmul(av[32 * j:32 * j + HD + 1, :], vals[:, k, t, gr * GH + j, :], probs[:, sl % 2, j, :],
                                 start=t == 0, stop=t == XKT - 1)
            last.then_inc(summed, 1)

        def pe_body(ph):
            for k in range(CH):
                for gr in range(NG):
                    for t in range(XKT):
                        sl = XKT * (NG * k + gr) + t
                        jobs = work_at(ph.tail, k, gr, t)
                        for j in range(GH):
                            pe_scores(k, gr, t, j)
                            pe_max(MXS * sl + j)
                        if jobs:
                            pe_job(ph, jobs[0])
                        if sl or ph.tail:
                            pe_values(ph, sl - 1)
                        pe_max(MXS * sl + GH)
                        for j in jobs[1:]:
                            pe_job(ph, j)

        def act_job(ph, job):
            act = nc.scalar
            name, i = job[0], job[1] if len(job) > 1 else 0
            if name not in ("oT", "x1T", "x2T", "kproj", "qproj", "enc", "mid"):
                return
            act.wait_ge(w_full, ph.order.after(job))
            if name == "x1T":
                act.activation(xT[:, i, :], W[:], ACT.Copy).then_inc(w_free, 1)
            elif name in ("oT", "x2T"):
                act.activation(x2T[:, i, :], W[:], ACT.Copy).then_inc(w_free, 1)
            elif name == "enc":
                act.activation(hT[:, i, :], W[:], ACT.Relu, bias=benc[:, i:i + 1]).then_inc(w_free, 1)
            elif name == "mid":
                act.activation(midT[0:ER, :], W[0:ER, :], ACT.Relu, bias=bdown[:]).then_inc(w_free, 1)
            elif name == "kproj":
                n = PIECES[i % NP][1]
                if i >= KBUF:
                    act.wait_ge(kparts_out[i % KBUF], 48 * (i // KBUF))
                act.activation(kpart[:, i % KBUF, 0, 0:n], W[:, 0:n], ACT.Copy).then_inc(khigh, 1)
            elif name == "qproj":
                if i:
                    act.wait_ge(qparts_out, 48)
                act.activation(qpart[:, 0, :], W[:], ACT.Copy, scale=float(HD) ** -0.5).then_inc(qhigh, 1)

        def act_later(ph, job):
            act = nc.scalar
            name, i = job[0], job[1] if len(job) > 1 else 0
            if name == "kproj":
                n = PIECES[i % NP][1]
                act.wait_ge(w_free, ph.order.after(job))
                act.activation(kpart[:, i % KBUF, 1, 0:n], krest[:, i % KBUF, 0:n], ACT.Copy).then_inc(kmid, 1)
            elif name == "qproj":
                act.wait_ge(w_free, ph.order.after(job))
                act.activation(qpart[:, 1, :], qrest[:], ACT.Copy).then_inc(qmid, 1)
            elif name == "dec":
                act.wait_ge(w_free, ph.order.after(job))
                act.activation(err[:, i % 2, :], err[:, i % 2, :], ACT.Square,
                               accum_out=loss[:, i:i + 1]).then_inc(sq_done, 1)

        def act_max_out(ph, m, n):
            nc.scalar.wait_ge(w_free, ph.order.after(("max", m)))
            nc.scalar.dma_start(g.max_dram, mrow[:]).then_inc(mrow_out, 16)

        def act_max_in(m, n):
            k, gr = divmod(m, NG)
            nc.scalar.wait_ge(mrow_out, 16 * n)
            nc.scalar.dma_start(qst[R_MAX:ROWS, k % CH, gr * GH:(gr + 1) * GH, :],
                                g.max_dram.rearrange("(r j q) n -> r j (q n)", r=2, j=GH)).then_inc(max_in, 16)

        def act_values_out(ph, m):
            if m < 0 and not ph.tail:
                return
            nc.scalar.wait_ge(summed, XKT * (m + 1) + ph.tail)
            if m >= 1 or m == 0 and ph.tail:
                nc.scalar.wait_ge(w_full, ph.order.after(("otr", (m - 1) % (CH * NG))))
            nc.scalar.activation(oS[:], av[:], ACT.Copy).then_inc(evac, 1)

        def act_body(ph):
            for k in range(CH):
                for gr in range(NG):
                    for t in range(XKT):
                        m = NG * k + gr
                        sl = XKT * m + t
                        if sl - 1 + ph.tail > 0:
                            nc.scalar.wait_ge(summed, sl - 1 + ph.tail)
                        for j in range(GH):
                            n = GH * sl + j
                            nc.scalar.wait_ge(made, n + 1)
                            nc.scalar.activation(probs[:, sl % 2, j, :], scores[n % SRING], ACT.Exp).then_inc(exped, 1)
                        if t == 0:
                            act_values_out(ph, m - 1)
                        for j in previous_jobs(ph, k, gr, t):
                            act_later(ph, j)
                        for j in work_at(ph.tail, k, gr, t):
                            act_job(ph, j)
                        if t == XKT - LEAD:
                            act_max_out(ph, m + 1, m + 1)
                        if t == XKT - LEAD + 1:
                            act_max_in(m + 1, m + 1)

        def previous_jobs(ph, k, gr, t):
            sl = XKT * (NG * k + gr) + t - 1
            if sl < 0:
                return []
            m, t = divmod(sl, XKT)
            return work_at(ph.tail, *divmod(m, NG), t)

        links = {"dve": 0, "mv": 0}

        def dve_link(ins):
            links["dve"] += 1
            ins.then_inc(own["dve"], 1)
            nc.vector.wait_ge(own["dve"], links["dve"])

        def dve_step(step):
            v = nc.vector
            name, what = step[0], step[1]
            x = xa if what == "x1" else x2
            if name == "stats":
                if what == "x1" and step[2] == 0:
                    v.wait_ge(sum_ready, 1)
                for q in range(2 * step[2], 2 * step[2] + 2):
                    last = v.bn_stats(stats[:, q, :], x[:, q, :])
                dve_link(last)
            elif name == "aggr":
                for q in range(QT):
                    last = v.bn_aggr(meanvar[:, q, :], stats[:, q, :])
                dve_link(last)
                links["mv"] += 1
                v.tensor_scalar(rstd[:], meanvar[:, :, 1], EPS, None, ALU.add).then_inc(mv_ready, 1)
            elif name == "apply":
                v.wait_ge(rstd_ready, links["mv"])
                for q in range(2 * step[2], 2 * step[2] + 2):
                    last = v.tensor_scalar(x[:, q, :], x[:, q, :], meanvar[:, q, 0:1], rstd[:, q:q + 1],
                                           ALU.subtract, ALU.mult)
                if step[2]:
                    last.then_inc(normed, 1)
            else:
                dve_choose(step[1])

        def dve_norm(what):
            for step in (("stats", what, 0), ("stats", what, 1), ("aggr", what), ("apply", what, 0), ("apply", what, 1)):
                dve_step(step)

        def dve_choose(part):
            v = nc.vector
            if part == 0:
                dve_link(v.tensor_reduce(sc[:, 0:1], l8[:], AX.X, ALU.min))
                dve_link(v.tensor_scalar(pick[:], l8[:], sc[:, 0:1], None, ALU.is_le))
                dve_link(v.tensor_tensor(pick[:], pick[:], iotam[:], ALU.mult))
            elif part == 1:
                dve_link(v.tensor_reduce(sc[:, 1:2], pick[:], AX.X, ALU.min))
                dve_link(v.tensor_scalar(pick[:], iotam[:], sc[:, 1:2], None, ALU.is_equal))
                dve_link(v.tensor_tensor(pick[:], pick[:], cidxf[:], ALU.mult))
                dve_link(v.tensor_reduce(sc[:, 2:3], pick[:], AX.X, ALU.add))
            else:
                dve_link(v.tensor_scalar(sc[:, 3:4], sc[:, 2:3], 0.0, float(NE), ALU.is_lt, ALU.mult))
                dve_link(v.tensor_tensor(sc[:, 2:3], sc[:, 2:3], sc[:, 3:4], ALU.add))
                dve_link(v.tensor_scalar(sc[:, 2:3], sc[:, 2:3], 0.0, float(NE - 1), ALU.max, ALU.min))
                v.tensor_copy(adp[:], sc[0:1, 2:3]).then_inc(adp_ready, 1)

        def dve_job(ph, job):
            v = nc.vector
            name, i = job[0], job[1] if len(job) > 1 else 0
            if name not in ("kproj", "qproj", "xo", "y", "v", "dec", "loss", "max", "otr"):
                return
            v.wait_ge(w_full, ph.order.after(job))
            W2 = W[:].rearrange("p (q d) -> p q d", q=2)
            if name == "kproj":
                n = PIECES[i % NP][1]
                v.wait_ge(khigh, i + 1)
                if i >= KBUF:
                    v.wait_ge(klow, i - KBUF + 1)
                v.tensor_tensor(krest[:, i % KBUF, 0:n], W[:, 0:n], kpart[:, i % KBUF, 0, 0:n],
                                ALU.subtract).then_inc(w_free, 1)
            elif name == "qproj":
                v.wait_ge(qhigh, i + 1)
                if i:
                    v.wait_ge(qlow, 1)
                v.scalar_tensor_tensor(qrest[:], W[:], float(HD) ** -0.5, qpart[:, 0, :], ALU.mult,
                                       ALU.subtract).then_inc(w_free, 1)
            elif name in ("xo", "y"):
                if name == "xo" and i == 0:
                    v.wait_ge(x1_in, 16)
                v.tensor_tensor(x2[:, 2 * i:2 * i + 2, :], W2, x2[:, 2 * i:2 * i + 2, :], ALU.add).then_inc(w_free, 1)
                v.wait_ge(w_free, ph.order.after(job))
            elif name == "v":
                c = (i // 4 + 1) % CH
                tiles = range(4 * (i % 4), min(4 * (i % 4) + 4, XKT))
                full = [tt for tt in tiles if (tt + 1) * P <= S2]
                if full:
                    v.tensor_copy(vals[:, c, full[0]:full[-1] + 1, :, 0:HD],
                                  W[:, 0:len(full) * P].rearrange("p (t h d) -> p t h d", t=len(full), d=HD)
                                  ).then_inc(w_free, 1)
                else:
                    rows = S2 - tiles[0] * P
                    v.tensor_copy(vals[0:rows, c, tiles[0], :, 0:HD],
                                  W[0:rows, 0:P].rearrange("p (h d) -> p h d", d=HD)).then_inc(w_free, 1)
            elif name == "dec":
                n, c = divmod(i, CH)
                if i >= 2:
                    v.wait_ge(sq_done, i - 1)
                v.scalar_tensor_tensor(err[:, i % 2, :], W[:], bdec[:, n, c:c + 1], x2T[:, c, :], ALU.add,
                                       ALU.subtract).then_inc(w_free, 1)
            elif name == "loss":
                v.tensor_reduce(l8[:], W[:, 0:NDEC].rearrange("p (n c) -> p n c", c=CH), AX.X,
                                ALU.add).then_inc(w_free, 1)
                v.wait_ge(w_free, ph.order.after(job))
            elif name == "max":
                if ph is not FIRST and i >= 2:
                    v.wait_ge(mrow_out, 16 * (i - 1))
                v.tensor_copy(mrow[:], Wb[0:2 * GH * QT, 0:P]).then_inc(w_free, 1)
            elif name == "otr":
                w4 = W[:].rearrange("p (q j r) -> p q j r", q=QT, r=2 * HD)
                dve_link(v.reciprocal(rz[:], w4[:, :, :, HD]))
                v.tensor_tensor(ox[:, :, i * GH * HD:(i + 1) * GH * HD].rearrange("p q (j d) -> p q j d", d=HD),
                                w4[:, :, :, 0:HD], rz[:].unsqueeze(3).broadcast_to([P, QT, GH, HD]),
                                ALU.mult).then_inc(w_free, 1)

        def dve_max_piece(x, n):
            w = PIECES[x % NP][1]
            nc.vector.wait_ge(mxd, n + 1)
            nc.vector.tensor_reduce(nmp[:, x // NP, x % NP:x % NP + 1], mx[n % MRING][:, 0:w], AX.X, ALU.max,
                                    negate=True).then_inc(mxr, 1)

        def dve_max(e):
            if MAXES[e]:
                dve_max_piece(MAXES[e][1], COUNT[e])

        def dve_max_parts(ph, n_read, n):
            nc.vector.wait_ge(mxr, n_read)
            dve_link(nc.vector.tensor_reduce(nm[:], nmp[:], AX.X, ALU.min))
            if n >= 2:
                nc.vector.wait_ge(w_full, ph.order.after(("max", n - 1)))
            dve_link(nc.vector.tensor_copy(comb[:, 0, :], nm[:]))
            nc.vector.tensor_tensor(comb[:, 1, :], nm[:], comb[:, 0, :], ALU.subtract).then_inc(comb_ready, 1)

        def dve_body(ph):
            for k in range(CH):
                for gr in range(NG):
                    for t in range(XKT):
                        m = NG * k + gr
                        sl = XKT * m + t
                        jobs = work_at(ph.tail, k, gr, t)
                        if t == XKT - LEAD:
                            dve_max_parts(ph, COUNT[MXS * sl], m + 1)
                        for i in range(GH):
                            dve_max(MXS * sl + i)
                        for step in vector_work_at(ph.tail, k, gr, t):
                            dve_step(step)
                        if jobs:
                            dve_job(ph, jobs[0])
                        dve_max(MXS * sl + GH)
                        for j in jobs[1:]:
                            dve_job(ph, j)

        def pool_sum():
            p = nc.gpsimd
            p.wait_ge(x_in, 32)
            p.tensor_tensor(xa[:], xa[:], bo[:].unsqueeze(1).broadcast_to([P, QT, D]), ALU.add).then_inc(own["pool"], 1)
            p.wait_ge(own["pool"], 1)
            p.tensor_tensor(xa[0:HD, 0, :], xa[0:HD, 0, :], at[:], ALU.add).then_inc(sum_ready, 1)

        def pool_rstd(n):
            nc.gpsimd.wait_ge(mv_ready, n)
            nc.gpsimd.tensor_tensor(rstd[:], rstd[:], g.mhalf[:, 0:QT], ALU.pow).then_inc(rstd_ready, 1)

        def pool_klow(i):
            n = PIECES[i % NP][1]
            nc.gpsimd.wait_ge(kmid, i + 1)
            nc.gpsimd.tensor_tensor(kpart[:, i % KBUF, 2, 0:n], krest[:, i % KBUF, 0:n], kpart[:, i % KBUF, 1, 0:n],
                                    ALU.subtract).then_inc(klow, 1)

        def pool_qlow(i):
            nc.gpsimd.wait_ge(qmid, i + 1)
            nc.gpsimd.tensor_tensor(qpart[:, 2, :], qrest[:], qpart[:, 1, :], ALU.subtract).then_inc(qlow, 1)

        def pool_body(ph):
            pool_sum()
            pool_rstd(1)
            if ph.tail:
                pool_rstd(2)
            for i in range(NP):
                pool_klow(i)
            pool_qlow(0)
            for i in range(NP):
                pool_klow(NP + i)
            pool_qlow(1)
            if ph.tail:
                pool_rstd(3)

        def sp_load_x(b):
            nc.sync.dma_start(xa[:], g.x[bass.ds(b, 1)].rearrange("b (q p) d -> p (b q) d", p=P)).then_inc(x_in, 16)
            nc.sync.dma_start(at[:], g.attn_dram[bass.ds(b, 1)].rearrange("b t d -> (b t) d")).then_inc(x_in, 16)

        def sp_load_ctx(b):
            nc.sync.dma_start(ctxT[:], g.ctxT[bass.ds(b, 1)].rearrange("b (c p) n -> p (b c) n", p=P)).then_inc(c_in, 16)

        def sp_key_parts(i, read):
            k0, n = PIECES[i % NP]
            if i % NP == 0 and read:
                nc.sync.wait_ge(stacked, read)
            nc.sync.wait_ge(khigh, i + 1)
            nc.sync.wait_ge(kmid, i + 1)
            nc.sync.wait_ge(klow, i + 1)
            for part in range(PARTS):
                nc.sync.dma_start(g.kpart_dram[part, :, k0:k0 + n], kpart[:, i % KBUF, part, 0:n]).then_inc(kparts_out[i % KBUF], 16)

        def sp_key_parts_out(n):
            for one in kparts_out:
                nc.sync.wait_ge(one, 48 * (n * NP // KBUF))

        def sp_query_parts(i):
            nc.sync.wait_ge(qlow, i + 1)
            nc.sync.wait_ge(qmid, i + 1)
            for part in range(PARTS):
                nc.sync.dma_start(g.part_dram[part], qpart[:, part, :]).then_inc(qparts_out, 16)

        def sp_stacks(b, c):
            for j, (pq, pk) in enumerate(zip(QPART, KPART)):
                rows = slice(HD * j, HD * (j + 1))
                nc.sync.dma_start(kst[rows, c, :, 0:S2],
                                  g.kpart_dram[pk].rearrange("(h d) n -> d h n", d=HD)).then_inc(stacked, 16)
                nc.sync.dma_start(qst[rows, c, :, :],
                                  g.part_dram[pq].rearrange("(h d) n -> d h n", d=HD)).then_inc(stacked, 16)
            nc.sync.dma_start(kst[R_MASK:R_MASK + 1, c, :, :],
                              g.mask_dram[bass.ds(b, 1)].unsqueeze(1).broadcast_to([1, HC, SP_])).then_inc(stacked, 16)

        def sp_stored():
            nc.sync.wait_ge(out_done, 16)
            nc.sync.sem_clear(out_done)

        def sp_load_x1(b):
            nc.sync.dma_start(x2[:], g.x1_dram[bass.ds(b, 1)].rearrange("b (q p) d -> p (b q) d", p=P)).then_inc(x1_in, 16)

        def sp_store_x1(ph, b):
            nc.sync.wait_ge(normed, normed_of(ph, "x1"))
            nc.sync.dma_start(g.x1_dram[bass.ds(b, 1)].rearrange("b (q p) d -> p (b q) d", p=P), xa[:]).then_inc(x1_out, 16)

        def sp_adapter():
            sp = nc.sync
            sp.wait_ge(adp_ready, 1)
            n = sp.value_load(adp[0:1, 0:1], min_val=0, max_val=NE - 1)
            sp.dma_start(wdown[:], g.Wdown[bass.ds(n, 1)].rearrange("n (c p) r -> p (n c) r", p=P)).then_inc(adp_in, 16)
            sp.dma_start(wup[0:ER, :], g.Wup[bass.ds(n, 1)].rearrange("n r d -> (n r) d")).then_inc(adp_in, 16)
            sp.dma_start(wup[ER:ER + 1, :], g.bup[bass.ds(n, 1)]).then_inc(adp_in, 16)
            with nc.allow_non_contiguous_dma(reason="a bias column"):
                sp.dma_start(bdown[:], g.bdown[bass.ds(n, 1)].rearrange("n r -> r n")).then_inc(adp_in, 16)

        def sp_store_out(ph, b):
            nc.sync.wait_ge(normed, normed_of(ph, "y"))
            nc.sync.dma_start(g.out[bass.ds(b, 1)].rearrange("b (q p) d -> p (b q) d", p=P), x2[:]).then_inc(out_done, 16)

        def sp_body(ph, b, nxt):
            sp_load_x(nxt)
            if ph.tail:
                sp_stored()
                sp_load_x1(b - 1)
            sp_stacks(b, 1)
            nc.sync.wait_ge(w_full, ph.order.after(("v", 3)))
            sp_load_ctx(nxt)
            sp_store_x1(ph, nxt)
            for i in range(NP):
                sp_key_parts(i, 16 * STACK_DMAS)
            sp_query_parts(0)
            nc.sync.wait_ge(made, GH * NG * XKT)
            sp_key_parts_out(1)
            nc.sync.wait_ge(qparts_out, 48)
            sp_stacks(nxt, 0)
            for i in range(NP):
                sp_key_parts(NP + i, 32 * STACK_DMAS)
                if i == 1 and ph.tail:
                    sp_adapter()
            sp_query_parts(1)
            if ph.tail:
                sp_store_out(ph, b - 1)
            nc.sync.wait_ge(x1_out, 16)
            sp_key_parts_out(2)
            nc.sync.wait_ge(qparts_out, 96)
            nc.sync.wait_ge(stacked, 32 * STACK_DMAS)
            nc.sync.wait_ge(max_in, 16 * NG * CH)

        first_pieces = [(0, x) for x in range(MXG)] + [(1, x) for x in range(LEAD * MXS)]
        N_LOADS = 16 * (5 + 2 * NE + 6)
        with nc.Block() as blk:
            @blk.sync
            def _(sp):
                n = 0
                sp_load_x(0)
                sp_load_ctx(0)
                sp.wait_ge(zeroed, 3)
                with nc.allow_non_contiguous_dma(reason="bias columns and rows, once"):
                    for dst, src in ((xqT[:], g.xWqT), (xkT[:], g.xWkT), (xvT[:], g.xWvT),
                                     (xoT[:], g.xWoT), (wbase[:], g.Wbase)):
                        sp.dma_start(dst, src.rearrange("(c p) d -> p c d", p=P)).then_inc(loaded, 16)
                        n += 16
                    for e in range(NE):
                        sp.dma_start(wenc[:, :, e, :], g.Wenc[e].rearrange("(c p) h -> p c h", p=P)).then_inc(loaded, 16)
                        half = EH * (e % 2)
                        sp.dma_start(wdec[half:half + EH, e, :], g.Wdec[e]).then_inc(loaded, 16)
                        n += 32
                    for dst, src in ((bo[:], g.bo.unsqueeze(0).broadcast_to([P, D])),
                                     (benc[:], g.benc.rearrange("n h -> (n h)").rearrange("(j p) -> p j", p=P)),
                                     (bdec[:], g.bdec.rearrange("n (c p) -> p n c", p=P)),
                                     (cidx[:], g.cidx.unsqueeze(0).broadcast_to([P, NE])),
                                     (iota[:], g.c_iota.broadcast_to([P, NE])),
                                     (wup[ER + 1:ER + 2, :], g.bbase.unsqueeze(0))):
                        sp.dma_start(dst, src).then_inc(loaded, 16)
                        n += 16
                assert n == N_LOADS
                sp_store_x1(FIRST, 0)
                for i in range(NP):
                    sp_key_parts(i, 0)
                sp_query_parts(0)
                sp_key_parts_out(1)
                sp.wait_ge(qparts_out, 48)
                sp_stacks(0, 0)
                for i in range(NP):
                    sp_key_parts(NP + i, 16 * STACK_DMAS)
                sp_query_parts(1)
                sp.wait_ge(x1_out, 16)
                sp_key_parts_out(2)
                sp.wait_ge(qparts_out, 96)
                sp.wait_ge(max_in, 16)
                sp.wait_ge(loaded, N_LOADS)

            @blk.gpsimd
            def _(pool):
                p = nc.gpsimd
                p.memset(wdec[:], 0.0).then_inc(zeroed, 1)
                p.memset(ones[:], 1.0).then_inc(zeroed, 1)
                pool.wait_ge(zeroed, 2)
                p.memset(midT[ER:ER + 2, :], 1.0).then_inc(zeroed, 1)
                pool.wait_ge(zeroed, 3)
                p.memset(kst[64:128, :, :, :], 1.0).then_inc(zeroed, 1)
                pool.wait_ge(zeroed, 4)
                p.memset(qst[96:128, :, :, :], 1.0).then_inc(zeroed, 1)
                pool.wait_ge(zeroed, 5)
                p.memset(kst[0:96, :, :, S2:SP_], 0.0).then_inc(zeroed, 1)
                pool.wait_ge(zeroed, 6)
                p.memset(vals[:], 0.0).then_inc(zeroed, 1)
                pool.wait_ge(zeroed, 7)
                p.memset(vals[:, :, :, :, HD:HD + 1], 1.0).then_inc(zeroed, 1)
                pool.wait_ge(loaded, N_LOADS)
                pool.wait_ge(zeroed, 8)
                pool_sum()
                pool_rstd(1)
                for i in range(NP):
                    pool_klow(i)
                pool_qlow(0)
                for i in range(NP):
                    pool_klow(NP + i)
                pool_qlow(1)

            first_jobs = FIRST.order.names

            @blk.scalar
            def _(act):
                before = None
                for job in first_jobs[:-1]:
                    if before:
                        act_later(FIRST, before)
                    act_job(FIRST, job)
                    before = job
                act_later(FIRST, before)
                act_max_out(FIRST, 0, 1)
                act_max_in(0, 1)

            @blk.vector
            def _(dve):
                v = nc.vector
                dve.wait_ge(zeroed, 8)
                dve_link(v.memset(av[:], 0.0))
                dve.wait_ge(loaded, N_LOADS)
                dve_link(v.tensor_copy(cidxf[:], cidx[:]))
                dve_link(v.tensor_scalar(iotam[:], iota[:], float(NE), None, ALU.subtract))
                dve_norm("x1")
                for job in first_jobs[:-1]:
                    dve_job(FIRST, job)
                for n, (m, x) in enumerate(first_pieces):
                    if n == MXG:
                        dve_max_parts(FIRST, MXG, 1)
                        dve_job(FIRST, ("max", 0))
                    dve_max_piece(x, n)

            @blk.tensor
            def _(pe):
                pe.wait_ge(loaded, N_LOADS)
                pe.wait_ge(zeroed, 8)
                for job in first_jobs[:-1]:
                    pe_job(FIRST, job)
                for n, (m, x) in enumerate(first_pieces):
                    if n == 0:
                        pe.wait_ge(stacked, 16 * STACK_DMAS)
                    if n == MXG:
                        pe_job(FIRST, ("max", 0))
                    pe_max_piece(m, x, n)

        def clear():
            with nc.Block() as blk:
                @blk.sync
                def _(sp):
                    for one in cleared_early + cleared:
                        sp.sem_clear(one)
            links.update(dve=0, mv=0)

        clear()

        with nc.Block() as blk:
            @blk.tensor
            def _(pe):
                pe_body(BODY0)

            @blk.scalar
            def _(act):
                act_body(BODY0)

            @blk.vector
            def _(dve):
                dve_body(BODY0)

            @blk.gpsimd
            def _(pool):
                pool_body(BODY0)

            @blk.sync
            def _(sp):
                sp_body(BODY0, 0, 1)
                sp.sem_inc(out_done, 16)

        clear()

        def leave(eng, i):
            eng.drain().then_inc(arrived, 1)
            eng.wait_ge(go, i)

        with nc.Block() as blk:
            @blk.tensor
            def _(pe):
                with pe.Fori(1, B) as i:
                    pe_body(BODY)
                    leave(pe, i)

            @blk.scalar
            def _(act):
                with act.Fori(1, B) as i:
                    act_body(BODY)
                    leave(act, i)

            @blk.vector
            def _(dve):
                with dve.Fori(1, B) as i:
                    dve_body(BODY)
                    leave(dve, i)

            @blk.gpsimd
            def _(pool):
                with pool.Fori(1, B) as i:
                    pool_body(BODY)
                    leave(pool, i)

            @blk.sync
            def _(sp):
                with sp.Fori(1, B) as i:
                    sp_body(BODY, i, (i + 1) % B)
                    for one in cleared_early:
                        sp.sem_clear(one)
                    sp.wait_ge(arrived, 4)
                    for one in cleared:
                        sp.sem_clear(one)
                    sp.sem_inc(go, 1)

        links.update(dve=0, mv=0)

        with nc.Block() as blk:
            last_jobs = LAST.order.names

            @blk.sync
            def _(sp):
                sp_stored()
                sp_load_x1(B - 1)
                sp_adapter()
                sp_store_out(LAST, B - 1)
                sp.wait_ge(out_done, 16)

            @blk.gpsimd
            def _(pool):
                pool_rstd(1)
                pool_rstd(2)

            @blk.scalar
            def _(act):
                before = None
                act_values_out(LAST, -1)
                for job in last_jobs:
                    if before:
                        act_later(LAST, before)
                    act_job(LAST, job)
                    before = job

            @blk.vector
            def _(dve):
                for job in last_jobs:
                    dve_job(LAST, job)
                    if job in (("xo", 1), ("y", 1)):
                        dve_norm("x2" if job[0] == "xo" else "y")
                    if job == ("loss",):
                        for part in range(3):
                            dve_choose(part)

            @blk.tensor
            def _(pe):
                pe_values(LAST, -1)
                for job in last_jobs:
                    pe_job(LAST, job)


def constants():
    import numpy as np
    head = np.arange(P)[:, None] // HD == np.arange(HC)[None]
    batch = np.arange(TOK) // HD
    return {
        "c_ident": np.eye(P, dtype=np.float32),
        "c_head": head.astype(np.float32),
        "c_hide": np.where(batch[:, None] == batch[None], 0.0, NEG).astype(np.float32),
        "c_iota": np.arange(NE, dtype=np.float32)[None],
    }


def layout(inputs):
    import numpy as np
    a = {k: np.asarray(v) for k, v in inputs.items()}

    def t(name):
        return np.ascontiguousarray(a[name].T)

    r = {"x": a["x"], "ctxT": np.ascontiguousarray(a["ctx_1024"].transpose(0, 2, 1)),
         "mask": np.ascontiguousarray(a["mask_Bx1x1xS2_bf1"]).view(np.uint8).reshape(B, S2),
         **{f"W{n}T": t(f"L0_attn_W{n}") for n in ("q", "k", "v", "o", "lq", "lk", "lv")},
         "xWqT": t("L0_xattn_Wq"), "xWkT": t("L0_xattn_Wk"), "xWvT": t("L0_xattn_Wv"),
         "xWoT": t("L0_xattn_Wo")}
    for k, n in (("bq", "bq"), ("bv", "bv"), ("bo", "bo"), ("lna", "lna_w"), ("lnc", "lnc_w"), ("lnd", "lnd_w"),
                 ("blq", "blq"), ("blk", "blk"), ("blv", "blv")):
        r[k] = a[f"L0_attn_{n}"]
    for k in ("temp", "threshold", "factor"):
        r[k] = a[f"L0_attn_{k}"].reshape(1, 1)
    for k, n in (("Wbase", "W_base"), ("bbase", "b_base"), ("Wenc", "W_enc"), ("benc", "b_enc"), ("Wdec", "W_dec"),
                 ("bdec", "b_dec"), ("Wdown", "W_down"), ("bdown", "b_down"), ("Wup", "W_up"), ("bup", "b_up"),
                 ("cidx", "connected_idx")):
        r[k] = a[f"L0_ffn_{n}"]
    return {**r, **constants()}


def kernel(**inputs):
    import numpy as np
    import concourse.bacc as bacc
    from concourse.bass_utils import run_bass_kernel_spmd

    nc = bacc.Bacc("TRN2", target_bir_lowering=False, num_devices=1)
    arrays = {f"in_{k}": np.ascontiguousarray(v) for k, v in layout(inputs).items()}
    g = Shared({k[3:]: nc.dram_tensor(k, v.shape, mybir.dt.from_np(v.dtype), kind="ExternalInput").ap()
                for k, v in arrays.items()})
    g.out = nc.dram_tensor("out_dram", (B, T, D), F32, kind="ExternalOutput").ap()
    program(nc, g)
    r = run_bass_kernel_spmd(nc, [arrays], core_ids=[0])
    return r.results[0]["out_dram"]
```

```python
from contextlib import ExitStack

import concourse.bass as bass
from concourse import mybir

F32 = mybir.dt.float32
BF16 = mybir.dt.bfloat16
U8 = mybir.dt.uint8
I32 = mybir.dt.int32
ALU = mybir.AluOpType
ACT = mybir.ActivationFunctionType
AX = mybir.AxisListType

P = 128
B, T, D = 8, 512, 256
H, HD = 16, 16
S2 = 1601
QT = T // P
CH = D // P
HC = P // HD
GH = 4
NG = HC // GH
ITERS = 3
TOK = B * HD
EPS = 1e-5
SRING, MRING = 3, 3
NEG = -1e30
PARTS = 3
QPART = (0, 0, 1, 0, 1, 2)
KPART = (0, 1, 0, 2, 1, 0)
R_MASK = 6 * HD
R_MAX = R_MASK + 1
ROWS = R_MAX + 2


class Shared:

    def __init__(self, a):
        self.x, self.ctxT, self.mask = a["x"], a["ctxT"], a["mask"]
        self.x_head, self.rows, self.cols, self.Wl = a["x_head"], a["rows"], a["cols"], a["Wl"]
        self.WqT, self.WkT, self.WvT, self.WoT = a["WqT"], a["WkT"], a["WvT"], a["WoT"]
        self.bo = a["bo"]
        self.xWqT, self.xWkT, self.xWvT, self.xWoT = a["xWqT"], a["xWkT"], a["xWvT"], a["xWoT"]
        self.Wbase, self.bbase, self.Wenc, self.benc = a["Wbase"], a["bbase"], a["Wenc"], a["benc"]
        self.Wdec, self.bdec, self.Wdown, self.bdown = a["Wdec"], a["bdec"], a["Wdown"], a["bdown"]
        self.Wup, self.bup, self.cidx = a["Wup"], a["bup"], a["cidx"]
        self.c_ident, self.c_iota = a["c_ident"], a["c_iota"]


class Phase:

    def __init__(self, tail, order):
        self.tail, self.order = tail, Order(order)


class Order:

    def __init__(self, names):
        self.names = list(names)
        self.index = {n: i for i, n in enumerate(self.names)}

    def before(self, name):
        return self.index[name]

    def after(self, name):
        return self.index[name] + 1


def sbuf(nc, stack, name, shape, dt=F32):
    return stack.enter_context(nc.sbuf_tensor(name, shape, dt))


def program(nc, g):
    with ExitStack() as whole:
        g.sem = lambda name: whole.enter_context(nc.semaphore(name))
        banks = whole.enter_context(nc.psum_tensor("banks", [P, 6, T], F32))
        g.st = [banks[:, 2 * i:2 * i + 2, :] for i in range(2)]
        g.mx = [banks[:, 4 + i, :] for i in range(2)]
        g.scores = [banks[:, i, :] for i in range(SRING)]
        g.max_scores = [banks[:, SRING + i, :] for i in range(MRING)]
        g.av = whole.enter_context(nc.psum_tensor("values", [P, T], F32))
        g.W = whole.enter_context(nc.psum_tensor("work", [P, T], F32))
        g.ident = sbuf(nc, whole, "ident", [P, P])
        g.ident_b = sbuf(nc, whole, "ident_b", [P, P], BF16)
        g.mhalf = sbuf(nc, whole, "mhalf", [P, 2 * H])
        g.attn_dram = nc.dram_tensor("attn_dram", (B, HD, D), F32, kind="Internal").ap()
        g.part_dram = nc.dram_tensor("parts_dram", (PARTS, P, T), BF16, kind="Internal").ap()
        g.kpart_dram = nc.dram_tensor("key_parts_dram", (PARTS, P, S2), BF16, kind="Internal").ap()
        g.mask_dram = nc.dram_tensor("mask_dram", (B, SP_), BF16, kind="Internal").ap()
        g.x1_dram = nc.dram_tensor("x1_dram", (B, T, D), F32, kind="Internal").ap()
        g.max_dram = nc.dram_tensor("max_dram", (2 * GH * QT, P), BF16, kind="Internal").ap()

        cross_attention_and_ffn(nc, g)


XKT = -(-S2 // P)
ROW_VECTORS = D + 5 * HD + ITERS + 2
COLUMNS = HC + TOK + 2 * CH
SP_ = XKT * P
PIECES = ((0, 401), (401, 400), (801, 400), (1201, 400))
MXG = GH * QT * len(PIECES)
MXS = 5
XSLOTS = CH * NG * XKT
KBUF = 4
LEAD = 4
NE, EH, ER = 8, 64, 64
NDEC = NE * CH


def short_self_attention(nc, g, s, view, beside):
    ident, av, st, mx, sem = g.ident, g.av, g.st, g.mx, g.sem
    W = st[0][:, 0, :]
    def sb(name, shape, dt=F32):
        return sbuf(nc, s, name, shape, dt)

    x, xn, xnT = view["x"], view["xn"], view["xnT"]
    wq, wk, wv, wo = view["wq"], view["wk"], view["wv"], view["wo"]
    wl = sb("s_wl", [P, 3, P])
    rowv = sb("s_row_vectors", [TOK, ROW_VECTORS])
    lna = rowv[:, 0:D]
    bl = rowv[:, D:D + 3 * HD].rearrange("p (n d) -> p n d", d=HD)
    lncd = rowv[:, D + 3 * HD:D + 5 * HD].rearrange("p (n d) -> p n d", d=HD)
    tt = rowv[:, D + 5 * HD:D + 5 * HD + ITERS]
    tf = rowv[:, D + 5 * HD + ITERS:ROW_VECTORS]
    colv = sb("s_columns", [P, COLUMNS])
    head = colv[:, 0:HC]
    hide = colv[:, HC:HC + TOK]
    bq = colv[:, HC + TOK:HC + TOK + CH]
    bv = colv[:, HC + TOK + CH:COLUMNS]
    tone, tpos, tpow = (sb(n, [TOK, ITERS]) for n in ("s_tone", "s_tpos", "s_tpow"))
    ln_w = sb("s_ln_w", [TOK, ITERS, 2, HD])
    state = view["state"]
    cen, sq = view["cen"], view["sq"]
    qsT, ksM = view["qsT"], view["ksM"]
    sc, pT = view["sc"], view["pT"]
    m8, mb = view["m8"], view["mb"]
    stats = sb("s_stats", [TOK, 6])
    meanvar = sb("s_meanvar", [TOK, 2])
    rows = sb("s_rows", [TOK, 3, H, HD])
    msum = sb("s_sums", [TOK, 2 * H])
    var = sb("s_vars", [TOK, 2 * H])
    nmax = sb("s_neg_max", [TOK, H])
    rsum = sb("s_rsum", [TOK, H])
    outs = sb("s_outs", [TOK, ITERS, D])
    adiff = sb("s_abs_diff", [TOK, D])
    asum = sb("s_abs_sum", [TOK, 1])
    ones = sb("s_ones", [P, P])
    diff, lim, keep, other = (sb(n, [P, 1]) for n in ("s_diff", "s_lim", "s_keep", "s_other"))
    proj = view["proj"]

    early = sem("s_early_in")
    loaded = sem("s_in")
    late = sem("s_late_in")
    zeroed = sem("s_zeroed")
    own = sem("s_own")
    xn_ready = sem("s_x_normed")
    bias_ready = sem("s_bias")
    kv_made = sem("s_kv_transposed")
    oT_made = sem("s_out_transposed")
    diff_ready = sem("s_diff")
    asum_ready = sem("s_abs")
    sel_ready = sem("s_selected")
    mm = sem("s_products")
    read = sem("s_read")
    var_ready = sem("s_var")
    root_ready = sem("s_roots")
    cen_ready = sem("s_centered_in")
    sq_ready = sem("s_squared")
    qk_ready = sem("s_qk_normed")
    rows_ready = sem("s_rows_in")
    t_ready = sem("s_transposed")
    sc_ready = sem("s_scored")
    p_ready = sem("s_exped")
    p_out = sem("s_probs_taken")
    o_ready = sem("s_out")
    st_ready = sem("s_state_in")
    mask_ready = sem("s_mask")
    stored = sem("s_stored")
    early_n = 16 * 3
    loaded_n = 16 * 5
    MMS = 8

    def self_sp(sp):
        for dst, src in ((x, g.x_head), (ident[:], g.c_ident), (rowv[:], g.rows.broadcast_to([TOK, ROW_VECTORS]))):
            sp.dma_start(dst, src).then_inc(early, 16)
        for dst, src in ((wq, g.WqT), (wk, g.WkT)):
            sp.dma_start(dst[:], src.rearrange("(c p) d -> p c d", p=P)).then_inc(loaded, 16)
        sp.dma_start(m8[:], g.mask).then_inc(late, 16)
        sp.dma_start(wo[:], g.WoT.rearrange("(c p) d -> p c d", p=P)).then_inc(late, 16)
        beside("sp", 0)
        sp.wait_ge(mask_ready, 1)
        sp.dma_start(g.mask_dram, mb[:]).then_inc(stored, 16)
        sp.wait_ge(stored, 16)
        beside("sp", 1)
        sp.wait_ge(mm, 4 + MMS * ITERS)
        beside("sp", 2)
        sp.wait_ge(read, 3)
        sp.dma_start(g.attn_dram.rearrange("b t d -> (b t) d"), proj[:]).then_inc(g.attn_out, 16)

    def self_pool(pool):
        p = nc.gpsimd
        p.memset(g.mhalf[:], -0.5).then_inc(zeroed, 1)
        p.memset(ones[:], 1.0).then_inc(zeroed, 1)
        p.memset(mb[:], NEG).then_inc(zeroed, 1)
        pool.wait_ge(zeroed, 3)

        def root(buf, n):
            pool.wait_ge(var_ready, n)
            p.tensor_tensor(buf, buf, g.mhalf[:, 0:buf.shape[-1]], ALU.pow).then_inc(root_ready, 1)

        root(meanvar[:, 1:2], 1)
        root(tpow[:], 2)
        for it in range(ITERS):
            root(var[:], 3 + it)
            pool.wait_ge(root_ready, 3 + it)
            beside("pool", it)
        beside("pool", ITERS)
        pool.wait_ge(read, 3)

    def self_act(act):
        a = nc.scalar
        act.dma_start(wl[:], g.Wl.rearrange("n p d -> p n d")).then_inc(loaded, 16)
        act.dma_start(wv[:], g.WvT.rearrange("(c p) d -> p c d", p=P)).then_inc(loaded, 16)
        act.dma_start(colv[:], g.cols).then_inc(loaded, 16)
        act.wait_ge(mm, 1)
        a.activation(xnT[:], W[:, 0:D].rearrange("p (c t) -> p c t", c=CH), ACT.Copy).then_inc(read, 1)
        act.wait_ge(loaded, loaded_n)
        act.wait_ge(bias_ready, 1)
        for i, bank in enumerate((W, mx[0], mx[1])):
            act.wait_ge(mm, 2 + i)
            for c in range(CH):
                src = bank[:, c * TOK:(c + 1) * TOK]
                if i == 0:
                    last = a.activation(state[:, i, c, :], src, ACT.Identity, bias=bq[:, c:c + 1],
                                        scale=float(HD) ** -0.25)
                elif i == 1:
                    last = a.activation(state[:, i, c, :], src, ACT.Copy, scale=float(HD) ** -0.25)
                else:
                    last = a.activation(state[:, i, c, :], src, ACT.Identity, bias=bv[:, c:c + 1])
            last.then_inc(st_ready, 1)
        for it in range(ITERS):
            base = 4 + MMS * it
            act.wait_ge(cen_ready, it + 1)
            a.activation(sq[:], cen[:], ACT.Square).then_inc(sq_ready, 1)
            beside("act", it)
            act.wait_ge(mm, base + 3)
            a.activation(qsT[:], mx[0][:, 0:D].rearrange("p (c t) -> p c t", c=CH), ACT.Copy).then_inc(t_ready, 1)
            if it < ITERS - 1:
                act.wait_ge(kv_made, it + 1)
                a.activation(state[:, 1:3, :, :], mx[1].rearrange("p (i c t) -> p i c t", i=2, c=CH),
                             ACT.Copy).then_inc(st_ready, 1)
            act.wait_ge(sc_ready, it + 1)
            for h in range(H):
                last = a.activation(sc[:, h, :], sc[:, h, :], ACT.Exp, bias=nmax[:, h:h + 1],
                                    accum_out=rsum[:, h:h + 1])
                if h % HC == HC - 1:
                    last.then_inc(p_ready, 1)
            act.wait_ge(mm, base + 6)
            a.activation(pT[:, 0:HC, :], st[0].rearrange("p a (h t) -> p (a h) t", t=TOK),
                         ACT.Copy).then_inc(p_out, 1)
        act.wait_ge(diff_ready, 1)
        a.activation(adiff[:], adiff[:], ACT.Abs, accum_out=asum[:]).then_inc(asum_ready, 1)

    def self_pe(pe):
        def transposes(bank, pieces):
            for i, src in enumerate(pieces):
                last = pe.transpose(bank[:, i * TOK:(i + 1) * TOK], src, ident[:])
            return last

        pe.wait_ge(early, early_n)
        pe.wait_ge(xn_ready, 1)
        transposes(W, [xn[:, c * P:(c + 1) * P] for c in range(CH)]).then_inc(mm, 1)
        pe.wait_ge(read, 1)
        pe.wait_ge(loaded, loaded_n)
        for w, bank in ((wq, W), (wk, mx[0]), (wv, mx[1])):
            for c in range(CH):
                for kin in range(CH):
                    last = pe.matmul(bank[:, c * TOK:(c + 1) * TOK], w[:, kin, c * P:(c + 1) * P],
                                     xnT[:, kin, :], start=kin == 0, stop=kin == CH - 1)
            last.then_inc(mm, 1)
        for it in range(ITERS):
            pe.wait_ge(st_ready, 3 + 2 * it)
            for n, bank, first in ((0, W, 0), (1, W, D), (2, av, 0)):
                for c in range(CH):
                    last = pe.matmul(bank[:, first + c * P:first + (c + 1) * P], state[:, n, c, :], wl[:, n, :],
                                     start=True, stop=True)
                if n:
                    last.then_inc(mm, 1)
            beside("pe", it)
            pe.wait_ge(qk_ready, it + 1)
            cenr = cen[:].rearrange("p (n c h) d -> p n c (h d)", n=2, c=CH)
            transposes(mx[0], [cenr[:, 0, c, :] for c in range(CH)])
            pe.wait_ge(rows_ready, it + 1)
            transposes(av, [cenr[:, 1, c, :] for c in range(CH)]).then_inc(mm, 1)
            if it < ITERS - 1:
                rowsr = rows[:].rearrange("p n (c h) d -> p n c (h d)", c=CH)
                transposes(mx[1], [rowsr[:, n, c, :] for n in (1, 2) for c in range(CH)]).then_inc(kv_made, 1)
            pe.wait_ge(t_ready, (1 + CH) * (it + 1))
            for c in range(CH):
                for half in range(2):
                    last = pe.matmul(st[c][:, half, :], qsT[:, c, :],
                                     ksM[:, c, half * GH:(half + 1) * GH, :].rearrange("p h t -> p (h t)"),
                                     start=True, stop=True)
                last.then_inc(mm, 1)
            beside("pe values", it)
            for c in range(CH):
                pe.wait_ge(p_ready, CH * it + c + 1)
                for h in range(HC):
                    last = pe.transpose(st[c][:, h // GH, h % GH * TOK:(h % GH + 1) * TOK],
                                        sc[:, c * HC + h, :], ident[:])
                last.then_inc(mm, 1)
            pe.wait_ge(p_out, 2 * it + 2)
            for h in range(H):
                last = pe.matmul(av[:, h * HD:(h + 1) * HD], pT[:, h, :], rows[:, 2, h, :], start=True, stop=True)
            last.then_inc(mm, 1)
            if it < ITERS - 1:
                pe.wait_ge(o_ready, it + 1)
                transposes(W, [outs[:, it, c * P:(c + 1) * P] for c in range(CH)]).then_inc(oT_made, 1)
        pe.wait_ge(asum_ready, 1)
        pe.matmul(W[:, 0:1], ones[:], asum[:], start=True, stop=True).then_inc(mm, 1)
        pe.wait_ge(late, 32)
        pe.wait_ge(sel_ready, 1)
        transposes(mx[0], [xn[:, c * P:(c + 1) * P] for c in range(CH)]).then_inc(mm, 1)
        pe.wait_ge(read, 2)
        for kin in range(CH):
            last = pe.matmul(av[:, 0:D], xnT[:, kin, :], wo[:, kin, :], start=kin == 0, stop=kin == CH - 1)
        last.then_inc(mm, 1)

    def self_dve(dve):
        v = nc.vector
        n = [0]

        def link(ins):
            n[0] += 1
            ins.then_inc(own, 1)
            dve.wait_ge(own, n[0])

        dve.wait_ge(early, early_n)
        link(v.bn_stats(stats[:], x[:]))
        link(v.bn_aggr(meanvar[:], stats[:]))
        v.tensor_scalar(meanvar[:, 1:2], meanvar[:, 1:2], EPS, None, ALU.add).then_inc(var_ready, 1)
        dve.wait_ge(root_ready, 1)
        link(v.tensor_scalar(xn[:], x[:], meanvar[:, 0:1], meanvar[:, 1:2], ALU.subtract, ALU.mult))
        v.tensor_tensor(xn[:], xn[:], lna[:], ALU.mult).then_inc(xn_ready, 1)
        v.tensor_copy(g.ident_b[:], ident[:])
        dve.wait_ge(loaded, loaded_n)
        for i in range(1, ITERS):
            link(v.tensor_scalar(tt[:, i:i + 1], tt[:, i:i + 1], 0.005 * i, None, ALU.add))
        v.tensor_scalar(tpow[:], tt[:], 1e-37, None, ALU.max).then_inc(var_ready, 1)
        link(v.tensor_scalar(tone[:], tt[:], 1.0, None, ALU.not_equal))
        link(v.tensor_scalar(tpos[:], tt[:], 0.0, None, ALU.is_gt))
        link(v.tensor_tensor(tone[:], tone[:], tpos[:], ALU.mult))
        v.tensor_scalar(bq[:], bq[:], float(HD) ** -0.25, None, ALU.mult).then_inc(bias_ready, 1)
        dve.wait_ge(root_ready, 2)
        link(v.tensor_scalar(tpow[:], tpow[:], 1.0, None, ALU.subtract))
        link(v.tensor_tensor(tpow[:], tpow[:], tone[:], ALU.mult))
        link(v.tensor_scalar(tpow[:], tpow[:], 1.0, None, ALU.add))
        for it in range(ITERS):
            v.tensor_scalar(ln_w[:, it, 0, :], lncd[:, 0, :], tpow[:, it:it + 1], float(HD) ** -0.5,
                            ALU.mult, ALU.mult)
            link(v.tensor_copy(ln_w[:, it, 1, :], lncd[:, 1, :]))
        dve.wait_ge(zeroed, 3)
        dve.wait_ge(late, 32)
        v.tensor_scalar(mb[:, 0:S2], m8[:], 0.0, NEG, ALU.is_equal, ALU.mult).then_inc(mask_ready, 1)
        for it in range(ITERS):
            base = 4 + MMS * it
            heads = W[:].rearrange("p (n h d) -> p n h d", n=2, d=HD)
            dve.wait_ge(mm, base + 1)
            link(v.tensor_tensor(rows[:, 0:2, :, :], heads,
                                 bl[:, 0:2, :].unsqueeze(2).broadcast_to([TOK, 2, H, HD]), ALU.add))
            dve.wait_ge(mm, base + 2)
            v.tensor_tensor(rows[:, 2, :, :], av[:, 0:D].rearrange("p (h d) -> p h d", d=HD),
                            bl[:, 2, :].unsqueeze(1).broadcast_to([TOK, H, HD]), ALU.add).then_inc(rows_ready, 1)
            qk = rows[:, 0:2, :, :].rearrange("p n h d -> p (n h) d")
            link(v.tensor_reduce(msum[:], qk, AX.X, ALU.add))
            link(v.tensor_scalar(msum[:], msum[:], 1.0 / HD, None, ALU.mult))
            v.tensor_tensor(cen[:], qk, msum[:].unsqueeze(2).broadcast_to([TOK, 2 * H, HD]),
                            ALU.subtract).then_inc(cen_ready, 1)
            dve.wait_ge(sq_ready, it + 1)
            link(v.tensor_reduce(var[:], sq[:], AX.X, ALU.add))
            v.tensor_scalar(var[:], var[:], 1.0 / HD, EPS, ALU.mult, ALU.add).then_inc(var_ready, 1)
            link(v.tensor_tensor(cen[:].rearrange("p (n h) d -> p n h d", n=2),
                                 cen[:].rearrange("p (n h) d -> p n h d", n=2),
                                 ln_w[:, it, :, :].unsqueeze(2).broadcast_to([TOK, 2, H, HD]), ALU.mult))
            beside("dve", it)
            dve.wait_ge(root_ready, 3 + it)
            v.tensor_tensor(cen[:], cen[:], var[:].unsqueeze(2).broadcast_to([TOK, 2 * H, HD]),
                            ALU.mult).then_inc(qk_ready, 1)
            dve.wait_ge(mm, base + 3)
            for c in range(CH):
                v.tensor_tensor(ksM[:, c, :, :],
                                av[:, c * TOK:(c + 1) * TOK].unsqueeze(1).broadcast_to([P, HC, TOK]),
                                head[:].unsqueeze(2).broadcast_to([P, HC, TOK]), ALU.mult).then_inc(t_ready, 1)
            for c in range(CH):
                dve.wait_ge(mm, base + 4 + c)
                link(v.tensor_tensor(sc[:, c * HC:(c + 1) * HC, :], st[c].rearrange("p a (h t) -> p (a h) t", t=TOK),
                                     hide[:].unsqueeze(1).broadcast_to([TOK, HC, TOK]), ALU.add))
            v.tensor_reduce(nmax[:], sc[:], AX.X, ALU.max, negate=True).then_inc(sc_ready, 1)
            beside("dve values", it)
            dve.wait_ge(p_ready, CH * (it + 1))
            link(v.reciprocal(rsum[:], rsum[:]))
            dve.wait_ge(mm, base + 7)
            v.tensor_copy(pT[:, HC:H, :], st[1].rearrange("p a (h t) -> p (a h) t", t=TOK)).then_inc(p_out, 1)
            dve.wait_ge(mm, base + 8)
            v.tensor_tensor(outs[:, it, :].rearrange("p (h d) -> p h d", d=HD),
                            av[:, 0:D].rearrange("p (h d) -> p h d", d=HD),
                            rsum[:].unsqueeze(2).broadcast_to([TOK, H, HD]), ALU.mult).then_inc(o_ready, 1)
            if it < ITERS - 1:
                dve.wait_ge(oT_made, it + 1)
                v.tensor_tensor(state[:, 0, :, :], state[:, 0, :, :],
                                W[:, 0:D].rearrange("p (c t) -> p c t", c=CH), ALU.add).then_inc(st_ready, 1)
        dve.wait_ge(o_ready, ITERS)
        v.tensor_tensor(adiff[:], outs[:, 1, :], outs[:, 0, :], ALU.subtract).then_inc(diff_ready, 1)
        end = 4 + MMS * ITERS
        dve.wait_ge(mm, end + 1)
        link(v.tensor_scalar(diff[:], W[:, 0:1], 1.0 / (B * T * D), None, ALU.mult))
        link(v.tensor_scalar(lim[:], diff[:], tf[:, 1:2], tf[:, 0:1], ALU.mult, ALU.add))
        link(v.tensor_tensor(keep[:], diff[:], lim[:], ALU.is_lt))
        link(v.tensor_scalar(other[:], keep[:], -1.0, 1.0, ALU.mult, ALU.add))
        link(v.tensor_scalar(outs[:, 1, :], outs[:, 1, :], keep[:], None, ALU.mult))
        v.scalar_tensor_tensor(xn[:], outs[:, 2, :], other[:], outs[:, 1, :], ALU.mult,
                               ALU.add).then_inc(sel_ready, 1)
        dve.wait_ge(mm, end + 2)
        v.tensor_copy(xnT[:], mx[0][:, 0:D].rearrange("p (c t) -> p c t", c=CH)).then_inc(read, 1)
        dve.wait_ge(mm, end + 3)
        v.tensor_copy(proj[:], av[:, 0:D]).then_inc(read, 1)

    return self_sp, self_pool, self_act, self_pe, self_dve


def cross_attention_and_ffn(nc, g):
    sem, W, ident, ident_b, scores, mx, av = g.sem, g.W, g.ident, g.ident_b, g.scores, g.max_scores, g.av
    Wb = W[:].bitcast(BF16)
    with ExitStack() as s:
        def sb(name, shape, dt=F32):
            return sbuf(nc, s, name, shape, dt)

        xqT, xkT, xvT, xoT, wbase = (sb(n, [P, CH, D]) for n in ("xqT", "xkT", "xvT", "xoT", "wbase"))
        wenc = sb("wenc", [P, CH, NE, EH])
        wdec = sb("wdec", [P, NE, D])
        bo = sb("bo_rows", [P, D])
        benc = sb("benc_cols", [P, NE * EH // P])
        bdec = sb("bdec_cols", [P, NE, CH])
        cidx = sb("cidx", [P, NE], I32)
        cidxf = sb("cidx_f", [P, NE])
        iota = sb("iota", [P, NE])
        iotam = sb("iota_minus", [P, NE])
        ones = sb("ones", [P, P])
        wdown = sb("wdown", [P, CH, ER])
        bdown = sb("bdown_col", [ER, 1])
        wup = sb("wup", [ER + 2, D])
        midT = sb("midT", [ER + 2, T])
        ctxT = sb("ctxT_sb", [P, CH, S2])
        kst = sb("xk_stacks", [P, 2, HC, SP_], BF16)
        qst = sb("xq_stacks", [P, 2, HC, T], BF16)
        vals = sb("xv_rows", [P, 2, XKT, HC, HD + 1])
        probs = sb("xprobs", [P, 2, GH, T])
        oS = sb("xo_unnormed", [P, T])
        rz = sb("xrsum", [P, QT, GH])
        nmp = sb("xneg_max_pieces", [P, 2, GH * QT, len(PIECES)])
        nm = sb("xneg_max", [P, GH * QT])
        comb = sb("xneg_max_parts", [P, 2, GH * QT], BF16)
        mrow = sb("xneg_max_rows", [2 * GH * QT, P], BF16)
        kpart = sb("xk_parts", [P, KBUF, PARTS, PIECES[0][1]], BF16)
        krest = sb("xk_rest", [P, KBUF, PIECES[0][1]])
        qpart = sb("xq_parts", [P, PARTS, T], BF16)
        qrest = sb("xq_rest", [P, T])
        xa = sb("xa", [P, QT, D])
        at = sb("attn_rows", [HD, D])
        xT = sb("xT", [P, CH, T])
        ox = sb("ox", [P, QT, D])
        x2 = sb("x2", [P, QT, D])
        x2T = sb("x2T", [P, CH, T])
        hT = sb("hT", [P, NE * EH // P, T])
        err = sb("err", [P, 2, T])
        loss = sb("loss", [P, NDEC])
        l8 = sb("l8", [P, NE])
        pick = sb("pick", [P, NE])
        sc = sb("sc", [P, 4])
        adp = sb("adp", [1, 1], I32)
        stats = sb("xstats", [P, QT, 6])
        meanvar = sb("xmeanvar", [P, QT, 2])
        rstd = sb("xrstd", [P, QT])

        loaded = sem("x_weights_in")
        zeroed = sem("x_zeroed")
        made = sem("x_made")
        exped = sem("x_exped")
        summed = sem("x_summed")
        evac = sem("x_values_out")
        mxd = sem("x_max_made")
        mxr = sem("x_max_read")
        comb_ready = sem("x_max_parts")
        mrow_out = sem("x_max_rows_out")
        max_in = sem("x_max_in")
        w_full = sem("x_work_full")
        w_free = sem("x_work_free")
        khigh = sem("x_k_high")
        kmid = sem("x_k_mid")
        klow = sem("x_k_low")
        kparts_out = [sem(f"x_k_parts_out{i}") for i in range(KBUF)]
        qhigh = sem("x_q_high")
        qmid = sem("x_q_mid")
        qlow = sem("x_q_low")
        qparts_out = sem("x_q_parts_out")
        stacked = sem("x_stacked")
        c_in = sem("x_ctx_in")
        x_in = sem("x_x_in")
        sum_ready = sem("x_summed_x")
        mv_ready = sem("x_meanvar")
        rstd_ready = sem("x_rstd")
        normed = sem("x_normed")
        x1_out = sem("x_x1_out")
        x1_in = sem("x_x1_in")
        sq_done = sem("x_err_squared")
        adp_ready = sem("x_adapter")
        adp_in = sem("x_adapter_in")
        out_done = sem("x_out")
        own = {e: sem(f"x_own_{e}") for e in ("dve", "pool")}
        arrived = sem("x_arrived")
        go = sem("x_go")
        cleared_early = [mrow_out, max_in, khigh, kmid, klow, *kparts_out, qhigh, qmid, qlow, qparts_out, stacked, c_in,
                         x_in, sum_ready, mv_ready, rstd_ready, normed, x1_out, x1_in, sq_done, adp_ready, adp_in]
        cleared = [made, exped, summed, evac, mxd, mxr, comb_ready, w_full, w_free, *own.values(), arrived]

        NP = len(PIECES)
        keys = [("kproj", i) for i in range(NP)]
        CHOOSE_STEPS = 11
        SLOT_WORK = {
            (0, 0): {0: [("v", 0)], 1: [("otr", 3), ("v", 1)], 2: [("v", 2)], 3: [("v", 3)], 4: [("oT", 0)],
                     5: [("oT", 1)], 6: [("xo", 0)], 7: [("xo", 1)], 8: [("x1T", 0)], 9: [("x1T", 1), ("max", 1)],
                     10: [keys[0]], 11: [keys[1]], 12: [("x2T", 0)]},
            (0, 1): {0: [("x2T", 1)], 1: [("otr", 0), ("enc", 0)], 2: [("enc", 1)], 3: [("enc", 2)], 4: [("enc", 3)],
                     5: [keys[2]], 6: [keys[3]], 7: [("qproj", 0)], 8: [("dec", 0)], 9: [("dec", 1), ("max", 2)],
                     **{10 + i: [("dec", 2 + i)] for i in range(3)}},
            (1, 0): {0: [("dec", 5)], 1: [("otr", 1), ("dec", 6)], **{2 + i: [("dec", 7 + i)] for i in range(7)},
                     9: [("dec", 14), ("max", 3)], 10: [("dec", 15)], 11: [("kproj", NP), ("loss",)],
                     12: [("kproj", NP + 1)]},
            (1, 1): {0: [("kproj", NP + 2)], 1: [("otr", 2), ("kproj", NP + 3)], 2: [("qproj", 1)], 3: [("mid",)],
                     4: [("y", 0)], 5: [("y", 1)], 6: [("v", 4)], 7: [("v", 5)], 8: [("v", 6)],
                     9: [("max", 4)], 10: [("v", 7)]},
        }
        def norm_steps(step, what, first, last):
            return [(step, what, q) for q in range(first, last)]

        def choose_steps(first, last):
            return [("choose", "adapter", n) for n in range(first, last)]

        VECTOR_WORK = {
            (0, 0): {2: norm_steps("stats", "x1", 0, 2), 3: norm_steps("stats", "x1", 2, 4), 4: [("aggr", "x1", 0)],
                     5: norm_steps("apply", "x1", 0, 2), 6: norm_steps("apply", "x1", 2, 4),
                     7: norm_steps("stats", "x2", 0, 2), 8: norm_steps("stats", "x2", 2, 4) + [("aggr", "x2", 0)],
                     10: norm_steps("apply", "x2", 0, 2), 11: norm_steps("apply", "x2", 2, 4)},
            (0, 1): {}, (1, 0): {12: choose_steps(0, 4)},
            (1, 1): {0: choose_steps(4, 8), 1: choose_steps(8, CHOOSE_STEPS),
                     5: norm_steps("stats", "y", 0, 2), 6: norm_steps("stats", "y", 2, 4) + [("aggr", "y", 0)],
                     7: norm_steps("apply", "y", 0, 4)},
        }
        TAIL = ("oT", "xo", "x2T", "enc", "dec", "loss", "mid", "y")

        def of_tail(job):
            return job[0] in TAIL or job == ("otr", 3)

        def work_at(tail, k, gr, t):
            w = SLOT_WORK[k, gr].get(t, [])
            return [j for j in w if tail or not of_tail(j)]

        def vector_work_at(tail, k, gr, t):
            w = VECTOR_WORK[k, gr].get(t, [])
            return [j for j in w if tail or j[1] == "x1"]

        def body_order(tail):
            return [j for k in range(CH) for gr in range(NG) for t in range(XKT) for j in work_at(tail, k, gr, t)]

        KEYS_BESIDE = [[("kproj", i) for i in one] for one in (range(0, 3), range(3, 6), range(6, 2 * NP))]
        VALUES_BESIDE = [[("v", 4), ("v", 5)], [("v", 6), ("v", 7)], []]
        AFTER = [("x1T", 0), ("x1T", 1), ("qproj", 0), ("max", 0), ("qproj", 1)]
        FIRST = Phase(False, [j for it in range(ITERS) for j in KEYS_BESIDE[it] + VALUES_BESIDE[it]] + AFTER)
        BODY0 = Phase(False, body_order(False))
        BODY = Phase(True, body_order(True))
        LAST = Phase(True, [j for kg in SLOT_WORK.values() for t in sorted(kg) for j in kg[t] if of_tail(j)])

        def second_bank(ph, job):
            return ph is LAST and job[0] in TAIL and len(job) > 1

        def bank_of(ph, job):
            return mx[0] if second_bank(ph, job) and job[1] % 2 else g.W[:]

        def pe_begin(ph, job):
            taken = ph.order.before(job) - (second_bank(ph, job) and job[1] > 0)
            if taken:
                nc.tensor.wait_ge(w_free, taken)

        def transposes(W, src, c):
            for q in range(QT):
                last = nc.tensor.transpose(W[:, q * P:(q + 1) * P], src[:, q, c * P:(c + 1) * P], ident[:])
            return last

        def rows_of(W, lhs, rhs, half, extra=None):
            for i in range(2):
                q = 2 * half + i
                for c in range(CH):
                    last = nc.tensor.matmul(W[:, i * D:(i + 1) * D], lhs[:, c, q * P:(q + 1) * P], rhs[:, c, :],
                                            start=c == 0, stop=c == CH - 1 and extra is None)
                if extra:
                    last = nc.tensor.matmul(W[:, i * D:(i + 1) * D], extra[0][:, q * P:(q + 1) * P], extra[1][:],
                                            start=False, stop=True)
            return last

        def pe_job(ph, job):
            pe = nc.tensor
            name, i = job[0], job[1] if len(job) > 1 else 0
            pe_begin(ph, job)
            W = bank_of(ph, job)
            if name == "x1T":
                pe.wait_ge(normed, normed_of(ph, "x1"))
                last = transposes(W, xa, i)
            elif name == "oT":
                last = transposes(W, ox, i)
            elif name == "x2T":
                pe.wait_ge(normed, normed_of(ph, "x2"))
                last = transposes(W, x2, i)
            elif name == "xo":
                pe.wait_ge(w_free, ph.order.after(("oT", 1)))
                last = rows_of(W, x2T, xoT, i)
            elif name == "y":
                pe.wait_ge(w_free, ph.order.after(("mid",)))
                last = rows_of(W, x2T, wbase, i, (midT, wup))
            elif name == "kproj":
                c, piece = divmod(i, NP)
                k0, n = PIECES[piece]
                pe.wait_ge(c_in, 16)
                for kin in range(CH):
                    last = pe.matmul(W[:, 0:n], xkT[:, kin, c * P:(c + 1) * P], ctxT[:, kin, k0:k0 + n],
                                     start=kin == 0, stop=kin == CH - 1)
            elif name == "qproj":
                pe.wait_ge(w_free, ph.order.after(("x1T", 1)))
                for kin in range(CH):
                    last = pe.matmul(W[:], xqT[:, kin, i * P:(i + 1) * P], xT[:, kin, :],
                                     start=kin == 0, stop=kin == CH - 1)
            elif name == "v":
                c = (i // 4 + 1) % CH
                for tt in range(4 * (i % 4), min(4 * (i % 4) + 4, XKT)):
                    rows = min(P, S2 - tt * P)
                    for kin in range(CH):
                        last = pe.matmul(W[0:rows, (tt % 4) * P:(tt % 4 + 1) * P], ctxT[:, kin, tt * P:tt * P + rows],
                                         xvT[:, kin, c * P:(c + 1) * P], start=kin == 0, stop=kin == CH - 1)
            elif name == "enc":
                pe.wait_ge(w_free, ph.order.after(("x2T", 1)))
                for kin in range(CH):
                    last = pe.matmul(W[:], wenc[:, kin, 2 * i:2 * i + 2, :].rearrange("p n h -> p (n h)"),
                                     x2T[:, kin, :], start=kin == 0, stop=kin == CH - 1)
            elif name == "dec":
                n, c = divmod(i, CH)
                pe.wait_ge(w_free, ph.order.after(("enc", n // 2)))
                last = pe.matmul(W[:], wdec[:, n, c * P:(c + 1) * P], hT[:, n // 2, :], start=True, stop=True)
            elif name == "loss":
                pe.wait_ge(sq_done, NDEC)
                last = pe.matmul(W[:, 0:NDEC], ones[:], loss[:], start=True, stop=True)
            elif name == "mid":
                pe.wait_ge(adp_in, 64)
                for kin in range(CH):
                    last = pe.matmul(W[0:ER, :], wdown[:, kin, :], x2T[:, kin, :], start=kin == 0, stop=kin == CH - 1)
            elif name == "max":
                pe.wait_ge(comb_ready, i if ph is not FIRST else 1)
                last = pe.transpose(Wb[0:2 * GH * QT, 0:P], comb[:].rearrange("p a b -> p (a b)"), ident_b[:])
            elif name == "otr":
                pe.wait_ge(evac, 1 if i == CH * NG - 1 else i + 1 + ph.tail)
                last = transposes(W, oS[:].rearrange("p (q n) -> p q n", q=QT), 0)
            last.then_inc(w_full, 1)

        def normed_of(ph, what):
            order = [n for n in ("x1", "x2", "y") if n == "x1" and ph is not LAST or n != "x1" and ph.tail]
            return order.index(what) + 1

        def max_event(e):
            m, x = divmod(e + LEAD * MXS, XKT * MXS)
            return (m + 1, x) if x < MXG else None

        MAXES = [max_event(e) for e in range(XSLOTS * MXS)]
        COUNT = [0]
        for one in MAXES:
            COUNT.append(COUNT[-1] + (one is not None))

        def pe_max_piece(m, x, n):
            pe = nc.tensor
            jq, piece = divmod(x, NP)
            j, q = divmod(jq, QT)
            k, gr = divmod(m, NG)
            k0, w = PIECES[piece]
            h = gr * GH + j
            if n >= MRING:
                pe.wait_ge(mxr, n - MRING + 1)
            pe.matmul(mx[n % MRING][:, 0:w], qst[0:R_MAX, k % 2, h, q * P:(q + 1) * P], kst[0:R_MAX, k % 2, h, k0:k0 + w],
                      start=True, stop=True).then_inc(mxd, 1)

        STACK_DMAS = 2 * len(QPART) + 1

        def pe_max(e):
            one = MAXES[e]
            if one:
                if one == (2, 0):
                    nc.tensor.wait_ge(stacked, 16 * STACK_DMAS)
                if one == (4, 0):
                    nc.tensor.wait_ge(stacked, 32 * STACK_DMAS)
                pe_max_piece(*one, COUNT[e])

        def pe_scores(k, gr, t, j):
            pe = nc.tensor
            m = NG * k + gr
            n = GH * (XKT * m + t) + j
            if t == 0 and m and j == 0:
                pe.wait_ge(max_in, 16 * m)
            if n >= SRING:
                pe.wait_ge(exped, n - SRING + 1)
            h = gr * GH + j
            pe.matmul(scores[n % SRING], kst[0:ROWS, k, h, t * P:(t + 1) * P], qst[0:ROWS, k, h, :],
                      start=True, stop=True).then_inc(made, 1)

        def pe_values(ph, sl):
            pe = nc.tensor
            m, t = divmod(sl, XKT)
            k, gr = divmod(m % (CH * NG), NG)
            if sl >= 0:
                pe.wait_ge(exped, GH * (sl + 1))
            if t == 0 and m + ph.tail:
                pe.wait_ge(evac, m + ph.tail)
            if t == 0 and m == NG:
                pe.wait_ge(w_free, ph.order.after(("v", 3)))
            for j in range(GH):
                last = pe.matmul(av[32 * j:32 * j + HD + 1, :], vals[:, k, t, gr * GH + j, :], probs[:, sl % 2, j, :],
                                 start=t == 0, stop=t == XKT - 1)
            last.then_inc(summed, 1)

        def pe_body(ph):
            for k in range(CH):
                for gr in range(NG):
                    for t in range(XKT):
                        sl = XKT * (NG * k + gr) + t
                        jobs = work_at(ph.tail, k, gr, t)
                        for j in range(GH):
                            pe_scores(k, gr, t, j)
                            if j < GH - 1:
                                pe_max(MXS * sl + j)
                        if jobs:
                            pe_job(ph, jobs[0])
                        pe_max(MXS * sl + GH - 1)
                        if sl or ph.tail:
                            pe_values(ph, sl - 1)
                        pe_max(MXS * sl + GH)
                        for j in jobs[1:]:
                            pe_job(ph, j)

        def act_job(ph, job):
            act = nc.scalar
            name, i = job[0], job[1] if len(job) > 1 else 0
            if name not in ("oT", "x1T", "x2T", "kproj", "qproj", "enc", "mid"):
                return
            act.wait_ge(w_full, ph.order.after(job))
            W = bank_of(ph, job)
            if name == "x1T":
                act.activation(xT[:, i, :], W[:], ACT.Copy).then_inc(w_free, 1)
            elif name in ("oT", "x2T"):
                act.activation(x2T[:, i, :], W[:], ACT.Copy).then_inc(w_free, 1)
            elif name == "enc":
                act.activation(hT[:, i, :], W[:], ACT.Relu, bias=benc[:, i:i + 1]).then_inc(w_free, 1)
            elif name == "mid":
                act.activation(midT[0:ER, :], W[0:ER, :], ACT.Relu, bias=bdown[:]).then_inc(w_free, 1)
            elif name == "kproj":
                n = PIECES[i % NP][1]
                if i >= KBUF:
                    act.wait_ge(kparts_out[i % KBUF], 48 * (i // KBUF))
                act.activation(kpart[:, i % KBUF, 0, 0:n], W[:, 0:n], ACT.Copy).then_inc(khigh, 1)
            elif name == "qproj":
                if i:
                    act.wait_ge(qparts_out, 48)
                act.activation(qpart[:, 0, :], W[:], ACT.Copy, scale=float(HD) ** -0.5).then_inc(qhigh, 1)

        def act_later(ph, job):
            act = nc.scalar
            name, i = job[0], job[1] if len(job) > 1 else 0
            if name == "kproj":
                n = PIECES[i % NP][1]
                act.wait_ge(w_free, ph.order.after(job))
                act.activation(kpart[:, i % KBUF, 1, 0:n], krest[:, i % KBUF, 0:n], ACT.Copy).then_inc(kmid, 1)
            elif name == "qproj":
                act.wait_ge(w_free, ph.order.after(job))
                act.activation(qpart[:, 1, :], qrest[:], ACT.Copy).then_inc(qmid, 1)
            elif name == "dec":
                act.wait_ge(w_free, ph.order.after(job))
                act.activation(err[:, i % 2, :], err[:, i % 2, :], ACT.Square,
                               accum_out=loss[:, i:i + 1]).then_inc(sq_done, 1)

        def act_max_out(ph, m, n):
            nc.scalar.wait_ge(w_free, ph.order.after(("max", m)))
            nc.scalar.dma_start(g.max_dram, mrow[:]).then_inc(mrow_out, 16)

        def act_max_in(m, n):
            k, gr = divmod(m, NG)
            nc.scalar.wait_ge(mrow_out, 16 * n)
            nc.scalar.dma_start(qst[R_MAX:ROWS, k % CH, gr * GH:(gr + 1) * GH, :],
                                g.max_dram.rearrange("(r j q) n -> r j (q n)", r=2, j=GH)).then_inc(max_in, 16)

        def act_values_out(ph, m):
            if m < 0 and not ph.tail:
                return
            nc.scalar.wait_ge(summed, XKT * (m + 1) + ph.tail)
            if m >= 1 or m == 0 and ph.tail:
                nc.scalar.wait_ge(w_full, ph.order.after(("otr", (m - 1) % (CH * NG))))
            nc.scalar.activation(oS[:], av[:], ACT.Copy).then_inc(evac, 1)

        def act_body(ph):
            for k in range(CH):
                for gr in range(NG):
                    for t in range(XKT):
                        m = NG * k + gr
                        sl = XKT * m + t
                        if sl - 1 + ph.tail > 0:
                            nc.scalar.wait_ge(summed, sl - 1 + ph.tail)
                        for j in range(GH):
                            n = GH * sl + j
                            nc.scalar.wait_ge(made, n + 1)
                            nc.scalar.activation(probs[:, sl % 2, j, :], scores[n % SRING], ACT.Exp).then_inc(exped, 1)
                            if t == 1 and j == 0:
                                act_values_out(ph, m - 1)
                        for j in previous_jobs(ph, k, gr, t):
                            act_later(ph, j)
                        for j in work_at(ph.tail, k, gr, t):
                            act_job(ph, j)
                        if t == XKT - LEAD + 1:
                            act_max_out(ph, m + 1, m + 1)
                        if t == XKT - LEAD + 2:
                            act_max_in(m + 1, m + 1)

        def previous_jobs(ph, k, gr, t):
            sl = XKT * (NG * k + gr) + t - 1
            if sl < 0:
                return []
            m, t = divmod(sl, XKT)
            return work_at(ph.tail, *divmod(m, NG), t)

        links = {"dve": 0, "mv": 0}

        def dve_mark(ins):
            links["dve"] += 1
            ins.then_inc(own["dve"], 1)

        def dve_settle():
            nc.vector.wait_ge(own["dve"], links["dve"])

        def dve_link(ins):
            dve_mark(ins)
            dve_settle()

        def dve_step(step):
            v = nc.vector
            name, what, q = step
            x = xa if what == "x1" else x2
            if name == "stats":
                if what == "x1" and q == 0:
                    v.wait_ge(sum_ready, 1)
                dve_mark(v.bn_stats(stats[:, q, :], x[:, q, :]))
            elif name == "aggr":
                dve_settle()
                for i in range(QT):
                    last = v.bn_aggr(meanvar[:, i, :], stats[:, i, :])
                dve_link(last)
                links["mv"] += 1
                v.tensor_scalar(rstd[:], meanvar[:, :, 1], EPS, None, ALU.add).then_inc(mv_ready, 1)
            elif name == "apply":
                if q == 0:
                    v.wait_ge(rstd_ready, links["mv"])
                last = v.tensor_scalar(x[:, q, :], x[:, q, :], meanvar[:, q, 0:1], rstd[:, q:q + 1],
                                       ALU.subtract, ALU.mult)
                if q == QT - 1:
                    last.then_inc(normed, 1)
            else:
                dve_choose(q)

        def dve_norm(what):
            for step in (norm_steps("stats", what, 0, QT) + [("aggr", what, 0)] + norm_steps("apply", what, 0, QT)):
                dve_step(step)

        def dve_choose(step):
            v = nc.vector
            if step:
                dve_settle()
            if step == 0:
                dve_mark(v.tensor_reduce(sc[:, 0:1], l8[:], AX.X, ALU.min))
            elif step == 1:
                dve_mark(v.tensor_scalar(pick[:], l8[:], sc[:, 0:1], None, ALU.is_le))
            elif step == 2:
                dve_mark(v.tensor_tensor(pick[:], pick[:], iotam[:], ALU.mult))
            elif step == 3:
                dve_mark(v.tensor_reduce(sc[:, 1:2], pick[:], AX.X, ALU.min))
            elif step == 4:
                dve_mark(v.tensor_scalar(pick[:], iotam[:], sc[:, 1:2], None, ALU.is_equal))
            elif step == 5:
                dve_mark(v.tensor_tensor(pick[:], pick[:], cidxf[:], ALU.mult))
            elif step == 6:
                dve_mark(v.tensor_reduce(sc[:, 2:3], pick[:], AX.X, ALU.add))
            elif step == 7:
                dve_mark(v.tensor_scalar(sc[:, 3:4], sc[:, 2:3], 0.0, float(NE), ALU.is_lt, ALU.mult))
            elif step == 8:
                dve_mark(v.tensor_tensor(sc[:, 2:3], sc[:, 2:3], sc[:, 3:4], ALU.add))
            elif step == 9:
                dve_mark(v.tensor_scalar(sc[:, 2:3], sc[:, 2:3], 0.0, float(NE - 1), ALU.max, ALU.min))
            else:
                v.tensor_copy(adp[:], sc[0:1, 2:3]).then_inc(adp_ready, 1)

        def dve_job(ph, job):
            v = nc.vector
            name, i = job[0], job[1] if len(job) > 1 else 0
            if name not in ("kproj", "qproj", "xo", "y", "v", "dec", "loss", "max", "otr"):
                return
            v.wait_ge(w_full, ph.order.after(job))
            W = bank_of(ph, job)
            W2 = W[:].rearrange("p (q d) -> p q d", q=2)
            if name == "kproj":
                n = PIECES[i % NP][1]
                v.wait_ge(khigh, i + 1)
                if i >= KBUF:
                    v.wait_ge(klow, i - KBUF + 1)
                v.tensor_tensor(krest[:, i % KBUF, 0:n], W[:, 0:n], kpart[:, i % KBUF, 0, 0:n],
                                ALU.subtract).then_inc(w_free, 1)
            elif name == "qproj":
                v.wait_ge(qhigh, i + 1)
                if i:
                    v.wait_ge(qlow, 1)
                v.scalar_tensor_tensor(qrest[:], W[:], float(HD) ** -0.5, qpart[:, 0, :], ALU.mult,
                                       ALU.subtract).then_inc(w_free, 1)
            elif name in ("xo", "y"):
                if name == "xo" and i == 0:
                    v.wait_ge(x1_in, 16)
                v.tensor_tensor(x2[:, 2 * i:2 * i + 2, :], W2, x2[:, 2 * i:2 * i + 2, :], ALU.add).then_inc(w_free, 1)
                v.wait_ge(w_free, ph.order.after(job))
            elif name == "v":
                c = (i // 4 + 1) % CH
                tiles = range(4 * (i % 4), min(4 * (i % 4) + 4, XKT))
                full = [tt for tt in tiles if (tt + 1) * P <= S2]
                if full:
                    v.tensor_copy(vals[:, c, full[0]:full[-1] + 1, :, 0:HD],
                                  W[:, 0:len(full) * P].rearrange("p (t h d) -> p t h d", t=len(full), d=HD)
                                  ).then_inc(w_free, 1)
                else:
                    rows = S2 - tiles[0] * P
                    v.tensor_copy(vals[0:rows, c, tiles[0], :, 0:HD],
                                  W[0:rows, 0:P].rearrange("p (h d) -> p h d", d=HD)).then_inc(w_free, 1)
            elif name == "dec":
                n, c = divmod(i, CH)
                if i >= 2:
                    v.wait_ge(sq_done, i - 1)
                v.scalar_tensor_tensor(err[:, i % 2, :], W[:], bdec[:, n, c:c + 1], x2T[:, c, :], ALU.add,
                                       ALU.subtract).then_inc(w_free, 1)
            elif name == "loss":
                v.tensor_reduce(l8[:], W[:, 0:NDEC].rearrange("p (n c) -> p n c", c=CH), AX.X,
                                ALU.add).then_inc(w_free, 1)
                v.wait_ge(w_free, ph.order.after(job))
            elif name == "max":
                if ph is not FIRST and i >= 2:
                    v.wait_ge(mrow_out, 16 * (i - 1))
                v.tensor_copy(mrow[:], Wb[0:2 * GH * QT, 0:P]).then_inc(w_free, 1)
            elif name == "otr":
                w4 = W[:].rearrange("p (q j r) -> p q j r", q=QT, r=2 * HD)
                dve_link(v.reciprocal(rz[:], w4[:, :, :, HD]))
                v.tensor_tensor(ox[:, :, i * GH * HD:(i + 1) * GH * HD].rearrange("p q (j d) -> p q j d", d=HD),
                                w4[:, :, :, 0:HD], rz[:].unsqueeze(3).broadcast_to([P, QT, GH, HD]),
                                ALU.mult).then_inc(w_free, 1)

        def dve_max_piece(m, x, n):
            w = PIECES[x % NP][1]
            nc.vector.wait_ge(mxd, n + 1)
            nc.vector.tensor_reduce(nmp[:, m % 2, x // NP, x % NP:x % NP + 1], mx[n % MRING][:, 0:w], AX.X, ALU.max,
                                    negate=True).then_inc(mxr, 1)

        def dve_max(e):
            if MAXES[e]:
                dve_max_piece(*MAXES[e], COUNT[e])

        def dve_max_parts(ph, n_read, n, step, first=False):
            if step == 0:
                nc.vector.wait_ge(mxr, n_read)
                dve_mark(nc.vector.tensor_reduce(nm[:], nmp[:, (n - 1 if first else n) % 2, :, :], AX.X, ALU.min))
            elif step == 1:
                if n >= 2:
                    nc.vector.wait_ge(w_full, ph.order.after(("max", n - 1)))
                dve_settle()
                dve_mark(nc.vector.tensor_copy(comb[:, 0, :], nm[:]))
            elif step == 2:
                dve_settle()
                nc.vector.tensor_tensor(comb[:, 1, :], nm[:], comb[:, 0, :], ALU.subtract).then_inc(comb_ready, 1)

        def dve_body(ph):
            for k in range(CH):
                for gr in range(NG):
                    for t in range(XKT):
                        m = NG * k + gr
                        sl = XKT * m + t
                        jobs = work_at(ph.tail, k, gr, t)
                        steps = vector_work_at(ph.tail, k, gr, t)
                        for i in range(GH):
                            if t == XKT - LEAD:
                                dve_max_parts(ph, COUNT[MXS * sl], m + 1, i)
                            if jobs and i == GH - 1:
                                dve_job(ph, jobs[0])
                            dve_max(MXS * sl + i)
                            if i < len(steps):
                                dve_step(steps[i])
                        dve_max(MXS * sl + GH)
                        for j in jobs[1:]:
                            dve_job(ph, j)

        def pool_sum():
            p = nc.gpsimd
            p.wait_ge(x_in, 32)
            p.tensor_tensor(xa[:], xa[:], bo[:].unsqueeze(1).broadcast_to([P, QT, D]), ALU.add).then_inc(own["pool"], 1)
            p.wait_ge(own["pool"], 1)
            p.tensor_tensor(xa[0:HD, 0, :], xa[0:HD, 0, :], at[:], ALU.add).then_inc(sum_ready, 1)

        def pool_rstd(n):
            nc.gpsimd.wait_ge(mv_ready, n)
            nc.gpsimd.tensor_tensor(rstd[:], rstd[:], g.mhalf[:, 0:QT], ALU.pow).then_inc(rstd_ready, 1)

        def pool_klow(i):
            n = PIECES[i % NP][1]
            nc.gpsimd.wait_ge(kmid, i + 1)
            nc.gpsimd.tensor_tensor(kpart[:, i % KBUF, 2, 0:n], krest[:, i % KBUF, 0:n], kpart[:, i % KBUF, 1, 0:n],
                                    ALU.subtract).then_inc(klow, 1)

        def pool_qlow(i):
            nc.gpsimd.wait_ge(qmid, i + 1)
            nc.gpsimd.tensor_tensor(qpart[:, 2, :], qrest[:], qpart[:, 1, :], ALU.subtract).then_inc(qlow, 1)

        def pool_body(ph):
            pool_sum()
            pool_rstd(1)
            if ph.tail:
                pool_rstd(2)
            for i in range(NP):
                pool_klow(i)
            pool_qlow(0)
            for i in range(NP):
                pool_klow(NP + i)
            pool_qlow(1)
            if ph.tail:
                pool_rstd(3)

        def sp_load_x(b):
            nc.sync.dma_start(xa[:], g.x[bass.ds(b, 1)].rearrange("b (q p) d -> p (b q) d", p=P)).then_inc(x_in, 16)
            nc.sync.dma_start(at[:], g.attn_dram[bass.ds(b, 1)].rearrange("b t d -> (b t) d")).then_inc(x_in, 16)

        def sp_load_ctx(b):
            nc.sync.dma_start(ctxT[:], g.ctxT[bass.ds(b, 1)].rearrange("b (c p) n -> p (b c) n", p=P)).then_inc(c_in, 16)

        def sp_key_parts(i, read):
            k0, n = PIECES[i % NP]
            if i % NP == 0 and read:
                nc.sync.wait_ge(stacked, read)
            for part, ready in enumerate((khigh, kmid, klow)):
                nc.sync.wait_ge(ready, i + 1)
                nc.sync.dma_start(g.kpart_dram[part, :, k0:k0 + n], kpart[:, i % KBUF, part, 0:n]).then_inc(kparts_out[i % KBUF], 16)

        def sp_key_parts_out(n):
            for one in kparts_out:
                nc.sync.wait_ge(one, 48 * (n * NP // KBUF))

        def sp_query_parts(i):
            for part, ready in enumerate((qhigh, qmid, qlow)):
                nc.sync.wait_ge(ready, i + 1)
                nc.sync.dma_start(g.part_dram[part], qpart[:, part, :]).then_inc(qparts_out, 16)

        def sp_key_stacks(b, c):
            for j, pk in enumerate(KPART):
                nc.sync.dma_start(kst[HD * j:HD * (j + 1), c, :, 0:S2],
                                  g.kpart_dram[pk].rearrange("(h d) n -> d h n", d=HD)).then_inc(stacked, 16)
            nc.sync.dma_start(kst[R_MASK:R_MASK + 1, c, :, :],
                              g.mask_dram[bass.ds(b, 1)].unsqueeze(1).broadcast_to([1, HC, SP_])).then_inc(stacked, 16)

        def sp_query_stacks(c):
            for j, pq in enumerate(QPART):
                nc.sync.dma_start(qst[HD * j:HD * (j + 1), c, :, :],
                                  g.part_dram[pq].rearrange("(h d) n -> d h n", d=HD)).then_inc(stacked, 16)

        def sp_stacks(b, c):
            sp_query_stacks(c)
            sp_key_stacks(b, c)

        def sp_stored():
            nc.sync.wait_ge(out_done, 16)
            nc.sync.sem_clear(out_done)

        def sp_load_x1(b):
            nc.sync.dma_start(x2[:], g.x1_dram[bass.ds(b, 1)].rearrange("b (q p) d -> p (b q) d", p=P)).then_inc(x1_in, 16)

        def sp_store_x1(ph, b):
            nc.sync.wait_ge(normed, normed_of(ph, "x1"))
            nc.sync.dma_start(g.x1_dram[bass.ds(b, 1)].rearrange("b (q p) d -> p (b q) d", p=P), xa[:]).then_inc(x1_out, 16)

        def sp_adapter():
            sp = nc.sync
            sp.wait_ge(adp_ready, 1)
            n = sp.value_load(adp[0:1, 0:1], min_val=0, max_val=NE - 1)
            sp.dma_start(wdown[:], g.Wdown[bass.ds(n, 1)].rearrange("n (c p) r -> p (n c) r", p=P)).then_inc(adp_in, 16)
            sp.dma_start(wup[0:ER, :], g.Wup[bass.ds(n, 1)].rearrange("n r d -> (n r) d")).then_inc(adp_in, 16)
            sp.dma_start(wup[ER:ER + 1, :], g.bup[bass.ds(n, 1)]).then_inc(adp_in, 16)
            with nc.allow_non_contiguous_dma(reason="a bias column"):
                sp.dma_start(bdown[:], g.bdown[bass.ds(n, 1)].rearrange("n r -> r n")).then_inc(adp_in, 16)

        def sp_store_out(ph, b):
            nc.sync.wait_ge(normed, normed_of(ph, "y"))
            nc.sync.dma_start(g.out[bass.ds(b, 1)].rearrange("b (q p) d -> p (b q) d", p=P), x2[:]).then_inc(out_done, 16)

        def sp_body(ph, b, nxt):
            sp_load_x(nxt)
            if ph.tail:
                sp_stored()
                sp_load_x1(b - 1)
            sp_stacks(b, 1)
            nc.sync.wait_ge(w_full, ph.order.after(("v", 3)))
            sp_load_ctx(nxt)
            sp_store_x1(ph, nxt)
            for i in range(NP):
                sp_key_parts(i, 16 * STACK_DMAS)
            sp_query_parts(0)
            nc.sync.wait_ge(made, GH * NG * XKT)
            sp_key_parts_out(1)
            nc.sync.wait_ge(qparts_out, 48)
            sp_stacks(nxt, 0)
            for i in range(NP):
                sp_key_parts(NP + i, 32 * STACK_DMAS)
                if i == 1 and ph.tail:
                    sp_adapter()
            sp_query_parts(1)
            if ph.tail:
                sp_store_out(ph, b - 1)
            nc.sync.wait_ge(x1_out, 16)
            sp_key_parts_out(2)
            nc.sync.wait_ge(qparts_out, 96)
            nc.sync.wait_ge(stacked, 32 * STACK_DMAS)
            nc.sync.wait_ge(max_in, 16 * NG * CH)

        first_pieces = [(0, x) for x in range(MXG)] + [(1, x) for x in range(LEAD * MXS)]
        keys_in = sem("x_keys_weights_in")
        N_LOADS = 16 * (3 + 2 * NE + 6)
        KEY_DMAS = len(KPART) + 1

        def sp_beside(it):
            sp = nc.sync
            if it == 0:
                sp_load_ctx(0)
                for dst, src in ((xkT[:], g.xWkT), (xvT[:], g.xWvT)):
                    sp.dma_start(dst, src.rearrange("(c p) d -> p c d", p=P)).then_inc(keys_in, 16)
                return
            if it == 2:
                sp.dma_start(xa[:], g.x[0].rearrange("(q p) d -> p q d", p=P)).then_inc(x_in, 16)
                return
            for i in range(NP):
                sp_key_parts(i, 0)
            n = 0
            sp.wait_ge(zeroed, 3)
            with nc.allow_non_contiguous_dma(reason="bias columns and rows, once"):
                for dst, src in ((xqT[:], g.xWqT), (xoT[:], g.xWoT), (wbase[:], g.Wbase)):
                    sp.dma_start(dst, src.rearrange("(c p) d -> p c d", p=P)).then_inc(loaded, 16)
                    n += 16
                for e in range(NE):
                    sp.dma_start(wenc[:, :, e, :], g.Wenc[e].rearrange("(c p) h -> p c h", p=P)).then_inc(loaded, 16)
                    half = EH * (e % 2)
                    sp.dma_start(wdec[half:half + EH, e, :], g.Wdec[e]).then_inc(loaded, 16)
                    n += 32
                for dst, src in ((bo[:], g.bo.unsqueeze(0).broadcast_to([P, D])),
                                 (benc[:], g.benc.rearrange("n h -> (n h)").rearrange("(j p) -> p j", p=P)),
                                 (bdec[:], g.bdec.rearrange("n (c p) -> p n c", p=P)),
                                 (cidx[:], g.cidx.unsqueeze(0).broadcast_to([P, NE])),
                                 (iota[:], g.c_iota.broadcast_to([P, NE])),
                                 (wup[ER + 1:ER + 2, :], g.bbase.unsqueeze(0))):
                    sp.dma_start(dst, src).then_inc(loaded, 16)
                    n += 16
            assert n == N_LOADS
            sp.wait_ge(zeroed, 8)
            sp_key_parts_out(1)
            sp_key_stacks(0, 0)
            for i in range(NP):
                sp_key_parts(NP + i, 16 * KEY_DMAS)

        def pool_beside(it):
            p, pool = nc.gpsimd, nc.gpsimd
            if it < ITERS:
                for job in KEYS_BESIDE[it]:
                    pool_klow(job[1])
                pool.wait_ge(klow, KEYS_BESIDE[it][-1][1] + 1)
            if it == 0:
                p.memset(wdec[:], 0.0).then_inc(zeroed, 1)
                p.memset(ones[:], 1.0).then_inc(zeroed, 1)
                pool.wait_ge(zeroed, 2)
                p.memset(midT[ER:ER + 2, :], 1.0).then_inc(zeroed, 1)
                pool.wait_ge(zeroed, 3)
                p.memset(vals[:], 0.0).then_inc(zeroed, 1)
                pool.wait_ge(zeroed, 4)
                p.memset(vals[:, :, :, :, HD:HD + 1], 1.0).then_inc(zeroed, 1)
                pool.wait_ge(zeroed, 5)
                p.memset(kst[64:128, 0:1, :, :], 1.0).then_inc(zeroed, 1)
                p.memset(kst[64:128, 1:2, :, :], 1.0).then_inc(zeroed, 1)
                pool.wait_ge(zeroed, 7)
                p.memset(kst[0:96, :, :, S2:SP_], 0.0).then_inc(zeroed, 1)
                pool.wait_ge(zeroed, 8)
            elif it == 1:
                p.memset(qst[96:128, :, :, :], 1.0).then_inc(zeroed, 1)
                pool.wait_ge(zeroed, 9)
            elif it == ITERS:
                pool.wait_ge(x_in, 16)
                pool.wait_ge(loaded, N_LOADS)
                p.tensor_tensor(xa[:], xa[:], bo[:].unsqueeze(1).broadcast_to([P, QT, D]),
                                ALU.add).then_inc(own["pool"], 1)
                pool.wait_ge(own["pool"], 1)

        def act_beside(it):
            before = None
            for job in KEYS_BESIDE[it]:
                if before:
                    act_later(FIRST, before)
                act_job(FIRST, job)
                before = job
            act_later(FIRST, before)

        def beside(engine, it):
            if engine == "sp":
                sp_beside(it)
            elif engine == "pool":
                pool_beside(it)
            elif engine == "act":
                act_beside(it)
            elif engine == "dve":
                for job in KEYS_BESIDE[it]:
                    dve_job(FIRST, job)
            elif engine == "dve values":
                nc.vector.wait_ge(zeroed, 5)
                for job in VALUES_BESIDE[it]:
                    dve_job(FIRST, job)
            else:
                if it == 0:
                    nc.tensor.wait_ge(keys_in, 32)
                for job in (KEYS_BESIDE if engine == "pe" else VALUES_BESIDE)[it]:
                    pe_job(FIRST, job)

        def rows_view(i):
            return x2[:, i, :]

        view = {
            "x": rows_view(0), "proj": rows_view(1), "xn": rows_view(2),
            "xnT": rows_view(3).rearrange("p (c t) -> p c t", c=CH),
            "wq": x2T[:, 0, :].rearrange("p (c d) -> p c d", c=CH), "wk": x2T[:, 1, :].rearrange("p (c d) -> p c d", c=CH),
            "wv": ox[:, 0:2, :], "wo": ox[:, 2:4, :],
            "cen": err[:, 0, :].rearrange("p (n d) -> p n d", d=HD), "sq": err[:, 1, :].rearrange("p (n d) -> p n d", d=HD),
            "sc": probs[:, 0, :, :].rearrange("p j t -> p (j t)").rearrange("p (h t) -> p h t", h=H),
            "pT": probs[:, 1, :, :].rearrange("p j t -> p (j t)").rearrange("p (h t) -> p h t", h=H),
            "ksM": hT[:].rearrange("p j t -> p (j t)").rearrange("p (c h t) -> p c h t", c=CH, h=HC),
            "state": xa[:, 0:3, :].rearrange("p n (c t) -> p n c t", c=CH),
            "qsT": xa[:, 3, :].rearrange("p (c t) -> p c t", c=CH),
            "m8": oS[:].bitcast(U8)[0:B, 0:S2],
            "mb": xT[:].rearrange("p c t -> p (c t)").bitcast(BF16)[0:B, 0:SP_],
        }
        g.attn_out = sem("x_attention_out")
        own_self = s.enter_context(ExitStack())
        self_sp, self_pool, self_act, self_pe, self_dve = short_self_attention(nc, g, own_self, view, beside)

        with nc.Block() as blk:
            @blk.sync
            def _(sp):
                self_sp(sp)
                sp_query_parts(0)
                sp.wait_ge(zeroed, 9)
                sp.wait_ge(qparts_out, 48)
                sp_query_stacks(0)
                sp_store_x1(FIRST, 0)
                sp_query_parts(1)
                sp.wait_ge(x1_out, 16)
                sp_key_parts_out(2)
                sp.wait_ge(qparts_out, 96)
                sp.wait_ge(max_in, 16)
                sp.wait_ge(loaded, N_LOADS)
                sp.wait_ge(g.attn_out, 16)

            @blk.gpsimd
            def _(pool):
                self_pool(pool)
                nc.gpsimd.tensor_tensor(xa[0:HD, 0, :], xa[0:HD, 0, :], view["proj"][0:HD, :],
                                        ALU.add).then_inc(sum_ready, 1)
                pool_rstd(1)
                pool_qlow(0)
                pool_qlow(1)

            @blk.scalar
            def _(act):
                self_act(act)
                before = None
                for job in (j for j in AFTER if j[0] != "max"):
                    if before:
                        act_later(FIRST, before)
                    act_job(FIRST, job)
                    before = job
                act_later(FIRST, before)
                act_max_out(FIRST, 0, 1)
                act_max_in(0, 1)

            @blk.vector
            def _(dve):
                self_dve(dve)
                v = nc.vector
                dve.wait_ge(loaded, N_LOADS)
                dve_link(v.tensor_copy(cidxf[:], cidx[:]))
                dve_link(v.tensor_scalar(iotam[:], iota[:], float(NE), None, ALU.subtract))
                dve_norm("x1")
                dve_link(v.memset(av[:], 0.0))
                for job in AFTER[:-1]:
                    if job != ("max", 0):
                        dve_job(FIRST, job)
                for n, (m, x) in enumerate(first_pieces):
                    if n == MXG:
                        for step in range(3):
                            dve_max_parts(FIRST, MXG, 1, step, first=True)
                        dve_job(FIRST, ("max", 0))
                        dve_job(FIRST, ("qproj", 1))
                    dve_max_piece(m, x, n)

            @blk.tensor
            def _(pe):
                self_pe(pe)
                pe.wait_ge(loaded, N_LOADS)
                for job in AFTER[:-2]:
                    pe_job(FIRST, job)
                for n, (m, x) in enumerate(first_pieces):
                    if n == 0:
                        pe.wait_ge(stacked, 16 * STACK_DMAS)
                    if n == MXG:
                        pe_job(FIRST, ("max", 0))
                        pe_job(FIRST, ("qproj", 1))
                    pe_max_piece(m, x, n)

        own_self.close()

        def clear():
            with nc.Block() as blk:
                @blk.sync
                def _(sp):
                    for one in cleared_early + cleared:
                        sp.sem_clear(one)
            links.update(dve=0, mv=0)

        clear()

        with nc.Block() as blk:
            @blk.tensor
            def _(pe):
                pe_body(BODY0)

            @blk.scalar
            def _(act):
                act_body(BODY0)

            @blk.vector
            def _(dve):
                dve_body(BODY0)

            @blk.gpsimd
            def _(pool):
                pool_body(BODY0)

            @blk.sync
            def _(sp):
                sp_body(BODY0, 0, 1)
                sp.sem_inc(out_done, 16)

        clear()

        def leave(eng, i):
            eng.drain().then_inc(arrived, 1)
            eng.wait_ge(go, i)

        with nc.Block() as blk:
            @blk.tensor
            def _(pe):
                with pe.Fori(1, B) as i:
                    pe_body(BODY)
                    leave(pe, i)

            @blk.scalar
            def _(act):
                with act.Fori(1, B) as i:
                    act_body(BODY)
                    leave(act, i)

            @blk.vector
            def _(dve):
                with dve.Fori(1, B) as i:
                    dve_body(BODY)
                    leave(dve, i)

            @blk.gpsimd
            def _(pool):
                with pool.Fori(1, B) as i:
                    pool_body(BODY)
                    leave(pool, i)

            @blk.sync
            def _(sp):
                with sp.Fori(1, B) as i:
                    sp_body(BODY, i, (i + 1) % B)
                    for one in cleared_early:
                        sp.sem_clear(one)
                    sp.wait_ge(arrived, 4)
                    for one in cleared:
                        sp.sem_clear(one)
                    sp.sem_inc(go, 1)

        links.update(dve=0, mv=0)

        with nc.Block() as blk:
            last_jobs = LAST.order.names

            @blk.sync
            def _(sp):
                sp_stored()
                sp_load_x1(B - 1)
                sp_adapter()
                sp_store_out(LAST, B - 1)
                sp.wait_ge(out_done, 16)

            @blk.gpsimd
            def _(pool):
                pool_rstd(1)
                pool_rstd(2)

            @blk.scalar
            def _(act):
                before = None
                act_values_out(LAST, -1)
                for job in last_jobs:
                    if before:
                        act_later(LAST, before)
                    act_job(LAST, job)
                    before = job

            @blk.vector
            def _(dve):
                for job in last_jobs:
                    dve_job(LAST, job)
                    if job in (("xo", 1), ("y", 1)):
                        dve_norm("x2" if job[0] == "xo" else "y")
                    if job == ("loss",):
                        for step in range(CHOOSE_STEPS):
                            dve_choose(step)

            @blk.tensor
            def _(pe):
                pe_values(LAST, -1)
                for job in last_jobs:
                    pe_job(LAST, job)


def constants():
    import numpy as np
    head = np.arange(P)[:, None] // HD == np.arange(HC)[None]
    batch = np.arange(TOK) // HD
    return {
        "c_ident": np.eye(P, dtype=np.float32),
        "c_head": head.astype(np.float32),
        "c_hide": np.where(batch[:, None] == batch[None], 0.0, NEG).astype(np.float32),
        "c_iota": np.arange(NE, dtype=np.float32)[None],
    }


def layout(inputs):
    import numpy as np
    a = {k: np.asarray(v) for k, v in inputs.items()}

    def t(name):
        return np.ascontiguousarray(a[name].T)

    r = {"x": a["x"], "ctxT": np.ascontiguousarray(a["ctx_1024"].transpose(0, 2, 1)),
         "mask": np.ascontiguousarray(a["mask_Bx1x1xS2_bf1"]).view(np.uint8).reshape(B, S2),
         **{f"W{n}T": t(f"L0_attn_W{n}") for n in ("q", "k", "v", "o")},
         "xWqT": t("L0_xattn_Wq"), "xWkT": t("L0_xattn_Wk"), "xWvT": t("L0_xattn_Wv"),
         "xWoT": t("L0_xattn_Wo")}
    r["bo"] = a["L0_attn_bo"]
    c = constants()
    r["x_head"] = a["x"][:, :HD, :].reshape(TOK, D)
    r["rows"] = np.concatenate(
        [a[f"L0_attn_{n}"].reshape(-1) for n in ("lna_w", "blq", "blk", "blv", "lnc_w", "lnd_w")]
        + [a["L0_attn_temp"].reshape(-1)] * ITERS + [a[f"L0_attn_{n}"].reshape(-1) for n in ("threshold", "factor")])[None]
    r["cols"] = np.concatenate([c.pop("c_head"), c.pop("c_hide")]
                               + [a[f"L0_attn_{n}"].reshape(CH, P).T for n in ("bq", "bv")], axis=1)
    r["Wl"] = np.zeros((3, P, P), np.float32)
    for i, n in enumerate("qkv"):
        for h in range(HC):
            r["Wl"][i, h * HD:(h + 1) * HD, h * HD:(h + 1) * HD] = t(f"L0_attn_Wl{n}")
    for k, n in (("Wbase", "W_base"), ("bbase", "b_base"), ("Wenc", "W_enc"), ("benc", "b_enc"), ("Wdec", "W_dec"),
                 ("bdec", "b_dec"), ("Wdown", "W_down"), ("bdown", "b_down"), ("Wup", "W_up"), ("bup", "b_up"),
                 ("cidx", "connected_idx")):
        r[k] = a[f"L0_ffn_{n}"]
    return {**r, **c}


def kernel(**inputs):
    import numpy as np
    import concourse.bacc as bacc
    from concourse.bass_utils import run_bass_kernel_spmd

    nc = bacc.Bacc("TRN2", target_bir_lowering=False, num_devices=1)
    arrays = {f"in_{k}": np.ascontiguousarray(v) for k, v in layout(inputs).items()}
    g = Shared({k[3:]: nc.dram_tensor(k, v.shape, mybir.dt.from_np(v.dtype), kind="ExternalInput").ap()
                for k, v in arrays.items()})
    g.out = nc.dram_tensor("out_dram", (B, T, D), F32, kind="ExternalOutput").ap()
    program(nc, g)
    r = run_bass_kernel_spmd(nc, [arrays], core_ids=[0])
    return r.results[0]["out_dram"]
```
